# Optimizing a Trainium2 kernel written in Bass

```python
import numpy as np
import jax
import jax.numpy as jnp

def _softmax(x, axis=-1):
    return jax.nn.softmax(x, axis=axis)

def _gelu(x):
    return jax.nn.gelu(x, approximate=True)

def _silu(x):
    return jax.nn.silu(x)

def _sigmoid(x):
    return jax.nn.sigmoid(x)

def _layernorm(x, axis=-1, eps=1e-05):
    m = jnp.mean(x, axis=axis, keepdims=True)
    v = jnp.var(x, axis=axis, keepdims=True)
    return (x - m) / jnp.sqrt(v + eps)

def _scatter_add(tgt, idx, src, axis=0):
    return tgt.at[idx].add(src)

def _segment_sum(src, seg, n):
    return jax.ops.segment_sum(src, seg, n)
kernel_name = 'mk_macaron_d1_jaxref_r4_137a34'

def setup_inputs(seed: int=0):
    np.random.seed(seed)
    _w = jnp.asarray

    def _L0_attn_setup():
        import jax, jax.numpy as jnp
        import numpy as np
        B, N, C = (4, 1370, 256)
        H, DH = (16, C // 16)
        N_ROPE = 1369

        def _rotate_half(x):
            x1, x2 = jnp.split(x, 2, axis=-1)
            return jnp.concatenate([-x2, x1], axis=-1)

        def _rope_apply(x, sin, cos):
            return x * cos + _rotate_half(x) * sin
        key = jax.random.key(seed)
        ks = jax.random.split(key, 7)
        return {'x': jax.random.normal(ks[0], (B, N, C), dtype=jnp.float32), 'sin': jax.random.normal(ks[1], (N_ROPE, DH), dtype=jnp.float32), 'cos': jax.random.normal(ks[2], (N_ROPE, DH), dtype=jnp.float32), 'w_qkv': jax.random.normal(ks[3], (C, 3 * C), dtype=jnp.float32) * C ** (-0.5), 'b_qkv': jax.random.normal(ks[4], (3 * C,), dtype=jnp.float32) * 0.02, 'w_proj': jax.random.normal(ks[5], (C, C), dtype=jnp.float32) * C ** (-0.5), 'b_proj': jax.random.normal(ks[6], (C,), dtype=jnp.float32) * 0.02}
    _L0_attn_in = _L0_attn_setup()

    def _L0_ffn_setup():
        import jax, jax.numpy as jnp
        import numpy as np
        B, T, D, F_FF, E, TOP_K = (8, 512, 256, 1024, 8, 2)
        CAP_FACTOR = 1.25
        key = jax.random.key(seed)
        ks = jax.random.split(key, 7)
        s = 0.02
        return {'x': jax.random.normal(ks[0], (B, T, D), dtype=jnp.float32), 'w_router': jax.random.normal(ks[1], (D, E), dtype=jnp.float32) * s, 'b_router': jnp.zeros((E,), dtype=jnp.float32), 'w1': jax.random.normal(ks[2], (E, D, F_FF), dtype=jnp.float32) * s, 'b1': jnp.zeros((E, F_FF), dtype=jnp.float32), 'w2': jax.random.normal(ks[3], (E, F_FF, D), dtype=jnp.float32) * s, 'b2': jnp.zeros((E, D), dtype=jnp.float32)}
    _L0_ffn_in = _L0_ffn_setup()
    _d = {'L0_attn_x': _L0_attn_in['x'], 'L0_attn_sin': _L0_attn_in['sin'], 'L0_attn_cos': _L0_attn_in['cos'], 'L0_attn_w_qkv': _L0_attn_in['w_qkv'], 'L0_attn_b_qkv': _L0_attn_in['b_qkv'], 'L0_attn_w_proj': _L0_attn_in['w_proj'], 'L0_attn_b_proj': _L0_attn_in['b_proj'], 'L0_ffn_w_router': _L0_ffn_in['w_router'], 'L0_ffn_b_router': _L0_ffn_in['b_router'], 'L0_ffn_w1': _L0_ffn_in['w1'], 'L0_ffn_b1': _L0_ffn_in['b1'], 'L0_ffn_w2': _L0_ffn_in['w2'], 'L0_ffn_b2': _L0_ffn_in['b2']}
    _x0 = _d['L0_attn_x']
    _d['L0_attn_x'] = jax.random.normal(jax.random.fold_in(jax.random.key(seed), 1), (2, 2048, 256), dtype=_x0.dtype)
    del _x0
    return _d

def reference(L0_attn_x, L0_attn_sin, L0_attn_cos, L0_attn_w_qkv, L0_attn_b_qkv, L0_attn_w_proj, L0_attn_b_proj, L0_ffn_w_router, L0_ffn_b_router, L0_ffn_w1, L0_ffn_b1, L0_ffn_w2, L0_ffn_b2):

    def _L0_attn_ref(x, sin, cos, w_qkv, b_qkv, w_proj, b_proj):
        import jax, jax.numpy as jnp
        import numpy as np
        B, N, C = (4, 1370, 256)
        H, DH = (16, C // 16)
        N_ROPE = 1369

        def _rotate_half(x):
            x1, x2 = jnp.split(x, 2, axis=-1)
            return jnp.concatenate([-x2, x1], axis=-1)

        def _rope_apply(x, sin, cos):
            return x * cos + _rotate_half(x) * sin
        b, n, c = x.shape
        qkv = (x @ w_qkv + b_qkv).reshape(b, n, 3, H, DH).transpose(2, 0, 3, 1, 4)
        q, k, v = (qkv[0], qkv[1], qkv[2])
        prefix = n - sin.shape[-2]
        q = jnp.concatenate([q[:, :, :prefix, :], _rope_apply(q[:, :, prefix:, :], sin, cos)], axis=-2)
        k = jnp.concatenate([k[:, :, :prefix, :], _rope_apply(k[:, :, prefix:, :], sin, cos)], axis=-2)
        scale = 1.0 / jnp.sqrt(jnp.asarray(DH, dtype=x.dtype))
        attn = jnp.einsum('bhqd,bhkd->bhqk', q, k) * scale
        attn = jax.nn.softmax(attn, axis=-1)
        out = jnp.einsum('bhqk,bhkd->bhqd', attn, v)
        out = out.transpose(0, 2, 1, 3).reshape(b, n, c)
        return out @ w_proj + b_proj

    def _L0_ffn_ref(x, w_router, b_router, w1, b1, w2, b2):
        import jax, jax.numpy as jnp
        import numpy as np
        B, T, D, F_FF, E, TOP_K = (8, 512, 256, 1024, 8, 2)
        CAP_FACTOR = 1.25
        b, t, d = x.shape
        n = b * t
        e = w_router.shape[1]
        xf = x.reshape(n, d)
        logits = xf.astype(jnp.float32) @ w_router + b_router
        gates = jax.nn.softmax(logits, axis=-1)
        topv, topi = jax.lax.top_k(gates, TOP_K)
        cap = max(1, int(CAP_FACTOR * n / e))
        e_flat = topi.reshape(-1)
        g_flat = topv.reshape(-1)
        tok = jnp.repeat(jnp.arange(n), TOP_K)
        onehot = jax.nn.one_hot(e_flat, e, dtype=jnp.int32)
        pos = jnp.cumsum(onehot, axis=0)[jnp.arange(n * TOP_K), e_flat] - 1
        keep = pos < cap
        posc = jnp.minimum(pos, cap - 1)
        buf = jnp.zeros((e, cap, d), x.dtype).at[e_flat, posc].add(jnp.where(keep[:, None], xf[tok], 0.0))
        h = jax.nn.gelu(jnp.einsum('ecd,edf->ecf', buf, w1) + b1[:, None, :], approximate=False)
        out = jnp.einsum('ecf,efd->ecd', h, w2) + b2[:, None, :]
        og = out[e_flat, posc]
        w = jnp.where(keep, g_flat, 0.0).astype(x.dtype)
        y = jnp.zeros((n, d), x.dtype).at[tok].add(w[:, None] * og)
        ws = jnp.zeros((n,), x.dtype).at[tok].add(w)
        y = jnp.where((ws > 0.0)[:, None], y / jnp.maximum(ws, 1e-06)[:, None], y)
        return y.reshape(b, t, d)
    x = L0_attn_x
    x = x + 0.5 * _L0_ffn_ref(_layernorm(x, axis=-1), L0_ffn_w_router, L0_ffn_b_router, L0_ffn_w1, L0_ffn_b1, L0_ffn_w2, L0_ffn_b2)
    x = x + _L0_attn_ref(_layernorm(x, axis=-1), L0_attn_sin, L0_attn_cos, L0_attn_w_qkv, L0_attn_b_qkv, L0_attn_w_proj, L0_attn_b_proj)
    x = x + 0.5 * _L0_ffn_ref(_layernorm(x, axis=-1), L0_ffn_w_router, L0_ffn_b_router, L0_ffn_w1, L0_ffn_b1, L0_ffn_w2, L0_ffn_b2)
    return x

_drawn_inputs = setup_inputs


def setup_inputs(seed=0):
    import zlib

    import numpy as np

    out = dict(_drawn_inputs(seed))
    spreads = {'L0_ffn_b_router': (0.0, 0.1), 'L0_ffn_b1': (0.0, 0.318), 'L0_ffn_b2': (0.0, 0.1)}
    factors = {}
    for name, (base, spread) in spreads.items():
        noise = np.random.default_rng([zlib.crc32(name.encode()), seed]).standard_normal(out[name].shape)
        drawn = base * np.exp(spread * noise) if base else spread * noise
        out[name] = jnp.asarray(drawn.astype(out[name].dtype))
    for name, factor in factors.items():
        out[name] = (out[name] * factor).astype(out[name].dtype)
    return out
```

```python
from contextlib import ExitStack

import concourse.bass as bass
from concourse import mybir

F32, BF16, I32 = mybir.dt.float32, mybir.dt.bfloat16, mybir.dt.int32
ALU = mybir.AluOpType
ACT = mybir.ActivationFunctionType
AX = mybir.AxisListType

P = 128
B, T, D = 2, 2048, 256
N = B * T
KD = D // P
H, DH = 16, 16
HALF = DH // 2
N_ROPE = 1369
PREFIX = T - N_ROPE
NE, FF = 8, 1024
KF = FF // P
CAP = int(1.25 * N / NE)
SLOT_TILES = CAP // P
TILES = N // P
CHUNK = 512
CT = CHUNK // P
NCH = N // CHUNK
BCH = T // CHUNK
ROW = D + 2
SLOTS = NE * CAP
EPS = 1e-5
NH = B * H
KT = T // P
PARTS = 3
SPLIT = 6
QROWS = SPLIT * DH
MROWS = QROWS + PARTS
LEAD = 4
FT = 4
HT = P // DH
HH = CAP // 2


def wait(eng, sem, value):
    if not isinstance(value, int) or value > 0:
        eng.wait_ge(sem, value)


def hold(eng, sem, value, passed):
    if not isinstance(value, int) or value > 0:
        eng.wait_ge(sem, value)
        eng.sem_inc(passed, 1)


class Norm:
    pass


class Steps:

    def __init__(self, eng, sem):
        self.eng, self.sem, self.base, self.n = eng, sem, 0, 0

    def add(self, ins):
        ins.then_inc(self.sem, 1)
        self.n += 1

    def settle(self):
        self.eng.wait_ge(self.sem, self.base + self.n)

    def settle_alone(self, passed):
        hold(self.eng, self.sem, self.base + self.n, passed)

    def restart(self, base):
        self.base, self.n = base, 0


def pair_loop(eng, steps, head, body, pairs):
    head()
    at = steps.n if steps else 0
    body(0, False)
    per = steps.n - at if steps else 0
    with eng.Fori(1, pairs - 1) as i:
        if steps:
            steps.restart(i * per + at)
        body(i, False)
    if steps:
        steps.restart((pairs - 1) * per + at)
    body(pairs - 1, True)


def build(nc, x, sin, cos, w_qkv, b_qkv, w_proj, b_proj, w_router, b_router, w1, b1, w2, b2, out):
    ctx = ExitStack()

    def sem(name):
        return ctx.enter_context(nc.semaphore(name))

    def pair(name):
        return [sem(f"{name}{q}") for q in range(2)]

    def sb(scope, name, shape, dt=F32):
        return scope.enter_context(nc.sbuf_tensor(name, shape, dt))

    def ps(scope, name, shape, dt=F32):
        return scope.enter_context(nc.psum_tensor(name, shape, dt))

    slots = nc.dram_tensor("slots", [SLOTS + 2 * N, ROW], F32).ap()
    resid = [nc.dram_tensor(f"resid{m}", [N + CAP, D], F32).ap() for m in range(2)]
    qk_parts = nc.dram_tensor("qk_parts", [NH * 2 * PARTS * DH, T], BF16).ap()
    max_rows = nc.dram_tensor("max_rows", [2, P, PARTS * 32], BF16).ap()
    attn = nc.dram_tensor("attn", [NH * 32, T], F32).ap()
    rden = nc.dram_tensor("rden", [NH, T], F32).ap()

    with ctx:
        XR = sb(ctx, "XR", [P, TILES, D])
        W1 = [sb(ctx, f"W1_{q}", [P, KD, FF]) for q in range(2)]
        W2 = [sb(ctx, f"W2_{q}", [P, KF, D]) for q in range(2)]
        B2 = [sb(ctx, f"B2_{q}", [P, D]) for q in range(2)]
        b1T = sb(ctx, "b1T", [P, NE * KF])
        ident = sb(ctx, "ident", [P, P])
        ones = sb(ctx, "ones", [P, P], BF16)
        before = sb(ctx, "before", [P, P], BF16)
        em8 = sb(ctx, "em8", [P, CT, NE])
        tok_id = sb(ctx, "tok_id", [P, TILES], I32)
        trash = sb(ctx, "trash", [P, 2, TILES])
        mhalf = sb(ctx, "mhalf", [P, CT])
        wr = sb(ctx, "wr", [P, KD, NE])
        br = sb(ctx, "br", [P, NE])
        wqk = sb(ctx, "wqk", [P, KD, FT * P])
        wv = sb(ctx, "wv", [P, KD, D])
        wp = sb(ctx, "wp", [P, KD, D])
        bqk = sb(ctx, "bqk", [P, FT])
        bv = sb(ctx, "bv", [P, D])
        bp = sb(ctx, "bp", [P, D])
        meta = sb(ctx, "meta", [P, NE, SLOT_TILES, 2])
        cosT = sb(ctx, "cosT", [P, T])
        sinT = sb(ctx, "sinT", [P, T])

        w_loaded = pair("w_loaded")
        slots_ready = sem("slots_ready")
        spare_ready = sem("spare_ready")
        passed = [sem(f"passed_{e}") for e in ("dve", "pool")]
        resid_ready = [sem(f"resid_ready{m}") for m in range(2)]
        consts = sem("consts")
        small_loaded = sem("small_loaded")

        def load_weights(sp, e, q):
            sp.dma_start(W1[q][:], w1[bass.ds(e * D, D), :].rearrange("(k p) f -> p k f", p=P)).then_inc(w_loaded[q], 16)
            sp.dma_start(W2[q][:], w2[bass.ds(e * FF, FF), :].rearrange("(k p) f -> p k f", p=P)).then_inc(w_loaded[q], 16)
            sp.dma_start(B2[q][:], b2[bass.ds(e, 1), :].to_broadcast([P, D])).then_inc(w_loaded[q], 16)

        def setup(scope):
            wq_nat = sb(scope, "wq_nat", [P, KD, 3 * D])
            b1_nat = sb(scope, "b1_nat", [NE * KF, P])
            tab = sb(scope, "tab", [P, 2, KT, DH])
            wide = sb(scope, "wide", [P, 2, 4, P])
            empty = sb(scope, "empty", [P, NE, SLOT_TILES, ROW])
            itmp = sb(scope, "itmp", [P, CT * NE], I32)
            itrash = sb(scope, "itrash", [P, 2 * TILES], I32)
            banks = ExitStack()
            pW = ps(banks, "pW", [P, 2, CHUNK])
            pB = ps(banks, "pB", [P, CHUNK])[:, 0:NE * KF]
            empty_made = sem("empty_made")
            tab_set = sem("tab_set")
            tab_loaded = sem("tab_loaded")
            wide_made = sem("wide_made")
            wide_turned = sem("wide_turned")
            tab_written = sem("tab_written")
            b1_turned = sem("b1_turned")
            setup_steps = sem("setup_steps")
            with nc.Block() as block:

                @block.sync
                def _(sp):
                    sp.dma_start(wq_nat[:], w_qkv.rearrange("(k p) f -> p k f", p=P)).then_inc(small_loaded, 16)
                    sp.dma_start(wp[:], w_proj.rearrange("(k p) f -> p k f", p=P)).then_inc(small_loaded, 16)
                    sp.dma_start(wr[:], w_router.rearrange("(k p) f -> p k f", p=P)).then_inc(small_loaded, 16)
                    sp.dma_start(br[:], b_router.to_broadcast([P, NE])).then_inc(small_loaded, 16)
                    sp.dma_start(bv[:], b_qkv[:, 2 * D:3 * D].to_broadcast([P, D])).then_inc(small_loaded, 16)
                    sp.dma_start(bp[:], b_proj.to_broadcast([P, D])).then_inc(small_loaded, 16)
                    sp.dma_start(b1_nat[:], b1.rearrange("e (k p) -> (e k) p", p=P)).then_inc(small_loaded, 16)
                    for f in range(FT):
                        for s in range(2):
                            src = b_qkv[0, f * P:(f + 1) * P].rearrange("(h s d) -> s h d", h=HT, s=2)[s]
                            sp.dma_start(bqk[s * 64:(s + 1) * 64, f:f + 1], src).then_inc(small_loaded, 16)
                    sp.wait_ge(tab_set, 1)
                    t0, p0 = PREFIX // P, PREFIX % P
                    for n, src in enumerate((cos, sin)):
                        sp.dma_start(tab[p0:P, n, t0, :], src[0:P - p0, :]).then_inc(tab_loaded, 16)
                        sp.dma_start(tab[:, n, t0 + 1:KT, :],
                                     src[P - p0:N_ROPE, :].rearrange("(t p) d -> p t d", p=P)).then_inc(tab_loaded, 16)

                @block.gpsimd
                def _(pool):
                    steps = Steps(pool, setup_steps)
                    nc.gpsimd.memset(tab[:, 0], 1.0)
                    nc.gpsimd.memset(tab[:, 1], 0.0).then_inc(tab_set, 1)
                    steps.add(nc.gpsimd.memset(empty[:], 0.0))
                    steps.add(nc.gpsimd.memset(ident[:], 0.0))
                    steps.add(nc.gpsimd.memset(before[:], 0.0))
                    nc.gpsimd.memset(ones[:], 1.0)
                    nc.gpsimd.memset(mhalf[:], -0.5)
                    steps.settle()
                    nc.gpsimd.iota(empty[:].bitcast(I32)[:, :, :, D + 1], pattern=[[0, NE], [1, SLOT_TILES]], base=N,
                                   channel_multiplier=SLOT_TILES).then_inc(empty_made, 1)
                    nc.gpsimd.tensor_copy(meta[:].bitcast(I32)[:, :, :, 0], empty[:].bitcast(I32)[:, :, :, D])
                    pool.wait_ge(empty_made, 1)
                    nc.gpsimd.tensor_copy(meta[:].bitcast(I32)[:, :, :, 1], empty[:].bitcast(I32)[:, :, :, D + 1])
                    nc.gpsimd.affine_select(out=ident[:], in_=ident[:], compare_op=ALU.not_equal, fill=1.0, base=0,
                                            pattern=[[-1, P]], channel_multiplier=1).then_inc(consts, 1)
                    nc.gpsimd.affine_select(out=before[:], in_=before[:], compare_op=ALU.is_ge, fill=1.0, base=0,
                                            pattern=[[-1, P]], channel_multiplier=1)
                    nc.gpsimd.iota(tok_id[:], pattern=[[P, TILES]], base=0, channel_multiplier=1)
                    steps.add(nc.gpsimd.iota(itmp[:], pattern=[[0, CT], [1, NE]], base=-NE, channel_multiplier=0))
                    steps.add(nc.gpsimd.iota(itrash[:], pattern=[[N, 2], [P, TILES]], base=SLOTS, channel_multiplier=1))
                    steps.settle()
                    nc.gpsimd.tensor_copy(em8[:].rearrange("p a b -> p (a b)"), itmp[:])
                    nc.gpsimd.tensor_copy(trash[:].rearrange("p a b -> p (a b)"), itrash[:]).then_inc(consts, 1)
                    pool.wait_ge(small_loaded, 15 * 16)
                    for k in range(KD):
                        for f in range(FT):
                            dst = wqk[:, k, f * P:(f + 1) * P].rearrange("p (s h d) -> p s h d", s=2, h=HT)
                            src = wq_nat[:, k, f * P:(f + 1) * P].rearrange("p (h s d) -> p s h d", h=HT, s=2)
                            nc.gpsimd.tensor_copy(dst, src)
                    nc.gpsimd.tensor_copy(wv[:], wq_nat[:, :, 2 * D:3 * D]).then_inc(consts, 1)
                    pool.wait_ge(consts, 3)

                @block.vector
                def _(dve):
                    dve.wait_ge(tab_loaded, 64)
                    for g in range(8):
                        n, t0 = g // 4, 4 * (g % 4)
                        if g >= 2:
                            dve.wait_ge(wide_turned, g - 1)
                        for s in range(2):
                            src = s if n == 0 else 1 - s
                            src = tab[:, n, t0:t0 + 4, src * HALF:(src + 1) * HALF].unsqueeze(2).to_broadcast([P, 4, HT, HALF])
                            dst = wide[:, g % 2, :, s * 64:(s + 1) * 64].rearrange("p t (h d) -> p t h d", h=HT)
                            last = nc.vector.tensor_scalar(dst, src, -1.0 if n == 1 and s == 1 else 1.0, None, ALU.mult)
                        last.then_inc(wide_made, 1)

                @block.tensor
                def _(pe):
                    pe.wait_ge(consts, 1)
                    for g in range(8):
                        pe.wait_ge(wide_made, g + 1)
                        if g >= 2:
                            pe.wait_ge(tab_written, g - 1)
                        for j in range(4):
                            last = nc.tensor.transpose(pW[:, g % 2, j * P:(j + 1) * P], wide[:, g % 2, j, :], ident[:])
                        last.then_inc(wide_turned, 1)
                    pe.wait_ge(small_loaded, 15 * 16)
                    nc.tensor.transpose(pB, b1_nat[:], ident[0:NE * KF, 0:NE * KF]).then_inc(b1_turned, 1)

                @block.scalar
                def _(act):
                    act.wait_ge(empty_made, 1)
                    for e in range(NE):
                        act.dma_start(slots[e * CAP:(e + 1) * CAP, :].rearrange("(p j) d -> p j d", p=P), empty[:, e]).then_inc(slots_ready, 16)
                    for m in range(2):
                        act.dma_start(resid[m][N:N + CAP, :].rearrange("(p j) d -> p j d", p=P), empty[:, 0, :, 0:D]).then_inc(spare_ready, 16)
                    for g in range(8):
                        act.wait_ge(wide_turned, g + 1)
                        dst = (cosT, sinT)[g // 4][:, (g % 4) * CHUNK:(g % 4 + 1) * CHUNK]
                        nc.scalar.activation(dst, pW[:, g % 2, :], ACT.Copy).then_inc(tab_written, 1)
                    act.wait_ge(b1_turned, 1)
                    nc.scalar.activation(b1T[:], pB, ACT.Copy).then_inc(tab_written, 1)
                    act.wait_ge(tab_written, 9)
            banks.close()

        def norm_buffers(scope, tag):
            nb = Norm()
            nb.st = [sb(scope, f"st{tag}{q}", [P, CT, 6]) for q in range(2)]
            nb.mv = [sb(scope, f"mv{tag}{q}", [P, CT, 2]) for q in range(2)]
            nb.ve = [sb(scope, f"ve{tag}{q}", [P, CT]) for q in range(2)]
            nb.rs = [sb(scope, f"rs{tag}{q}", [P, CT]) for q in range(2)]
            nb.pT = ps(scope, f"pT{tag}", [P, KD, CHUNK])
            nb.xT = [sb(scope, f"xT{tag}{q}", [P, KD, CHUNK]) for q in range(2)]
            nb.stats, nb.ve_made, nb.rstd = sem(f"stats{tag}"), sem(f"ve_made{tag}"), sem(f"rstd{tag}")
            nb.normed, nb.turned, nb.xT_ready = sem(f"normed{tag}"), sem(f"turned{tag}"), sem(f"xT_ready{tag}")
            return nb

        def norm_stats(nb, steps, c, q):
            for j in range(CT):
                ins = nc.vector.bn_stats(nb.st[q][:, j, :], XR[:, bass.ds(c * CT + j, 1), :].rearrange("p a d -> p (a d)"))
            steps.add(ins)
            steps.settle_alone(passed[0])
            for j in range(CT):
                ins = nc.vector.bn_aggr(nb.mv[q][:, j, :], nb.st[q][:, j, :])
            ins.then_inc(nb.stats, 1)

        def norm_rstd(pool, nb, c, q):
            hold(pool, nb.stats, c + 1, passed[1])
            nc.gpsimd.tensor_scalar(nb.ve[q][:], nb.mv[q][:, :, 1], EPS, None, ALU.add).then_inc(nb.ve_made, 1)
            pool.wait_ge(nb.ve_made, c + 1)
            nc.gpsimd.tensor_tensor(out=nb.rs[q][:], in0=nb.ve[q][:], in1=mhalf[:], op=ALU.pow).then_inc(nb.rstd, 1)

        def norm_apply(dve, nb, dst, c, q):
            dve.wait_ge(nb.stats, c + 1)
            dve.wait_ge(nb.rstd, c + 1)
            for j in range(CT):
                ins = nc.vector.tensor_scalar(dst[:, j, 0:D], XR[:, bass.ds(c * CT + j, 1), :].rearrange("p a d -> p (a d)"),
                                              nb.mv[q][:, j, 0:1], nb.rs[q][:, j:j + 1], ALU.subtract, ALU.mult)
            ins.then_inc(nb.normed, 1)

        def norm_turn(pe, nb, src, c):
            pe.wait_ge(nb.normed, c + 1)
            wait(pe, nb.xT_ready, c)
            for k in range(KD):
                for j in range(CT):
                    ins = nc.tensor.transpose(nb.pT[:, k, j * P:(j + 1) * P], src[:, j, k * P:(k + 1) * P], ident[:])
            ins.then_inc(nb.turned, 1)

        def norm_evacuate(act, nb, c, q):
            act.wait_ge(nb.turned, c + 1)
            nc.scalar.activation(nb.xT[q][:], nb.pT[:], ACT.Copy).then_inc(nb.xT_ready, 1)

        def bank_pair(scope, name):
            banks = ps(scope, name, [P, 2, CHUNK])
            return [banks[:, q, 0:CT * NE].rearrange("p (j e) -> p j e", j=CT) for q in range(2)]

        def route(m, project):
            tag = f"r{m}"
            with ExitStack() as scope:
                nb = norm_buffers(scope, tag)
                rows = [sb(scope, f"rows{tag}{q}", [P, 2, CT, ROW]) for q in range(2)]
                lg = [sb(scope, f"lg{tag}{q}", [P, CT, NE]) for q in range(2)]
                l2 = [sb(scope, f"l2{tag}{q}", [P, CT, NE]) for q in range(2)]
                eq = [sb(scope, f"eq{tag}{q}", [P, 2, CT, NE]) for q in range(2)]
                oh = [sb(scope, f"oh{tag}{q}", [P, 2, CT, NE]) for q in range(2)]
                top = [sb(scope, f"top{tag}{q}", [P, 2, CT]) for q in range(2)]
                em = [sb(scope, f"em{tag}{q}", [P, 2, CT]) for q in range(2)]
                mask = [sb(scope, f"mask{tag}{q}", [P, CT, NE], BF16) for q in range(2)]
                less = [sb(scope, f"less{tag}{q}", [P, CT, NE + 1]) for q in range(2)]
                ex = [sb(scope, f"ex{tag}{q}", [P, CT, NE + 1]) for q in range(2)]
                seen = [sb(scope, f"seen{tag}{q}", [P, NE]) for q in range(2)]
                seen_b = [sb(scope, f"seen_b{tag}{q}", [P, NE], BF16) for q in range(2)]
                here = sb(scope, f"here{tag}", [P, NE])
                hit = sb(scope, f"hit{tag}", [P, 2, CT, NE])
                pos = sb(scope, f"pos{tag}", [P, 2, CT])
                keep = sb(scope, f"keep{tag}", [P, 2, CT])
                slot = sb(scope, f"slot{tag}", [P, 2, CT])
                off = sb(scope, f"off{tag}", [P, 2, CT])
                gate = sb(scope, f"gate{tag}", [P, 2, CT])
                gsum = sb(scope, f"gsum{tag}", [P, 2, CT])
                dest = [sb(scope, f"dest{tag}{q}", [P, 2, CT], I32) for q in range(2)]
                pL = bank_pair(scope, f"pL{tag}")
                pP = bank_pair(scope, f"pP{tag}")
                steps_sem = sem(f"dve_steps{tag}")
                x_loaded = pair(f"x_loaded{tag}")
                row_copied, logits = sem(f"row_copied{tag}"), sem(f"logits{tag}")
                masked, prefixed = sem(f"masked{tag}"), sem(f"prefixed{tag}")
                less_made, exped = sem(f"less_made{tag}"), sem(f"exped{tag}")
                routed, scattered = sem(f"routed{tag}"), pair(f"scattered{tag}")
                x_ready, x_stored = sem(f"x_ready{tag}"), sem(f"x_stored{tag}")
                if project:
                    num = [sb(scope, f"num{q}", [P, KD, CHUNK]) for q in range(2)]
                    rcp = [sb(scope, f"rcp{q}", [P, KD, CHUNK]) for q in range(2)]
                    onT = [sb(scope, f"onT{q}", [P, KD, CHUNK]) for q in range(2)]
                    den = sb(scope, "den", [P, NH * T // P])
                    pY = ps(scope, "pY", [P, 2, 2, D])
                    den_loaded, den_inv, rden_stored = sem("den_loaded"), sem("den_inv"), sem("rden_stored")
                    o_loaded, o_made, projected = pair("o_loaded"), sem("o_made"), sem("projected")
                block = scope.enter_context(nc.Block())

                @block.sync
                def _(sp):
                    if not project:

                        def load(c, q, n):
                            wait(sp, x_loaded[q], 16 * n)
                            sp.dma_start(XR[:, bass.ds(c * CT, CT), :],
                                         x[bass.ds(c * CHUNK, CHUNK), :].rearrange("(t p) d -> p t d", p=P)).then_inc(x_loaded[q], 16)
                        for q in range(2):
                            load(q, q, 0)
                        with sp.Fori(1, NCH // 2) as i:
                            for q in range(2):
                                load(2 * i + q, q, i)
                        load_weights(sp, 0, 0)
                        sp.dma_start(resid[m][0:N, :], x).then_inc(resid_ready[m], 16)
                        load_weights(sp, 1, 1)
                        return
                    sp.dma_start(den[:], attn.rearrange("(n r) (a t) -> r n a t", r=32, a=4)[DH]).then_inc(den_loaded, 16)
                    sp.wait_ge(den_inv, 1)
                    sp.dma_start(rden.rearrange("n (a t) -> (n a) t", a=4), den[:]).then_inc(rden_stored, 16)
                    sp.wait_ge(rden_stored, 16)

                    def load(i, q):
                        if not isinstance(i, int) or i > 0:
                            sp.wait_ge(o_made, 2 * i + q - 1)
                        b, qc = i // 2, 2 * (i % 2) + q
                        for k in range(KD):
                            h0 = b * H + k * HT
                            src = attn[bass.ds(h0 * 32, HT * 32), bass.ds(qc * CHUNK, CHUNK)]
                            sp.dma_start(num[q][:, k, :], src.rearrange("(h r) t -> h r t", r=32)[:, 0:DH, :]).then_inc(o_loaded[q], 16)
                            src = rden[bass.ds(h0, HT), bass.ds(qc * CHUNK, CHUNK)]
                            sp.dma_start(rcp[q][:, k, :], src.unsqueeze(1).to_broadcast([HT, DH, CHUNK])).then_inc(o_loaded[q], 16)

                    def store(c):
                        sp.wait_ge(x_ready, c + 1)
                        sp.dma_start(resid[m][bass.ds(c * CHUNK, CHUNK), :].rearrange("(t p) d -> p t d", p=P),
                                     XR[:, bass.ds(c * CT, CT), :]).then_inc(x_stored, 16)
                        sp.wait_ge(x_stored, 16 * (c + 1))
                    load(0, 0)
                    load(0, 1)
                    with sp.Fori(1, NCH // 2) as i:
                        for q in range(2):
                            store(2 * i + q - 2)
                            load(i, q)
                    for c in (NCH - 2, NCH - 1):
                        store(c)

                @block.tensor
                def _(pe):
                    def attend(c, q):
                        pe.wait_ge(o_made, c + 1)
                        wait(pe, x_ready, c)
                        for j in range(CT):
                            for k in range(KD):
                                ins = nc.tensor.matmul(pY[:, j // 2, j % 2, :], onT[q][:, k, j * P:(j + 1) * P], wp[:, k, :],
                                                       start=(k == 0), stop=(k == KD - 1))
                        ins.then_inc(projected, 1)

                    def score(c, q):
                        norm_turn(pe, nb, rows[q][:, 0], c)
                        pe.wait_ge(nb.xT_ready, c + 1)
                        wait(pe, masked, c - 1)
                        for j in range(CT):
                            for k in range(KD):
                                ins = nc.tensor.matmul(pL[q][:, j, :], nb.xT[q][:, k, j * P:(j + 1) * P], wr[:, k, :],
                                                       start=(k == 0), stop=(k == KD - 1))
                        ins.then_inc(logits, 1)

                    def prefix(c, q):
                        pe.wait_ge(masked, c + 1)
                        nc.tensor.matmul(pP[q], before[:], mask[q][:], start=True, stop=False)
                        for j in range(CT - 1):
                            nc.tensor.matmul(pP[q][:, j + 1:CT, :], ones[:],
                                             mask[q][:, j:j + 1, :].to_broadcast([P, CT - 1 - j, NE]), start=False, stop=False)
                        nc.tensor.matmul(pP[q], ones[:], seen_b[q][:].unsqueeze(1).to_broadcast([P, CT, NE]),
                                         start=False, stop=True).then_inc(prefixed, 1)

                    def head():
                        if project:
                            attend(0, 0)
                        score(0, 0)

                    def body(i, last):
                        for q in range(2):
                            c = 2 * i + q
                            more = not (last and q)
                            if project and more:
                                attend(c + 1, 1 - q)
                            prefix(c, q)
                            if more:
                                score(c + 1, 1 - q)
                    pair_loop(pe, None, head, body, NCH // 2)

                @block.scalar
                def _(act):
                    def evacuate(c, q, n):
                        wait(act, logits, c - 1)
                        norm_evacuate(act, nb, c, q)
                        act.wait_ge(nb.normed, c + 1)
                        wait(act, scattered[q], 128 * n)
                        nc.scalar.activation(rows[q][:, 1, :, 0:D], rows[q][:, 0, :, 0:D], ACT.Copy).then_inc(row_copied, 1)

                    def body(i, last):
                        for q in range(2):
                            c = 2 * i + q
                            act.wait_ge(less_made, c + 1)
                            nc.scalar.activation(ex[q][:], less[q][:], ACT.Exp).then_inc(exped, 1)
                            if not (last and q):
                                evacuate(c + 1, 1 - q, i + q)
                    pair_loop(act, None, lambda: evacuate(0, 0, 0), body, NCH // 2)

                @block.gpsimd
                def _(pool):
                    def scatter(c, q):
                        pool.wait_ge(routed, c + 1)
                        hold(pool, row_copied, c + 1, passed[1])
                        for k in range(2):
                            for j in range(CT):
                                nc.gpsimd.indirect_dma_start(
                                    out=slots, out_offset=bass.IndirectOffsetOnAxis(ap=dest[q][:, k, j:j + 1], axis=0),
                                    in_=rows[q][:, k, j, :], in_offset=None).then_inc(scattered[q], 16)

                    def body(i, last):
                        for q in range(2):
                            if not (last and q):
                                norm_rstd(pool, nb, 2 * i + q + 1, 1 - q)
                            scatter(2 * i + q, q)
                    pool.wait_ge(slots_ready, 16 * NE * (m + 1))
                    pair_loop(pool, None, lambda: norm_rstd(pool, nb, 0, 0), body, NCH // 2)
                    for q in range(2):
                        pool.wait_ge(scattered[q], 128 * (NCH // 2))
                    pool.wait_ge(spare_ready, 32)

                @block.vector
                def _(dve):
                    steps = Steps(dve, steps_sem)

                    def divide(c, q, n):
                        dve.wait_ge(o_loaded[q], 64 * (n + 1))
                        wait(dve, projected, c - 1)
                        nc.vector.tensor_tensor(out=onT[q][:], in0=num[q][:], in1=rcp[q][:], op=ALU.mult).then_inc(o_made, 1)

                    def residual(c, q, n):
                        if not project:
                            hold(dve, x_loaded[q], 16 * (n + 1), passed[0])
                            return
                        dve.wait_ge(projected, c + 1)
                        for g in range(2):
                            xs = XR[:, bass.ds(c * CT + 2 * g, 2), :]
                            ins = nc.vector.tensor_tensor(out=xs, in0=pY[:, g], in1=xs, op=ALU.add)
                        ins.then_inc(x_ready, 1)
                        hold(dve, x_ready, c + 1, passed[0])

                    def bc(ap):
                        return ap.unsqueeze(2).to_broadcast([P, CT, NE])

                    def choose(c, q):
                        dve.wait_ge(logits, c + 1)
                        steps.add(nc.vector.tensor_tensor(out=lg[q][:], in0=pL[q],
                                                          in1=br[:].unsqueeze(1).to_broadcast([P, CT, NE]), op=ALU.add))
                        steps.settle()
                        for k, src in enumerate((lg[q], l2[q])):
                            steps.add(nc.vector.tensor_reduce(out=top[q][:, k, :], in_=src[:], axis=AX.X, op=ALU.max))
                            steps.settle()
                            steps.add(nc.vector.tensor_tensor(out=eq[q][:, k], in0=src[:], in1=bc(top[q][:, k, :]), op=ALU.is_equal))
                            steps.settle()
                            steps.add(nc.vector.tensor_tensor(out=hit[:, k], in0=eq[q][:, k], in1=em8[:], op=ALU.mult))
                            steps.settle()
                            steps.add(nc.vector.tensor_reduce(out=em[q][:, k, :], in_=hit[:, k], axis=AX.X, op=ALU.min))
                            steps.settle()
                            steps.add(nc.vector.tensor_tensor(out=oh[q][:, k], in0=em8[:], in1=bc(em[q][:, k, :]), op=ALU.is_equal))
                            steps.settle()
                            if k == 0:
                                steps.add(nc.vector.scalar_tensor_tensor(out=l2[q][:], in0=oh[q][:, 0], scalar=-3e38,
                                                                         in1=lg[q][:], op0=ALU.mult, op1=ALU.add))
                                steps.settle()
                        nc.vector.tensor_tensor(out=mask[q][:], in0=oh[q][:, 0], in1=oh[q][:, 1], op=ALU.add).then_inc(masked, 1)
                        nc.vector.tensor_tensor(out=less[q][:, :, 0:NE], in0=lg[q][:], in1=bc(top[q][:, 0, :]), op=ALU.subtract)
                        nc.vector.tensor_tensor(out=less[q][:, :, NE], in0=top[q][:, 1, :], in1=top[q][:, 0, :],
                                                op=ALU.subtract).then_inc(less_made, 1)

                    def place(c, q, n):
                        dve.wait_ge(prefixed, c + 1)
                        dve.wait_ge(masked, c + 1)
                        steps.add(nc.vector.tensor_tensor(out=hit[:], in0=oh[q][:],
                                                          in1=pP[q].unsqueeze(1).to_broadcast([P, 2, CT, NE]), op=ALU.mult))
                        steps.add(nc.vector.tensor_reduce(out=here[:], in_=mask[q][:].rearrange("p j e -> p e j"), axis=AX.X, op=ALU.add))
                        steps.settle()
                        steps.add(nc.vector.tensor_reduce(out=pos[:], in_=hit[:], axis=AX.X, op=ALU.add))
                        steps.add(nc.vector.tensor_tensor(out=seen[1 - q][:], in0=seen[q][:], in1=here[:], op=ALU.add))
                        steps.add(nc.vector.tensor_scalar(slot[:], em[q][:], float(NE), float(CAP), ALU.add, ALU.mult))
                        dve.wait_ge(exped, c + 1)
                        steps.add(nc.vector.tensor_reduce(out=gsum[:, 0, :], in_=ex[q][:, :, 0:NE], axis=AX.X, op=ALU.add))
                        steps.settle()
                        steps.add(nc.vector.tensor_copy(seen_b[1 - q][:], seen[1 - q][:]))
                        steps.add(nc.vector.tensor_scalar(keep[:], pos[:], float(CAP), None, ALU.is_lt))
                        steps.add(nc.vector.tensor_tensor(out=off[:], in0=slot[:], in1=pos[:], op=ALU.add))
                        steps.add(nc.vector.reciprocal(gate[:, 0, :], gsum[:, 0, :]))
                        steps.settle()
                        steps.add(nc.vector.tensor_tensor(out=off[:], in0=off[:], in1=trash[:, :, bass.ds(c * CT, CT)], op=ALU.subtract))
                        steps.add(nc.vector.tensor_tensor(out=gate[:, 1, :], in0=ex[q][:, :, NE], in1=gate[:, 0, :], op=ALU.mult))
                        steps.settle()
                        steps.add(nc.vector.tensor_tensor(out=off[:], in0=off[:], in1=keep[:], op=ALU.mult))
                        steps.add(nc.vector.tensor_tensor(out=gate[:], in0=gate[:], in1=keep[:], op=ALU.mult))
                        steps.settle()
                        wait(dve, scattered[q], 128 * n)
                        steps.add(nc.vector.tensor_tensor(out=dest[q][:], in0=off[:], in1=trash[:, :, bass.ds(c * CT, CT)], op=ALU.add))
                        steps.add(nc.vector.tensor_tensor(out=gsum[:, 0, :], in0=gate[:, 0, :], in1=gate[:, 1, :], op=ALU.add))
                        steps.settle()
                        steps.add(nc.vector.tensor_scalar(gsum[:, 0, :], gsum[:, 0, :], 1e-6, 2.0, ALU.max, ALU.mult))
                        steps.settle()
                        steps.add(nc.vector.reciprocal(gsum[:, 1, :], gsum[:, 0, :]))
                        steps.settle()
                        nc.vector.tensor_copy(rows[q][:].bitcast(I32)[:, :, :, D + 1],
                                              tok_id[:, bass.ds(c * CT, CT)].unsqueeze(1).to_broadcast([P, 2, CT]))
                        nc.vector.tensor_tensor(out=rows[q][:, :, :, D], in0=gate[:],
                                                in1=gsum[:, 1, :].unsqueeze(1).to_broadcast([P, 2, CT]),
                                                op=ALU.mult).then_inc(routed, 1)

                    def normalise(c, q, n):
                        wait(dve, scattered[q], 128 * n)
                        norm_apply(dve, nb, rows[q][:, 0], c, q)

                    def head():
                        steps.add(nc.vector.memset(seen[0][:], 0.0))
                        steps.add(nc.vector.memset(seen_b[0][:], 0.0))
                        if project:
                            dve.wait_ge(den_loaded, 16)
                            nc.vector.reciprocal(den[:], den[:]).then_inc(den_inv, 1)
                            divide(0, 0, 0)
                        residual(0, 0, 0)
                        norm_stats(nb, steps, 0, 0)
                        normalise(0, 0, 0)

                    def body(i, last):
                        for q in range(2):
                            c = 2 * i + q
                            more = not (last and q)
                            if project and more:
                                divide(c + 1, 1 - q, i + q)
                            choose(c, q)
                            if more:
                                residual(c + 1, 1 - q, i + q)
                                norm_stats(nb, steps, c + 1, 1 - q)
                            place(c, q, i)
                            if more:
                                normalise(c + 1, 1 - q, i + q)
                    pair_loop(dve, steps, head, body, NCH // 2)

        def experts(m):
            tag = f"e{m}"
            with ExitStack() as scope:
                XE = [sb(scope, f"XE{tag}{q}", [P, SLOT_TILES, ROW]) for q in range(2)]
                XT = [sb(scope, f"XT{tag}{q}", [P, KD, CAP]) for q in range(2)]
                hid = sb(scope, f"hid{tag}", [P, KF, CAP])
                b1c = [sb(scope, f"b1c{tag}{q}", [P, KF]) for q in range(2)]
                Y = [sb(scope, f"Y{tag}{q}", [P, SLOT_TILES, D]) for q in range(2)]
                yb = [sb(scope, f"yb{tag}{q}", [P, D]) for q in range(2)]
                pX = ps(scope, f"pX{tag}", [P, 2, KD, D])
                pH = ps(scope, f"pH{tag}", [P, 2, 2, CHUNK])
                pO = ps(scope, f"pO{tag}", [P, 2, CHUNK])
                x_in, x_turned, x_out = pair(f"x_in{tag}"), sem(f"x_turned{tag}"), sem(f"x_out{tag}")
                h_made, h_out, bias_in = sem(f"h_made{tag}"), sem(f"h_out{tag}"), sem(f"bias_in{tag}")
                o_made, o_out, y_made = sem(f"o_made{tag}"), sem(f"o_out{tag}"), sem(f"y_made{tag}")
                added = sem(f"added{tag}")
                block = scope.enter_context(nc.Block())
                GROUPS = [(0, 2), (2, 4), (4, 5)]
                NG = len(GROUPS)

                @block.sync
                def _(sp):
                    def load_slots(e, q):
                        sp.dma_start(XE[q][:], slots[bass.ds(e * CAP, CAP), :].rearrange("(j p) d -> p j d", p=P)).then_inc(x_in[q], 16)

                    for q in range(2):
                        load_slots(q, q)

                    def body(i):
                        for q in range(2):
                            e = 2 * i + q + 2
                            sp.wait_ge(added, 16 * SLOT_TILES * (e - 1))
                            load_slots(e, q)
                            sp.wait_ge(o_out, SLOT_TILES * (e - 1))
                            load_weights(sp, e, q)
                    with sp.Fori(0, NE // 2 - 1) as i:
                        body(i)
                    if m == 0:
                        for q in range(2):
                            sp.wait_ge(o_out, SLOT_TILES * (NE - 1 + q))
                            load_weights(sp, q, q)

                @block.tensor
                def _(pe):
                    def turn(e, q, n):
                        pe.wait_ge(x_in[q], 16 * (n + 1))
                        for g, (a, b) in enumerate(GROUPS):
                            wait(pe, x_out, NG * e + g - 1)
                            for j in range(a, b):
                                for k in range(KD):
                                    ins = nc.tensor.transpose(pX[:, (NG * q + g) % 2, k, (j - a) * P:(j - a + 1) * P],
                                                              XE[q][:, j, k * P:(k + 1) * P], ident[:])
                            ins.then_inc(x_turned, 1)

                    def up(e, q, n):
                        pe.wait_ge(w_loaded[q], 48 * (n + 1 + (NE // 2) * m))
                        pe.wait_ge(x_out, NG * (e + 1))
                        for f in range(KF):
                            wait(pe, h_out, KF * e + f - 1)
                            for h in range(2):
                                for k in range(KD):
                                    ins = nc.tensor.matmul(pH[:, f % 2, h, 0:HH], W1[q][:, k, f * P:(f + 1) * P],
                                                           XT[q][:, k, h * HH:(h + 1) * HH], start=(k == 0), stop=(k == KD - 1))
                            ins.then_inc(h_made, 1)

                    def down(e, q):
                        for j in range(SLOT_TILES):
                            wait(pe, o_out, SLOT_TILES * e + j - 1)
                            for f in range(KF):
                                if j == 0:
                                    pe.wait_ge(h_out, KF * e + f + 1)
                                ins = nc.tensor.matmul(pO[:, (SLOT_TILES * q + j) % 2, 0:D], hid[:, f, j * P:(j + 1) * P],
                                                       W2[q][:, f, :], start=(f == 0), stop=(f == KF - 1))
                            ins.then_inc(o_made, 1)

                    def body(i, last):
                        for q in range(2):
                            e = 2 * i + q
                            up(e, q, i)
                            if not (last and q):
                                turn(e + 1, 1 - q, i + q)
                            down(e, q)
                    pair_loop(pe, None, lambda: turn(0, 0, 0), body, NE // 2)

                @block.scalar
                def _(act):
                    def body(i, last):
                        for q in range(2):
                            e = 2 * i + q
                            nc.scalar.activation(b1c[q][:], b1T[:, bass.ds(e * KF, KF)], ACT.Copy).then_inc(bias_in, 1)
                            act.wait_ge(bias_in, e + 1)
                            for f in range(KF):
                                act.wait_ge(h_made, KF * e + f + 1)
                                nc.scalar.activation(hid[:, f, :].rearrange("p (h c) -> p h c", h=2), pH[:, f % 2, :, 0:HH],
                                                     ACT.Gelu, bias=b1c[q][:, f:f + 1]).then_inc(h_out, 1)
                    pair_loop(act, None, lambda: None, body, NE // 2)

                @block.vector
                def _(dve):
                    def evacuate(e, q):
                        for g, (a, b) in enumerate(GROUPS):
                            dve.wait_ge(x_turned, NG * e + g + 1)
                            nc.vector.tensor_copy(XT[q][:, :, a * P:b * P], pX[:, (NG * q + g) % 2, :, 0:(b - a) * P]).then_inc(x_out, 1)

                    def body(i, last):
                        for q in range(2):
                            e = 2 * i + q
                            if not (last and q):
                                evacuate(e + 1, 1 - q)
                            wait(dve, added, 16 * SLOT_TILES * (e - 1))
                            for j in range(SLOT_TILES):
                                n = SLOT_TILES * e + j
                                dve.wait_ge(o_made, n + 1)
                                y = yb[(SLOT_TILES * q + j) % 2]
                                nc.vector.tensor_tensor(out=y[:], in0=pO[:, (SLOT_TILES * q + j) % 2, 0:D], in1=B2[q][:],
                                                        op=ALU.add).then_inc(o_out, 1)
                                dve.wait_ge(o_out, n + 1)
                                ins = nc.vector.tensor_scalar(Y[q][:, j, :], y[:], XE[q][:, j, D:D + 1], None, ALU.mult)
                                ins.then_inc(y_made, 1)
                    pair_loop(dve, None, lambda: evacuate(0, 0), body, NE // 2)

                @block.gpsimd
                def _(pool):
                    if m == 0:
                        pool.wait_ge(resid_ready[0], 16)

                    def body(i, last):
                        for q in range(2):
                            e = 2 * i + q
                            wait(pool, added, 16 * SLOT_TILES * e)
                            for j in range(SLOT_TILES):
                                hold(pool, y_made, SLOT_TILES * e + j + 1, passed[1])
                                nc.gpsimd.indirect_dma_start(
                                    out=resid[m], out_offset=bass.IndirectOffsetOnAxis(ap=XE[q][:].bitcast(I32)[:, j, D + 1:D + 2], axis=0),
                                    in_=Y[q][:, j, :], in_offset=None, compute_op=ALU.add).then_inc(added, 16)
                    pair_loop(pool, None, lambda: None, body, NE // 2)
                    pool.wait_ge(added, 16 * SLOT_TILES * NE)

        def qkv(VA, Vscope):
            with ExitStack() as scope:
                nb = norm_buffers(scope, "q")
                xn = [sb(scope, f"xn{q}", [P, CT, D]) for q in range(2)]
                RING = 4
                LAG = 2
                ta = [sb(scope, f"ta{r}", [P, CHUNK]) for r in range(2)]
                tb = [sb(scope, f"tb{r}", [P, CHUNK]) for r in range(2)]
                tr = [sb(scope, f"tr{r}", [P, CHUNK]) for r in range(RING)]
                rem = [sb(scope, f"rem{r}", [P, CHUNK]) for r in range(RING)]
                spl = [sb(scope, f"spl{r}", [P, PARTS, CHUNK], BF16) for r in range(RING)]
                pQ = ps(scope, "pQ", [P, 2, CHUNK])
                pV = ps(scope, "pV", [P, 2, 2, D])
                steps_sem = sem("dve_stepsq")
                x_loaded = pair("x_loadedq")
                q_made, q_read, summed = sem("q_made"), sem("q_read"), sem("summed")
                hi, rem_made, mid, low = sem("hi"), sem("rem_made"), sem("mid"), sem("low")
                v_made, v_out = sem("v_made"), sem("v_out")
                stored = [sem(f"parts_stored{r}") for r in range(RING)]
                block = scope.enter_context(nc.Block())
                ITEMS = 2 * FT

                @block.sync
                def _(sp):
                    def load(c, q, n):
                        wait(sp, x_loaded[q], 16 * n)
                        sp.dma_start(XR[:, bass.ds(c * CT, CT), :],
                                     resid[0][bass.ds(c * CHUNK, CHUNK), :].rearrange("(t p) d -> p t d", p=P)).then_inc(x_loaded[q], 16)
                    for q in range(2):
                        load(q, q, 0)
                    with sp.Fori(1, NCH // 2) as i:
                        for q in range(2):
                            load(2 * i + q, q, i)

                    with sp.Fori(0, NCH // 2) as i:
                        for k in range(ITEMS):
                            q, f = divmod(k, FT)
                            sp.wait_ge(low, ITEMS * i + k + 1)
                            sp.wait_ge(mid, ITEMS * i + k + 1)
                            b, qc = i // 2, 2 * (i % 2) + q
                            which, g = divmod(f, 2)
                            base = (b * H + g * HT) * 2 * PARTS * DH
                            dst = qk_parts[bass.ds(base, HT * 2 * PARTS * DH), bass.ds(qc * CHUNK, CHUNK)]
                            dst = dst.rearrange("(h w a s d) t -> w a s h d t", w=2, a=PARTS, s=2, d=HALF)
                            for a in range(PARTS):
                                for s in range(2):
                                    sp.dma_start(dst[which, a, s], spl[k % RING][s * 64:(s + 1) * 64, a, :]).then_inc(stored[k % RING], 16)
                    for r in range(RING):
                        sp.wait_ge(stored[r], 96 * ITEMS // RING * (NCH // 2))

                @block.tensor
                def _(pe):
                    def turn(c, q):
                        norm_turn(pe, nb, xn[q], c)

                    def body(i, last):
                        for q in range(2):
                            c = 2 * i + q
                            pe.wait_ge(nb.xT_ready, c + 1)
                            for f in range(FT):
                                if f == 2 and not (last and q):
                                    turn(c + 1, 1 - q)
                                wait(pe, q_read, FT * c + f - 1)
                                for k in range(KD):
                                    ins = nc.tensor.matmul(pQ[:, f % 2, :], wqk[:, k, f * P:(f + 1) * P], nb.xT[q][:, k, :],
                                                           start=(k == 0), stop=(k == KD - 1))
                                ins.then_inc(q_made, 1)
                            for g in range(2):
                                wait(pe, v_out, 2 * c + g - 1)
                                for j in range(2):
                                    for k in range(KD):
                                        t = 2 * g + j
                                        ins = nc.tensor.matmul(pV[:, g, j, :], nb.xT[q][:, k, t * P:(t + 1) * P], wv[:, k, :],
                                                               start=(k == 0), stop=(k == KD - 1))
                                ins.then_inc(v_made, 1)
                    pair_loop(pe, None, lambda: turn(0, 0), body, NCH // 2)

                @block.scalar
                def _(act):
                    def evacuate(c, q):
                        wait(act, v_made, 2 * (c - 1))
                        norm_evacuate(act, nb, c, q)

                    def high(n, r, uses):
                        act.wait_ge(summed, n + 1)
                        wait(act, stored[r], 96 * uses)
                        nc.scalar.activation(spl[r][:, 0, :], tr[r][:], ACT.Copy).then_inc(hi, 1)

                    def middle(n, r):
                        act.wait_ge(rem_made, n + 1)
                        nc.scalar.activation(spl[r][:, 1, :], rem[r][:], ACT.Copy).then_inc(mid, 1)

                    def body(i, last):
                        for k in range(ITEMS):
                            n = ITEMS * i + k
                            high(n, k % RING, 2 * i + k // RING)
                            if k % FT == 2 and not (last and k >= FT):
                                evacuate(2 * i + k // FT + 1, 1 - k // FT)
                            if not (isinstance(i, int) and i == 0 and k < LAG):
                                middle(n - LAG, (k - LAG) % RING)
                    pair_loop(act, None, lambda: evacuate(0, 0), body, NCH // 2)
                    total = ITEMS * (NCH // 2)
                    for n in range(total - LAG, total):
                        middle(n, n % RING)

                @block.gpsimd
                def _(pool):
                    def add(n, k):
                        pool.wait_ge(q_read, n + 1)
                        wait(pool, rem_made, n - RING + 1)
                        nc.gpsimd.tensor_tensor(out=tr[k % RING][:], in0=ta[k % 2][:], in1=tb[k % 2][:], op=ALU.add).then_inc(summed, 1)

                    def lowest(n, r):
                        pool.wait_ge(mid, n + 1)
                        nc.gpsimd.tensor_tensor(out=spl[r][:, 2, :], in0=rem[r][:], in1=spl[r][:, 1, :], op=ALU.subtract).then_inc(low, 1)

                    def body(i, last):
                        for k in range(ITEMS):
                            n = ITEMS * i + k
                            if k % FT == 1 and not (last and k >= FT):
                                norm_rstd(pool, nb, 2 * i + k // FT + 1, 1 - k // FT)
                            add(n, k)
                            if not (isinstance(i, int) and i == 0 and k < LAG + 1):
                                lowest(n - LAG - 1, (k - LAG - 1) % RING)
                    pair_loop(pool, None, lambda: norm_rstd(pool, nb, 0, 0), body, NCH // 2)
                    total = ITEMS * (NCH // 2)
                    for n in range(total - LAG - 1, total):
                        lowest(n, n % RING)
                    pool.wait_ge(nb.normed, NCH)
                    nc.gpsimd.tensor_tensor(out=XR[:], in0=XR[:], in1=bp[:].unsqueeze(1).to_broadcast([P, TILES, D]),
                                            op=ALU.add).then_inc(low, 1)
                    pool.wait_ge(low, total + 1)

                @block.vector
                def _(dve):
                    steps = Steps(dve, steps_sem)

                    def stats(c, q, n):
                        hold(dve, x_loaded[q], 16 * (n + 1), passed[0])
                        norm_stats(nb, steps, c, q)

                    def rope(n, k, qc):
                        f = k % FT
                        dve.wait_ge(q_made, n + 1)
                        wait(dve, summed, n - 1)
                        cs = cosT[:, bass.ds(qc * CHUNK, CHUNK)]
                        sn = sinT[:, bass.ds(qc * CHUNK, CHUNK)]
                        nc.vector.scalar_tensor_tensor(out=ta[k % 2][:], in0=pQ[:, f % 2, :], scalar=bqk[:, f:f + 1], in1=cs,
                                                       op0=ALU.add, op1=ALU.mult)
                        for a, b in ((0, 64), (64, 0)):
                            ins = nc.vector.scalar_tensor_tensor(out=tb[k % 2][a:a + 64, :], in0=pQ[b:b + 64, f % 2, :],
                                                                 scalar=bqk[b:b + 64, f:f + 1], in1=sn[b:b + 64, :],
                                                                 op0=ALU.add, op1=ALU.mult)
                        ins.then_inc(q_read, 1)

                    def remainder(n, r):
                        dve.wait_ge(hi, n + 1)
                        wait(dve, low, n - RING + 1)
                        nc.vector.tensor_tensor(out=rem[r][:], in0=tr[r][:], in1=spl[r][:, 0, :], op=ALU.subtract).then_inc(rem_made, 1)

                    def head():
                        stats(0, 0, 0)
                        norm_apply(dve, nb, xn[0], 0, 0)

                    def body(i, last):
                        for k in range(ITEMS):
                            n = ITEMS * i + k
                            q, f = divmod(k, FT)
                            c = 2 * i + q
                            more = not (last and q)
                            if f == 0 and more:
                                stats(c + 1, 1 - q, i + q)
                            rope(n, k, 2 * (i % 2) + q)
                            if f == 1 and more:
                                wait(dve, nb.turned, c)
                                norm_apply(dve, nb, xn[1 - q], c + 1, 1 - q)
                            if not (isinstance(i, int) and i == 0 and k < LAG):
                                remainder(n - LAG, (k - LAG) % RING)
                            if f == 3:
                                for g in range(2):
                                    dve.wait_ge(v_made, 2 * c + g + 1)
                                    nc.vector.tensor_tensor(out=VA[:, bass.ds(c * CT + 2 * g, 2), :], in0=pV[:, g],
                                                            in1=bv[:].unsqueeze(1).to_broadcast([P, 2, D]), op=ALU.add).then_inc(v_out, 1)
                    pair_loop(dve, steps, head, body, NCH // 2)
                    total = ITEMS * (NCH // 2)
                    for n in range(total - LAG, total):
                        remainder(n, n % RING)
                    dve.wait_ge(v_out, 2 * NCH)

        def attention(VA):
            with ExitStack() as scope:
                mq = [sb(scope, f"mq{q}", [QROWS, T], BF16) for q in range(2)]
                mk = [sb(scope, f"mk{q}", [QROWS, T], BF16) for q in range(2)]
                eq = [sb(scope, f"eq{q}", [MROWS, T], BF16) for q in range(2)]
                ek = [sb(scope, f"ek{q}", [MROWS, T], BF16) for q in range(2)]
                RING = 4
                pt = [sb(scope, f"pt{r}", [P, T]) for r in range(RING)]
                vh = [sb(scope, f"vh{q}", [P, KT, 32]) for q in range(2)]
                mx4 = [sb(scope, f"mx4{q}", [P, KT, 4]) for q in range(2)]
                mx = sb(scope, "mx", [P, KT])
                ma = sb(scope, "ma", [P, 3, KT])
                mp = sb(scope, "mp", [P, PARTS, 32], BF16)
                mt = sb(scope, "mt", [P, PARTS, 32], BF16)
                oe = [sb(scope, f"oe{q}", [P, CHUNK]) for q in range(2)]
                pS = ps(scope, "pS", [P, 2, 2, CHUNK])
                MB = 3
                pM = ps(scope, "pM", [P, MB, CHUNK])
                pO = ps(scope, "pOv", [P, CHUNK])
                inited = sem("inited")
                m_loaded, e_loaded, m_rows = pair("m_loaded"), pair("e_loaded"), pair("m_rows")
                max_stored = sem("max_stored")
                m_scored, m_reduced, m_done = sem("m_scored"), sem("m_reduced"), sem("m_done")
                pool_steps, m_parted, m_turned = sem("pool_stepsa"), sem("m_parted"), sem("m_turned")
                scored, exped, summed, o_out = sem("scored"), sem("expeda"), sem("summeda"), sem("o_outa")
                v_ready = sem("v_ready")
                o_stored = pair("o_stored")
                block = scope.enter_context(nc.Block())
                HALFS = 2 * KT
                MS = 4 * KT

                def maxima_of(n, u):
                    return (n + 1, u + LEAD) if u + LEAD < KT else (n + 2, u + LEAD - KT)

                def exists(h):
                    return not isinstance(h, int) or h < NH

                def run(eng, body, steps=None):
                    body(-1, 1)
                    if steps:
                        per0 = steps.n
                    body(0, 0)
                    if steps:
                        per = steps.n - per0
                    body(1, 1)
                    with eng.Fori(1, NH // 2 - 2) as i:
                        for q in range(2):
                            if steps:
                                steps.restart(per0 + (2 * i + q) * per)
                            body(2 * i + q, q)
                    for n in range(NH - 4, NH):
                        if steps:
                            steps.restart(per0 + n * per)
                        body(n, n % 2)

                @block.sync
                def _(sp):
                    def load(n, dq, dk, sm):
                        base = n * 2 * PARTS * DH
                        src = [qk_parts[bass.ds(base + w * PARTS * DH, PARTS * DH), :] for w in range(2)]
                        a = 0
                        for part, copies in ((0, 3), (1, 2), (2, 1)):
                            rows = slice(a * DH, (a + copies) * DH)
                            qs = src[0][part * DH:(part + 1) * DH, :].unsqueeze(0).to_broadcast([copies, DH, T])
                            sp.dma_start(dq[rows, :], qs).then_inc(sm, 16)
                            sp.dma_start(dk[rows, :], src[1][0:copies * DH, :]).then_inc(sm, 16)
                            a += copies

                    def max_to_rows(h, q):
                        sp.wait_ge(m_turned, h + 1)
                        sp.dma_start(max_rows[q], mt[:].rearrange("p a i -> p (a i)")).then_inc(max_stored, 16)
                        sp.wait_ge(max_stored, 16 * (h + 1))
                        src = max_rows[q].rearrange("(b j) (a i) -> a j b i", b=4, a=PARTS)[:, 0:KT]
                        for a in range(PARTS):
                            sp.dma_start(eq[q][QROWS + a:QROWS + a + 1, :].rearrange("o (j b i) -> o j b i", j=KT, b=4),
                                         src[a:a + 1]).then_inc(m_rows[q], 16)

                    def body(n, q):
                        first = isinstance(n, int) and n < 0
                        if first:
                            load(0, mq[0], mk[0], m_loaded[0])
                            load(1, mq[1], mk[1], m_loaded[1])
                            load(0, eq[0], ek[0], e_loaded[0])
                            for e in range(NE):
                                sp.dma_start(slots[e * CAP:(e + 1) * CAP, D:D + 2].rearrange("(p j) d -> p j d", p=P),
                                             meta[:, e]).then_inc(slots_ready, 16)
                        else:
                            if exists(n + 1):
                                wait(sp, scored, HALFS * n)
                                load(n + 1, eq[1 - q], ek[1 - q], e_loaded[1 - q])
                            if not (isinstance(n, int) and n == 0):
                                store(n - 1, 1 - q)
                        if exists(n + 1):
                            max_to_rows(n + 1, 1 - q)
                            if exists(n + 3):
                                sp.wait_ge(m_reduced, MS * (n + 2))
                                load(n + 3, mq[1 - q], mk[1 - q], m_loaded[1 - q])

                    def store(h, q):
                        sp.wait_ge(o_out, h + 1)
                        sp.dma_start(attn[bass.ds(h * 32, 32), :].rearrange("r (j t) -> j r t", j=4), oe[q][:]).then_inc(o_stored[q], 16)
                    run(sp, body)
                    store(NH - 1, 1)
                    for q in range(2):
                        sp.wait_ge(o_stored[q], 16 * NH // 2)

                @block.tensor
                def _(pe):
                    def maxima(h, t, q):
                        if t == 0:
                            pe.wait_ge(m_loaded[q], 96 * ((h - q) // 2 + 1 if isinstance(h, int) else h // 2 + 1))
                        for j in range(4):
                            s = 4 * t + j
                            wait(pe, m_reduced, MS * h + (s - MB + 1 if s else 0))
                            nc.tensor.matmul(pM[:, s % MB, :], mq[q][:, t * P:(t + 1) * P], mk[q][:, j * CHUNK:(j + 1) * CHUNK],
                                             start=True, stop=True).then_inc(m_scored, 1)

                    def scores(n, u, g, q):
                        wait(pe, exped, HALFS * n + 2 * u + g - 1)
                        for j in range(2):
                            ins = nc.tensor.matmul(pS[:, g, j, :], ek[q][:, u * P:(u + 1) * P],
                                                   eq[q][:, (2 * g + j) * CHUNK:(2 * g + j + 1) * CHUNK], start=True, stop=True)
                        ins.then_inc(scored, 1)

                    def values(n, u, q):
                        pe.wait_ge(exped, HALFS * n + 2 * u + 2)
                        if u == 0:
                            pe.wait_ge(v_ready, n + 1)
                            wait(pe, o_out, n)
                        for j in range(4):
                            ins = nc.tensor.matmul(pO[32 * j:32 * (j + 1), :], vh[q][:, u, :], pt[u % RING][:, j * CHUNK:(j + 1) * CHUNK],
                                                   start=(u == 0), stop=(u == KT - 1))
                        ins.then_inc(summed, 1)

                    pe.wait_ge(inited, 1)
                    for t in range(LEAD):
                        maxima(0, t, 0)

                    def body(n, q):
                        real = not (isinstance(n, int) and n < 0)
                        for u in range(KT):
                            h, t = maxima_of(n, u)
                            mqq = 1 - q if t >= LEAD else q
                            if real:
                                if u == 0:
                                    half = n // 2
                                    pe.wait_ge(e_loaded[q], 96 * (half + 1))
                                    pe.wait_ge(m_rows[q], 48 * (half + 1))
                                scores(n, u, 0, q)
                            if exists(h):
                                maxima(h, t, mqq)
                            if real:
                                scores(n, u, 1, q)
                                if u:
                                    values(n, u - 1, q)
                                elif not (isinstance(n, int) and n == 0):
                                    values(n - 1, KT - 1, 1 - q)
                    run(pe, body)
                    values(NH - 1, KT - 1, 1)

                @block.scalar
                def _(act):
                    def evacuate(h, q, uses):
                        act.wait_ge(summed, KT * (h + 1))
                        wait(act, o_stored[q], 16 * uses)
                        nc.scalar.activation(oe[q][:], pO[:], ACT.Copy).then_inc(o_out, 1)

                    def body(n, q):
                        if isinstance(n, int) and n < 0:
                            return
                        for u in range(KT):
                            wait(act, summed, KT * n + u - RING + 1)
                            for g in range(2):
                                act.wait_ge(scored, HALFS * n + 2 * u + g + 1)
                                nc.scalar.activation(pt[u % RING][:, g * 1024:(g + 1) * 1024], pS[:, g], ACT.Exp,
                                                     scale=DH ** -0.5).then_inc(exped, 1)
                            if u == 0 and not (isinstance(n, int) and n == 0):
                                evacuate(n - 1, 1 - q, (n - 1) // 2)
                    run(act, body)
                    evacuate(NH - 1, 1, NH // 2 - 1)

                @block.vector
                def _(dve):
                    def reduce(h, t, q):
                        for j in range(4):
                            s = 4 * t + j
                            dve.wait_ge(m_scored, MS * h + s + 1)
                            nc.vector.tensor_reduce(out=mx4[q][:, t, j:j + 1], in_=pM[:, s % MB, :], axis=AX.X,
                                                    op=ALU.max).then_inc(m_reduced, 1)

                    for q in range(2):
                        nc.vector.memset(vh[q][:], 1.0)
                        nc.vector.memset(ek[q][QROWS:MROWS, :], 1.0)
                    nc.vector.memset(mp[:], 0.0).then_inc(inited, 1)
                    for t in range(LEAD):
                        reduce(0, t, 0)

                    def body(n, q):
                        for u in range(KT):
                            h, t = maxima_of(n, u)
                            if exists(h):
                                reduce(h, t, 1 - q if t >= LEAD else q)
                                if t == KT - 1:
                                    dve.wait_ge(m_reduced, MS * (h + 1))
                                    wait(dve, m_parted, h)
                                    nc.vector.tensor_reduce(out=mx[:], in_=mx4[1 - q][:], axis=AX.X, op=ALU.max).then_inc(m_done, 1)
                            if u == KT - 3 and exists(n + 1):
                                dve.wait_ge(m_parted, n + 2)
                                wait(dve, max_stored, 16 * (n + 1))
                                nc.vector.transpose(mt[:], mp[:]).then_inc(m_turned, 1)
                    run(dve, body)

                @block.gpsimd
                def _(pool):
                    steps = Steps(pool, pool_steps)

                    def split_maxima(h):
                        pool.wait_ge(m_done, h + 1)
                        hold(pool, m_turned, h, passed[1])
                        steps.add(nc.gpsimd.tensor_scalar(ma[:, 0], mx[:], -1.0, None, ALU.mult))
                        for a in range(2):
                            steps.settle_alone(passed[1])
                            steps.add(nc.gpsimd.tensor_copy(mp[:, a, 0:KT], ma[:, a]))
                            steps.settle()
                            steps.add(nc.gpsimd.tensor_tensor(out=ma[:, a + 1], in0=ma[:, a], in1=mp[:, a, 0:KT], op=ALU.subtract))
                        steps.settle_alone(passed[1])
                        nc.gpsimd.tensor_copy(mp[:, 2, 0:KT], ma[:, 2]).then_inc(m_parted, 1)

                    pool.wait_ge(inited, 1)

                    def body(n, q):
                        if exists(n + 1):
                            hold(pool, summed, KT * n, passed[1])
                            b = (n + 1) // H
                            h0 = ((n + 1) % H) * DH
                            src = VA[:, bass.ds(b * KT, KT), bass.ds(h0, DH)]
                            nc.gpsimd.tensor_copy(vh[1 - q][:, :, 0:DH], src).then_inc(v_ready, 1)
                            split_maxima(n + 1)
                    run(pool, body, steps)

        with ExitStack() as scope:
            setup(scope)
            route(0, False)
        experts(0)
        with ExitStack() as scope:
            VA = sb(scope, "VA", [P, TILES, D])
            qkv(VA, scope)
            attention(VA)
        route(1, True)
        experts(1)
        with ExitStack() as scope:
            out_stored = sem("out_stored")
            block = scope.enter_context(nc.Block())

            @block.sync
            def _(sp):
                sp.dma_start(out, resid[1][0:N, :]).then_inc(out_stored, 16)
                sp.wait_ge(out_stored, 16)


_INS = ["L0_attn_x", "L0_attn_sin", "L0_attn_cos", "L0_attn_w_qkv", "L0_attn_b_qkv", "L0_attn_w_proj", "L0_attn_b_proj",
        "L0_ffn_w_router", "L0_ffn_b_router", "L0_ffn_w1", "L0_ffn_b1", "L0_ffn_w2", "L0_ffn_b2"]


def kernel(**inputs):
    import numpy as np
    import concourse.bacc as bacc
    from concourse.bass_utils import run_bass_kernel_spmd

    shapes = {"L0_attn_x": (N, D), "L0_attn_b_qkv": (1, 3 * D), "L0_attn_b_proj": (1, D), "L0_ffn_b_router": (1, NE),
              "L0_ffn_w1": (NE * D, FF), "L0_ffn_w2": (NE * FF, D)}
    nc = bacc.Bacc("TRN2", target_bir_lowering=False, num_devices=1)
    arrays, args = {}, []
    for name in _INS:
        a = np.ascontiguousarray(inputs[name])
        a = a.reshape(shapes.get(name, a.shape))
        arrays[name] = a
        args.append(nc.dram_tensor(name, a.shape, mybir.dt.from_np(a.dtype), kind="ExternalInput").ap())
    out = nc.dram_tensor("out", (N, D), F32, kind="ExternalOutput").ap()
    build(nc, *args, out)
    r = run_bass_kernel_spmd(nc, [arrays], core_ids=[0])
    return r.results[0]["out"].reshape(B, T, D)
```

```python
from contextlib import ExitStack

import concourse.bass as bass
from concourse import mybir

F32, BF16, I32 = mybir.dt.float32, mybir.dt.bfloat16, mybir.dt.int32
ALU = mybir.AluOpType
ACT = mybir.ActivationFunctionType
AX = mybir.AxisListType

P = 128
B, T, D = 2, 2048, 256
N = B * T
KD = D // P
H, DH = 16, 16
HALF = DH // 2
N_ROPE = 1369
PREFIX = T - N_ROPE
NE, FF = 8, 1024
KF = FF // P
CAP = int(1.25 * N / NE)
SLOT_TILES = CAP // P
TILES = N // P
CHUNK = 512
CT = CHUNK // P
NCH = N // CHUNK
BCH = T // CHUNK
ROW = D + 2
SLOTS = NE * CAP
EPS = 1e-5
NH = B * H
KT = T // P
PARTS = 3
SPLIT = 6
QROWS = SPLIT * DH
MROWS = QROWS + PARTS
LEAD = 4
FT = 4
HT = P // DH
HH = CAP // 2


def wait(eng, sem, value):
    if not isinstance(value, int) or value > 0:
        eng.wait_ge(sem, value)


def hold(eng, sem, value, passed):
    if not isinstance(value, int) or value > 0:
        eng.wait_ge(sem, value)
        eng.sem_inc(passed, 1)


class Norm:
    pass


class Steps:

    def __init__(self, eng, sem):
        self.eng, self.sem, self.base, self.n = eng, sem, 0, 0

    def add(self, ins):
        ins.then_inc(self.sem, 1)
        self.n += 1

    def settle(self):
        self.eng.wait_ge(self.sem, self.base + self.n)

    def settle_alone(self, passed):
        hold(self.eng, self.sem, self.base + self.n, passed)

    def restart(self, base):
        self.base, self.n = base, 0


def pair_loop(eng, steps, head, body, pairs):
    head()
    at = steps.n if steps else 0
    body(0, False)
    per = steps.n - at if steps else 0
    with eng.Fori(1, pairs - 1) as i:
        if steps:
            steps.restart(i * per + at)
        body(i, False)
    if steps:
        steps.restart((pairs - 1) * per + at)
    body(pairs - 1, True)


def build(nc, x, sin, cos, w_qkv, b_qkv, w_proj, b_proj, w_router, b_router, w1, b1, w2, b2, out):
    ctx = ExitStack()

    def sem(name):
        return ctx.enter_context(nc.semaphore(name))

    def pair(name):
        return [sem(f"{name}{q}") for q in range(2)]

    def sb(scope, name, shape, dt=F32):
        return scope.enter_context(nc.sbuf_tensor(name, shape, dt))

    def ps(scope, name, shape, dt=F32):
        return scope.enter_context(nc.psum_tensor(name, shape, dt))

    slots = nc.dram_tensor("slots", [SLOTS + 2 * N, ROW], F32).ap()
    resid = [nc.dram_tensor(f"resid{m}", [N + CAP, D], F32).ap() for m in range(2)]
    qk_parts = nc.dram_tensor("qk_parts", [B * FT * PARTS * P, T], BF16).ap()
    max_rows = nc.dram_tensor("max_rows", [2, P, PARTS * 32], BF16).ap()
    attn = nc.dram_tensor("attn", [NH * 32, T], F32).ap()
    rden = nc.dram_tensor("rden", [NH, T], F32).ap()

    with ctx:
        XR = sb(ctx, "XR", [P, TILES, D])
        W1 = [sb(ctx, f"W1_{q}", [P, KD, FF]) for q in range(2)]
        W2 = [sb(ctx, f"W2_{q}", [P, KF, D]) for q in range(2)]
        B2 = [sb(ctx, f"B2_{q}", [P, D]) for q in range(2)]
        b1T = sb(ctx, "b1T", [P, NE * KF])
        ident = sb(ctx, "ident", [P, P])
        ones = sb(ctx, "ones", [P, P], BF16)
        before = sb(ctx, "before", [P, P], BF16)
        em8 = sb(ctx, "em8", [P, CT, NE])
        tok_id = sb(ctx, "tok_id", [P, TILES], I32)
        trash = sb(ctx, "trash", [P, 2, TILES])
        mhalf = sb(ctx, "mhalf", [P, CT])
        wr = sb(ctx, "wr", [P, KD, NE])
        br = sb(ctx, "br", [P, NE])
        wqk = sb(ctx, "wqk", [P, KD, FT * P])
        wv = sb(ctx, "wv", [P, KD, D])
        wp = sb(ctx, "wp", [P, KD, D])
        bqk = sb(ctx, "bqk", [P, FT])
        bv = sb(ctx, "bv", [P, D])
        bp = sb(ctx, "bp", [P, D])
        meta = sb(ctx, "meta", [P, SLOT_TILES, 2])
        cosT = sb(ctx, "cosT", [P, T])
        sinT = sb(ctx, "sinT", [P, T])

        w_loaded = pair("w_loaded")
        slots_ready = sem("slots_ready")
        spare_ready = sem("spare_ready")
        passed = [sem(f"passed_{e}") for e in ("dve", "pool", "sp")]
        resid_ready = [sem(f"resid_ready{m}") for m in range(2)]

        def load_weights(sp, e, q):
            sp.dma_start(W1[q][:], w1[bass.ds(e * D, D), :].rearrange("(k p) f -> p k f", p=P)).then_inc(w_loaded[q], 16)
            sp.dma_start(W2[q][:], w2[bass.ds(e * FF, FF), :].rearrange("(k p) f -> p k f", p=P)).then_inc(w_loaded[q], 16)
            sp.dma_start(B2[q][:], b2[bass.ds(e, 1), :].to_broadcast([P, D])).then_inc(w_loaded[q], 16)

        consts = sem("consts")
        CONSTS = 3

        class Setup:
            pass

        def setup(scope):
            b1_nat = sb(scope, "b1_nat", [NE * KF, P])
            empty = sb(scope, "empty", [P, SLOT_TILES, ROW])
            itmp = sb(scope, "itmp", [P, CT * NE], I32)
            itrash = sb(scope, "itrash", [P, 2 * TILES], I32)
            empty_made, setup_steps = sem("empty_made"), sem("setup_steps")
            first_loaded, b1_turned, b1_out = sem("first_loaded"), sem("b1_turned"), sem("b1_out")
            start = Setup()
            start.first_loaded = first_loaded

            def sync(sp):
                sp.dma_start(wr[:], w_router.rearrange("(k p) f -> p k f", p=P)).then_inc(first_loaded, 16)
                sp.dma_start(br[:], b_router.to_broadcast([P, NE])).then_inc(first_loaded, 16)
                sp.dma_start(b1_nat[:], b1.rearrange("e (k p) -> (e k) p", p=P)).then_inc(first_loaded, 16)

            def gpsimd(pool):
                steps = Steps(pool, setup_steps)
                steps.add(nc.gpsimd.memset(empty[:], 0.0))
                nc.gpsimd.memset(mhalf[:], -0.5)
                steps.settle()
                nc.gpsimd.iota(empty[:].bitcast(I32)[:, :, D + 1], pattern=[[1, SLOT_TILES]], base=N,
                               channel_multiplier=SLOT_TILES).then_inc(empty_made, 1)
                steps.add(nc.gpsimd.memset(ident[:], 0.0))
                steps.add(nc.gpsimd.memset(before[:], 0.0))
                nc.gpsimd.memset(ones[:], 1.0)
                steps.settle()
                nc.gpsimd.affine_select(out=ident[:], in_=ident[:], compare_op=ALU.not_equal, fill=1.0, base=0,
                                        pattern=[[-1, P]], channel_multiplier=1)
                nc.gpsimd.affine_select(out=before[:], in_=before[:], compare_op=ALU.is_ge, fill=1.0, base=0,
                                        pattern=[[-1, P]], channel_multiplier=1).then_inc(consts, 1)
                nc.gpsimd.iota(tok_id[:], pattern=[[P, TILES]], base=0, channel_multiplier=1)
                steps.add(nc.gpsimd.iota(itmp[:], pattern=[[0, CT], [1, NE]], base=-NE, channel_multiplier=0))
                steps.add(nc.gpsimd.iota(itrash[:], pattern=[[N, 2], [P, TILES]], base=SLOTS, channel_multiplier=1))
                steps.settle()
                nc.gpsimd.tensor_copy(em8[:].rearrange("p a b -> p (a b)"), itmp[:])
                nc.gpsimd.tensor_copy(trash[:].rearrange("p a b -> p (a b)"), itrash[:]).then_inc(consts, 1)
                nc.gpsimd.tensor_copy(meta[:].bitcast(I32)[:, :, 0], empty[:].bitcast(I32)[:, :, D])
                pool.wait_ge(empty_made, 1)
                nc.gpsimd.tensor_copy(meta[:].bitcast(I32)[:, :, 1], empty[:].bitcast(I32)[:, :, D + 1]).then_inc(consts, 1)

            def tensor(pe):
                pe.wait_ge(consts, 1)
                pe.wait_ge(first_loaded, 48)
                nc.tensor.transpose(start.bank, b1_nat[:], ident[0:NE * KF, 0:NE * KF]).then_inc(b1_turned, 1)
                pe.wait_ge(b1_out, 1)

            def scalar(act):
                act.wait_ge(empty_made, 1)
                for e in range(NE):
                    act.dma_start(slots[e * CAP:(e + 1) * CAP, :].rearrange("(p j) d -> p j d", p=P), empty[:]).then_inc(slots_ready, 16)
                for m in range(2):
                    act.dma_start(resid[m][N:N + CAP, :].rearrange("(p j) d -> p j d", p=P), empty[:, :, 0:D]).then_inc(spare_ready, 16)
                act.wait_ge(b1_turned, 1)
                nc.scalar.activation(b1T[:], start.bank, ACT.Copy).then_inc(b1_out, 1)

            start.sync, start.gpsimd, start.tensor, start.scalar = sync, gpsimd, tensor, scalar
            return start

        class Prepare:
            pass

        def prepare(scope):
            wq_nat = sb(scope, "wq_nat", [P, KD, 3 * D])
            tab = sb(scope, "tab", [P, 2, KT, DH])
            wide = sb(scope, "wide", [P, 2, 4, P])
            small_loaded, tab_set, tab_loaded = sem("small_loaded"), sem("tab_set"), sem("tab_loaded")
            wide_made, wide_turned, tab_written = sem("wide_made"), sem("wide_turned"), sem("tab_written")
            weights_made = sem("weights_made")
            SMALL = 4 + 2 * FT
            prep = Prepare()

            def sync(sp):
                sp.dma_start(wq_nat[:], w_qkv.rearrange("(k p) f -> p k f", p=P)).then_inc(small_loaded, 16)
                sp.dma_start(wp[:], w_proj.rearrange("(k p) f -> p k f", p=P)).then_inc(small_loaded, 16)
                sp.dma_start(bv[:], b_qkv[:, 2 * D:3 * D].to_broadcast([P, D])).then_inc(small_loaded, 16)
                sp.dma_start(bp[:], b_proj.to_broadcast([P, D])).then_inc(small_loaded, 16)
                for f in range(FT):
                    for s in range(2):
                        src = b_qkv[0, f * P:(f + 1) * P].rearrange("(h s d) -> s h d", h=HT, s=2)[s]
                        sp.dma_start(bqk[s * 64:(s + 1) * 64, f:f + 1], src).then_inc(small_loaded, 16)
                sp.wait_ge(tab_set, 1)
                t0, p0 = PREFIX // P, PREFIX % P
                for n, src in enumerate((cos, sin)):
                    sp.dma_start(tab[p0:P, n, t0, :], src[0:P - p0, :]).then_inc(tab_loaded, 16)
                    sp.dma_start(tab[:, n, t0 + 1:KT, :],
                                 src[P - p0:N_ROPE, :].rearrange("(t p) d -> p t d", p=P)).then_inc(tab_loaded, 16)

            def gpsimd(pool):
                nc.gpsimd.memset(tab[:, 0], 1.0)
                nc.gpsimd.memset(tab[:, 1], 0.0).then_inc(tab_set, 1)
                pool.wait_ge(small_loaded, 16 * SMALL)
                for k in range(KD):
                    for f in range(FT):
                        dst = wqk[:, k, f * P:(f + 1) * P].rearrange("p (s h d) -> p s h d", s=2, h=HT)
                        src = wq_nat[:, k, f * P:(f + 1) * P].rearrange("p (h s d) -> p s h d", h=HT, s=2)
                        nc.gpsimd.tensor_copy(dst, src)
                nc.gpsimd.tensor_copy(wv[:], wq_nat[:, :, 2 * D:3 * D]).then_inc(weights_made, 1)
                pool.wait_ge(weights_made, 1)

            def vector(dve):
                dve.wait_ge(tab_loaded, 64)
                for g in range(8):
                    n, t0 = g // 4, 4 * (g % 4)
                    if g >= 2:
                        dve.wait_ge(wide_turned, g - 1)
                    for s in range(2):
                        src = s if n == 0 else 1 - s
                        src = tab[:, n, t0:t0 + 4, src * HALF:(src + 1) * HALF].unsqueeze(2).to_broadcast([P, 4, HT, HALF])
                        dst = wide[:, g % 2, :, s * 64:(s + 1) * 64].rearrange("p t (h d) -> p t h d", h=HT)
                        last = nc.vector.tensor_scalar(dst, src, -1.0 if n == 1 and s == 1 else 1.0, None, ALU.mult)
                    last.then_inc(wide_made, 1)

            def tensor(pe):
                for g in range(8):
                    pe.wait_ge(wide_made, g + 1)
                    if g >= 2:
                        pe.wait_ge(tab_written, g - 1)
                    for j in range(4):
                        last = nc.tensor.transpose(prep.banks[g % 2][:, j * P:(j + 1) * P], wide[:, g % 2, j, :], ident[:])
                    last.then_inc(wide_turned, 1)

            def scalar(act):
                for g in range(8):
                    act.wait_ge(wide_turned, g + 1)
                    dst = (cosT, sinT)[g // 4][:, (g % 4) * CHUNK:(g % 4 + 1) * CHUNK]
                    nc.scalar.activation(dst, prep.banks[g % 2], ACT.Copy).then_inc(tab_written, 1)
                act.wait_ge(tab_written, 8)

            prep.sync, prep.gpsimd, prep.vector, prep.tensor, prep.scalar = sync, gpsimd, vector, tensor, scalar
            return prep

        def denominators(b):
            rows = attn[b * H * 32:(b + 1) * H * 32, :].rearrange("(h r) (a t) -> r h a t", r=32, a=P // H)
            return rows[DH]

        def reciprocals(b):
            return rden[b * H:(b + 1) * H, :].rearrange("h (a t) -> (h a) t", a=P // H)

        def norm_buffers(scope, tag):
            nb = Norm()
            nb.st = [sb(scope, f"st{tag}{q}", [P, CT, 6]) for q in range(2)]
            nb.mv = [sb(scope, f"mv{tag}{q}", [P, CT, 2]) for q in range(2)]
            nb.ve = [sb(scope, f"ve{tag}{q}", [P, CT]) for q in range(2)]
            nb.rs = [sb(scope, f"rs{tag}{q}", [P, CT]) for q in range(2)]
            nb.xn = [sb(scope, f"xn{tag}{q}", [P, CT, D]) for q in range(2)]
            nb.xT = [sb(scope, f"xT{tag}{q}", [P, KD, CHUNK]) for q in range(2)]
            nb.pT = ps(scope, f"pT{tag}", [P, KD, CHUNK])
            nb.stats, nb.ve_made, nb.rstd = sem(f"stats{tag}"), sem(f"ve_made{tag}"), sem(f"rstd{tag}")
            nb.normed, nb.turned, nb.xT_ready = sem(f"normed{tag}"), sem(f"turned{tag}"), sem(f"xT_ready{tag}")
            return nb

        def norm_stats(nb, steps, c, q):
            for j in range(CT):
                ins = nc.vector.bn_stats(nb.st[q][:, j, :], XR[:, bass.ds(c * CT + j, 1), :].rearrange("p a d -> p (a d)"))
            steps.add(ins)
            steps.settle_alone(passed[0])
            for j in range(CT):
                ins = nc.vector.bn_aggr(nb.mv[q][:, j, :], nb.st[q][:, j, :])
            ins.then_inc(nb.stats, 1)

        def norm_rstd(pool, nb, c, q):
            hold(pool, nb.stats, c + 1, passed[1])
            nc.gpsimd.tensor_scalar(nb.ve[q][:], nb.mv[q][:, :, 1], EPS, None, ALU.add).then_inc(nb.ve_made, 1)
            pool.wait_ge(nb.ve_made, c + 1)
            nc.gpsimd.tensor_tensor(out=nb.rs[q][:], in0=nb.ve[q][:], in1=mhalf[:], op=ALU.pow).then_inc(nb.rstd, 1)

        def norm_apply(dve, nb, c, q):
            wait(dve, nb.turned, c - 1)
            dve.wait_ge(nb.stats, c + 1)
            dve.wait_ge(nb.rstd, c + 1)
            for j in range(CT):
                ins = nc.vector.tensor_scalar(nb.xn[q][:, j, :], XR[:, bass.ds(c * CT + j, 1), :].rearrange("p a d -> p (a d)"),
                                              nb.mv[q][:, j, 0:1], nb.rs[q][:, j:j + 1], ALU.subtract, ALU.mult)
            ins.then_inc(nb.normed, 1)

        def norm_turn(pe, nb, c, q):
            pe.wait_ge(nb.normed, c + 1)
            wait(pe, nb.xT_ready, c)
            for k in range(KD):
                for j in range(CT):
                    ins = nc.tensor.transpose(nb.pT[:, k, j * P:(j + 1) * P], nb.xn[q][:, j, k * P:(k + 1) * P], ident[:])
            ins.then_inc(nb.turned, 1)

        def norm_evacuate(act, nb, c, q):
            act.wait_ge(nb.turned, c + 1)
            nc.scalar.activation(nb.xT[q][:], nb.pT[:], ACT.Copy).then_inc(nb.xT_ready, 1)

        def bank_pair(scope, name):
            banks = ps(scope, name, [P, 2, CHUNK])
            return [banks[:, q, 0:CT * NE].rearrange("p (j e) -> p j e", j=CT) for q in range(2)]

        def route(m, project, start=None):
            tag = f"r{m}"
            with ExitStack() as scope:
                nb = norm_buffers(scope, tag)
                rows = [sb(scope, f"rows{tag}{q}", [P, 2, CT, ROW]) for q in range(2)]
                lg = [sb(scope, f"lg{tag}{q}", [P, CT, NE]) for q in range(2)]
                l2 = [sb(scope, f"l2{tag}{q}", [P, CT, NE]) for q in range(2)]
                eq = [sb(scope, f"eq{tag}{q}", [P, 2, CT, NE]) for q in range(2)]
                oh = [sb(scope, f"oh{tag}{q}", [P, 2, CT, NE]) for q in range(2)]
                top = [sb(scope, f"top{tag}{q}", [P, 2, CT]) for q in range(2)]
                em = [sb(scope, f"em{tag}{q}", [P, 2, CT]) for q in range(2)]
                mask = [sb(scope, f"mask{tag}{q}", [P, CT, NE], BF16) for q in range(2)]
                less = [sb(scope, f"less{tag}{q}", [P, CT, NE + 1]) for q in range(2)]
                ex = [sb(scope, f"ex{tag}{q}", [P, CT, NE + 1]) for q in range(2)]
                seen = [sb(scope, f"seen{tag}{q}", [P, NE]) for q in range(2)]
                seen_b = [sb(scope, f"seen_b{tag}{q}", [P, NE], BF16) for q in range(2)]
                here = sb(scope, f"here{tag}", [P, NE])
                hit = sb(scope, f"hit{tag}", [P, 2, CT, NE])
                pos = sb(scope, f"pos{tag}", [P, 2, CT])
                keep = sb(scope, f"keep{tag}", [P, 2, CT])
                slot = sb(scope, f"slot{tag}", [P, 2, CT])
                off = sb(scope, f"off{tag}", [P, 2, CT])
                gate = sb(scope, f"gate{tag}", [P, 2, CT])
                gsum = sb(scope, f"gsum{tag}", [P, 2, CT])
                dest = [sb(scope, f"dest{tag}{q}", [P, 2, CT], I32) for q in range(2)]
                pL = bank_pair(scope, f"pL{tag}")
                pP = bank_pair(scope, f"pP{tag}")
                steps_sem = sem(f"dve_steps{tag}")
                x_loaded = pair(f"x_loaded{tag}")
                row_copied, logits = sem(f"row_copied{tag}"), sem(f"logits{tag}")
                masked, prefixed = sem(f"masked{tag}"), sem(f"prefixed{tag}")
                less_made, exped = sem(f"less_made{tag}"), sem(f"exped{tag}")
                routed, scattered = sem(f"routed{tag}"), pair(f"scattered{tag}")
                x_ready, x_stored = sem(f"x_ready{tag}"), sem(f"x_stored{tag}")
                if project:
                    num = [sb(scope, f"num{q}", [P, KD, CHUNK]) for q in range(2)]
                    rcp = [sb(scope, f"rcp{q}", [P, KD, CHUNK]) for q in range(2)]
                    onT = [sb(scope, f"onT{q}", [P, KD, CHUNK]) for q in range(2)]
                    den = sb(scope, "den1", [P, H * T // P])
                    pY = ps(scope, "pY", [P, 2, 2, D])
                    den_loaded, den_inv, rden_stored = sem("den_loaded"), sem("den_inv"), sem("rden_stored")
                    o_loaded, o_made, projected = pair("o_loaded"), sem("o_made"), sem("projected")
                if not project:
                    start.bank = nb.pT[:, 0, 0:NE * KF]
                block = scope.enter_context(nc.Block())

                @block.sync
                def _(sp):
                    if not project:

                        def load(c, q, n):
                            wait(sp, x_loaded[q], 16 * n)
                            sp.dma_start(XR[:, bass.ds(c * CT, CT), :],
                                         x[bass.ds(c * CHUNK, CHUNK), :].rearrange("(t p) d -> p t d", p=P)).then_inc(x_loaded[q], 16)
                        load(0, 0, 0)
                        load(1, 1, 0)
                        start.sync(sp)
                        with sp.Fori(1, NCH // 2) as i:
                            for q in range(2):
                                load(2 * i + q, q, i)
                        quarter = N // 4
                        for g in range(4):
                            sp.wait_ge(routed, 3 + g)
                            if g % 2 == 0:
                                load_weights(sp, g // 2, g // 2)
                            sp.dma_start(resid[m][g * quarter:(g + 1) * quarter, :],
                                         x[g * quarter:(g + 1) * quarter, :]).then_inc(resid_ready[m], 16)
                        return

                    def load(i, q):
                        if not isinstance(i, int) or i > 0:
                            hold(sp, o_made, 2 * i + q - 1, passed[2])
                        b, qc = i // 2, 2 * (i % 2) + q
                        for k in range(KD):
                            h0 = b * H + k * HT
                            src = attn[bass.ds(h0 * 32, HT * 32), bass.ds(qc * CHUNK, CHUNK)]
                            sp.dma_start(num[q][:, k, :], src.rearrange("(h r) t -> h r t", r=32)[:, 0:DH, :]).then_inc(o_loaded[q], 16)
                            src = rden[bass.ds(h0, HT), bass.ds(qc * CHUNK, CHUNK)]
                            sp.dma_start(rcp[q][:, k, :], src.unsqueeze(1).to_broadcast([HT, DH, CHUNK])).then_inc(o_loaded[q], 16)

                    def store(c):
                        sp.wait_ge(x_ready, c + 1)
                        sp.dma_start(resid[m][bass.ds(c * CHUNK, CHUNK), :].rearrange("(t p) d -> p t d", p=P),
                                     XR[:, bass.ds(c * CT, CT), :]).then_inc(x_stored, 16)
                        hold(sp, x_stored, 16 * (c + 1), passed[2])
                    load(0, 0)
                    load(0, 1)
                    sp.dma_start(den[:], denominators(1)).then_inc(den_loaded, 16)
                    for q in range(2):
                        load(1, q)
                        store(q)
                    sp.wait_ge(den_inv, 1)
                    sp.dma_start(reciprocals(1), den[:]).then_inc(rden_stored, 16)
                    sp.wait_ge(rden_stored, 16)
                    with sp.Fori(2, NCH // 2) as i:
                        for q in range(2):
                            load(i, q)
                            store(2 * i + q - 2)
                    for c in (NCH - 2, NCH - 1):
                        store(c)

                @block.tensor
                def _(pe):
                    def attend(c, q):
                        pe.wait_ge(o_made, c + 1)
                        wait(pe, x_ready, c)
                        for j in range(CT):
                            for k in range(KD):
                                ins = nc.tensor.matmul(pY[:, j // 2, j % 2, :], onT[q][:, k, j * P:(j + 1) * P], wp[:, k, :],
                                                       start=(k == 0), stop=(k == KD - 1))
                        ins.then_inc(projected, 1)

                    def score(c, q):
                        pe.wait_ge(nb.xT_ready, c + 1)
                        wait(pe, masked, c - 1)
                        for j in range(CT):
                            for k in range(KD):
                                ins = nc.tensor.matmul(pL[q][:, j, :], nb.xT[q][:, k, j * P:(j + 1) * P], wr[:, k, :],
                                                       start=(k == 0), stop=(k == KD - 1))
                        ins.then_inc(logits, 1)

                    def prefix(c, q):
                        pe.wait_ge(masked, c + 1)
                        nc.tensor.matmul(pP[q], before[:], mask[q][:], start=True, stop=False)
                        for j in range(CT - 1):
                            nc.tensor.matmul(pP[q][:, j + 1:CT, :], ones[:],
                                             mask[q][:, j:j + 1, :].to_broadcast([P, CT - 1 - j, NE]), start=False, stop=False)
                        nc.tensor.matmul(pP[q], ones[:], seen_b[q][:].unsqueeze(1).to_broadcast([P, CT, NE]),
                                         start=False, stop=True).then_inc(prefixed, 1)

                    def head():
                        if project:
                            attend(0, 0)
                            attend(1, 1)
                        else:
                            start.tensor(pe)
                        norm_turn(pe, nb, 0, 0)
                        score(0, 0)

                    def body(i, last):
                        for q in range(2):
                            c = 2 * i + q
                            if project and not last:
                                attend(c + 2, q)
                            if not (last and q):
                                norm_turn(pe, nb, c + 1, 1 - q)
                            prefix(c, q)
                            if not (last and q):
                                score(c + 1, 1 - q)
                    pair_loop(pe, None, head, body, NCH // 2)

                @block.scalar
                def _(act):
                    def evacuate(c, q):
                        wait(act, logits, c - 1)
                        norm_evacuate(act, nb, c, q)

                    def body(i, last):
                        for q in range(2):
                            c = 2 * i + q
                            if not (last and q):
                                evacuate(c + 1, 1 - q)
                            act.wait_ge(less_made, c + 1)
                            nc.scalar.activation(ex[q][:], less[q][:], ACT.Exp).then_inc(exped, 1)
                            act.wait_ge(nb.normed, c + 1)
                            wait(act, scattered[q], 128 * i)
                            nc.scalar.activation(rows[q][:, :, :, 0:D], nb.xn[q][:].unsqueeze(1).to_broadcast([P, 2, CT, D]),
                                                 ACT.Copy).then_inc(row_copied, 1)

                    def head():
                        if not project:
                            start.scalar(act)
                        evacuate(0, 0)
                    pair_loop(act, None, head, body, NCH // 2)

                @block.gpsimd
                def _(pool):
                    def scatter(c, q):
                        pool.wait_ge(routed, c + 1)
                        hold(pool, row_copied, c + 1, passed[1])
                        for k in range(2):
                            for j in range(CT):
                                nc.gpsimd.indirect_dma_start(
                                    out=slots, out_offset=bass.IndirectOffsetOnAxis(ap=dest[q][:, k, j:j + 1], axis=0),
                                    in_=rows[q][:, k, j, :], in_offset=None).then_inc(scattered[q], 16)

                    def body(i, last):
                        for q in range(2):
                            if not last:
                                norm_rstd(pool, nb, 2 * i + q + 2, q)
                            scatter(2 * i + q, q)

                    def head():
                        if not project:
                            start.gpsimd(pool)
                        norm_rstd(pool, nb, 0, 0)
                        norm_rstd(pool, nb, 1, 1)
                        pool.wait_ge(slots_ready, 16 * NE * (m + 1))
                    pair_loop(pool, None, head, body, NCH // 2)
                    for q in range(2):
                        pool.wait_ge(scattered[q], 128 * (NCH // 2))
                    pool.wait_ge(spare_ready, 32)

                @block.vector
                def _(dve):
                    steps = Steps(dve, steps_sem)

                    def divide(c, q, n):
                        dve.wait_ge(o_loaded[q], 64 * (n + 1))
                        wait(dve, projected, c - 1)
                        nc.vector.tensor_tensor(out=onT[q][:], in0=num[q][:], in1=rcp[q][:], op=ALU.mult).then_inc(o_made, 1)

                    def residual(c, q, n):
                        if not project:
                            hold(dve, x_loaded[q], 16 * (n + 1), passed[0])
                            return
                        dve.wait_ge(projected, c + 1)
                        for g in range(2):
                            xs = XR[:, bass.ds(c * CT + 2 * g, 2), :]
                            ins = nc.vector.tensor_tensor(out=xs, in0=pY[:, g], in1=xs, op=ALU.add)
                        ins.then_inc(x_ready, 1)
                        hold(dve, x_ready, c + 1, passed[0])

                    def bc(ap):
                        return ap.unsqueeze(2).to_broadcast([P, CT, NE])

                    def choose(c, q):
                        dve.wait_ge(logits, c + 1)
                        steps.add(nc.vector.tensor_tensor(out=lg[q][:], in0=pL[q],
                                                          in1=br[:].unsqueeze(1).to_broadcast([P, CT, NE]), op=ALU.add))
                        steps.settle()
                        for k, src in enumerate((lg[q], l2[q])):
                            steps.add(nc.vector.tensor_reduce(out=top[q][:, k, :], in_=src[:], axis=AX.X, op=ALU.max))
                            steps.settle()
                            steps.add(nc.vector.tensor_tensor(out=eq[q][:, k], in0=src[:], in1=bc(top[q][:, k, :]), op=ALU.is_equal))
                            steps.settle()
                            steps.add(nc.vector.tensor_tensor(out=hit[:, k], in0=eq[q][:, k], in1=em8[:], op=ALU.mult))
                            steps.settle()
                            steps.add(nc.vector.tensor_reduce(out=em[q][:, k, :], in_=hit[:, k], axis=AX.X, op=ALU.min))
                            steps.settle()
                            steps.add(nc.vector.tensor_tensor(out=oh[q][:, k], in0=em8[:], in1=bc(em[q][:, k, :]), op=ALU.is_equal))
                            steps.settle()
                            if k == 0:
                                steps.add(nc.vector.scalar_tensor_tensor(out=l2[q][:], in0=oh[q][:, 0], scalar=-3e38,
                                                                         in1=lg[q][:], op0=ALU.mult, op1=ALU.add))
                                steps.settle()
                        nc.vector.tensor_tensor(out=mask[q][:], in0=oh[q][:, 0], in1=oh[q][:, 1], op=ALU.add).then_inc(masked, 1)
                        nc.vector.tensor_tensor(out=less[q][:, :, 0:NE], in0=lg[q][:], in1=bc(top[q][:, 0, :]), op=ALU.subtract)
                        nc.vector.tensor_tensor(out=less[q][:, :, NE], in0=top[q][:, 1, :], in1=top[q][:, 0, :],
                                                op=ALU.subtract).then_inc(less_made, 1)

                    def place(c, q, n):
                        dve.wait_ge(prefixed, c + 1)
                        dve.wait_ge(masked, c + 1)
                        steps.add(nc.vector.tensor_tensor(out=hit[:], in0=oh[q][:],
                                                          in1=pP[q].unsqueeze(1).to_broadcast([P, 2, CT, NE]), op=ALU.mult))
                        steps.add(nc.vector.tensor_reduce(out=here[:], in_=mask[q][:].rearrange("p j e -> p e j"), axis=AX.X, op=ALU.add))
                        steps.settle()
                        steps.add(nc.vector.tensor_reduce(out=pos[:], in_=hit[:], axis=AX.X, op=ALU.add))
                        steps.add(nc.vector.tensor_tensor(out=seen[1 - q][:], in0=seen[q][:], in1=here[:], op=ALU.add))
                        steps.add(nc.vector.tensor_scalar(slot[:], em[q][:], float(NE), float(CAP), ALU.add, ALU.mult))
                        dve.wait_ge(exped, c + 1)
                        steps.add(nc.vector.tensor_reduce(out=gsum[:, 0, :], in_=ex[q][:, :, 0:NE], axis=AX.X, op=ALU.add))
                        steps.settle()
                        steps.add(nc.vector.tensor_copy(seen_b[1 - q][:], seen[1 - q][:]))
                        steps.add(nc.vector.tensor_scalar(keep[:], pos[:], float(CAP), None, ALU.is_lt))
                        steps.add(nc.vector.tensor_tensor(out=off[:], in0=slot[:], in1=pos[:], op=ALU.add))
                        steps.add(nc.vector.reciprocal(gate[:, 0, :], gsum[:, 0, :]))
                        steps.settle()
                        steps.add(nc.vector.tensor_tensor(out=off[:], in0=off[:], in1=trash[:, :, bass.ds(c * CT, CT)], op=ALU.subtract))
                        steps.add(nc.vector.tensor_tensor(out=gate[:, 1, :], in0=ex[q][:, :, NE], in1=gate[:, 0, :], op=ALU.mult))
                        steps.settle()
                        steps.add(nc.vector.tensor_tensor(out=off[:], in0=off[:], in1=keep[:], op=ALU.mult))
                        steps.add(nc.vector.tensor_tensor(out=gate[:], in0=gate[:], in1=keep[:], op=ALU.mult))
                        steps.settle()
                        wait(dve, scattered[q], 128 * n)
                        steps.add(nc.vector.tensor_tensor(out=dest[q][:], in0=off[:], in1=trash[:, :, bass.ds(c * CT, CT)], op=ALU.add))
                        steps.add(nc.vector.tensor_tensor(out=gsum[:, 0, :], in0=gate[:, 0, :], in1=gate[:, 1, :], op=ALU.add))
                        steps.settle()
                        steps.add(nc.vector.tensor_scalar(gsum[:, 0, :], gsum[:, 0, :], 1e-6, 2.0, ALU.max, ALU.mult))
                        steps.settle()
                        steps.add(nc.vector.reciprocal(gsum[:, 1, :], gsum[:, 0, :]))
                        steps.settle()
                        nc.vector.tensor_copy(rows[q][:].bitcast(I32)[:, :, :, D + 1],
                                              tok_id[:, bass.ds(c * CT, CT)].unsqueeze(1).to_broadcast([P, 2, CT]))
                        nc.vector.tensor_tensor(out=rows[q][:, :, :, D], in0=gate[:],
                                                in1=gsum[:, 1, :].unsqueeze(1).to_broadcast([P, 2, CT]),
                                                op=ALU.mult).then_inc(routed, 1)

                    def normalise(c, q):
                        wait(dve, row_copied, c - 1)
                        norm_apply(dve, nb, c, q)

                    def head():
                        steps.add(nc.vector.memset(seen[0][:], 0.0))
                        steps.add(nc.vector.memset(seen_b[0][:], 0.0))
                        if project:
                            divide(0, 0, 0)
                            divide(1, 1, 0)
                        for c in range(2):
                            residual(c, c, 0)
                            norm_stats(nb, steps, c, c)
                        normalise(0, 0)
                        if not project:
                            dve.wait_ge(consts, CONSTS)
                            dve.wait_ge(start.first_loaded, 48)

                    def body(i, last):
                        for q in range(2):
                            c = 2 * i + q
                            if project and not last:
                                divide(c + 2, q, i + 1)
                            if not (last and q):
                                normalise(c + 1, 1 - q)
                            choose(c, q)
                            if not last:
                                residual(c + 2, q, i + 1)
                                norm_stats(nb, steps, c + 2, q)
                            place(c, q, i)
                            if project and isinstance(i, int) and c == 0:
                                dve.wait_ge(den_loaded, 16)
                                nc.vector.reciprocal(den[:], den[:]).then_inc(den_inv, 1)
                    pair_loop(dve, steps, head, body, NCH // 2)

        def experts(m):
            tag = f"e{m}"
            with ExitStack() as scope:
                prep = prepare(scope) if m == 0 else None
                XE = [sb(scope, f"XE{tag}{q}", [P, SLOT_TILES, ROW]) for q in range(2)]
                XT = [sb(scope, f"XT{tag}{q}", [P, KD, CAP]) for q in range(2)]
                hid = sb(scope, f"hid{tag}", [P, KF, CAP])
                b1c = [sb(scope, f"b1c{tag}{q}", [P, KF]) for q in range(2)]
                Y = [sb(scope, f"Y{tag}{q}", [P, SLOT_TILES, D]) for q in range(2)]
                yb = [sb(scope, f"yb{tag}{q}", [P, D]) for q in range(2)]
                pX = ps(scope, f"pX{tag}", [P, 2, KD, D])
                pH = ps(scope, f"pH{tag}", [P, 2, 2, CHUNK])
                pO = ps(scope, f"pO{tag}", [P, 2, CHUNK])
                x_in, x_turned, x_out = pair(f"x_in{tag}"), sem(f"x_turned{tag}"), sem(f"x_out{tag}")
                h_made, h_out, bias_in = sem(f"h_made{tag}"), sem(f"h_out{tag}"), sem(f"bias_in{tag}")
                o_made, o_out, y_made = sem(f"o_made{tag}"), sem(f"o_out{tag}"), sem(f"y_made{tag}")
                added = sem(f"added{tag}")
                block = scope.enter_context(nc.Block())
                if prep:
                    prep.banks = [pO[:, g, :] for g in range(2)]
                GROUPS = [(0, 2), (2, 4), (4, 5)]
                NG = len(GROUPS)

                @block.sync
                def _(sp):
                    def load_slots(e, q):
                        sp.dma_start(XE[q][:], slots[bass.ds(e * CAP, CAP), :].rearrange("(j p) d -> p j d", p=P)).then_inc(x_in[q], 16)

                    for q in range(2):
                        load_slots(q, q)
                    if prep:
                        prep.sync(sp)

                    def body(i):
                        for q in range(2):
                            e = 2 * i + q + 2
                            sp.wait_ge(added, 16 * SLOT_TILES * (e - 1))
                            load_slots(e, q)
                            sp.wait_ge(o_out, SLOT_TILES * (e - 1))
                            load_weights(sp, e, q)
                    with sp.Fori(0, NE // 2 - 1) as i:
                        body(i)
                    if m == 0:
                        for q in range(2):
                            sp.wait_ge(o_out, SLOT_TILES * (NE - 1 + q))
                            load_weights(sp, q, q)

                @block.tensor
                def _(pe):
                    def turn(e, q, n):
                        pe.wait_ge(x_in[q], 16 * (n + 1))
                        for g, (a, b) in enumerate(GROUPS):
                            wait(pe, x_out, NG * e + g - 1)
                            for j in range(a, b):
                                for k in range(KD):
                                    ins = nc.tensor.transpose(pX[:, (NG * q + g) % 2, k, (j - a) * P:(j - a + 1) * P],
                                                              XE[q][:, j, k * P:(k + 1) * P], ident[:])
                            ins.then_inc(x_turned, 1)

                    def up(e, q, n):
                        pe.wait_ge(w_loaded[q], 48 * (n + 1 + (NE // 2) * m))
                        pe.wait_ge(x_out, NG * (e + 1))
                        for f in range(KF):
                            wait(pe, h_out, KF * e + f - 1)
                            for h in range(2):
                                for k in range(KD):
                                    ins = nc.tensor.matmul(pH[:, f % 2, h, 0:HH], W1[q][:, k, f * P:(f + 1) * P],
                                                           XT[q][:, k, h * HH:(h + 1) * HH], start=(k == 0), stop=(k == KD - 1))
                            ins.then_inc(h_made, 1)

                    def down(e, q):
                        for j in range(SLOT_TILES):
                            wait(pe, o_out, SLOT_TILES * e + j - 1)
                            for f in range(KF):
                                if j == 0:
                                    pe.wait_ge(h_out, KF * e + f + 1)
                                ins = nc.tensor.matmul(pO[:, (SLOT_TILES * q + j) % 2, 0:D], hid[:, f, j * P:(j + 1) * P],
                                                       W2[q][:, f, :], start=(f == 0), stop=(f == KF - 1))
                            ins.then_inc(o_made, 1)

                    def body(i, last):
                        for q in range(2):
                            e = 2 * i + q
                            up(e, q, i)
                            if not (last and q):
                                turn(e + 1, 1 - q, i + q)
                            down(e, q)
                    pair_loop(pe, None, lambda: turn(0, 0, 0), body, NE // 2)
                    if prep:
                        pe.wait_ge(o_out, SLOT_TILES * NE)
                        prep.tensor(pe)

                @block.scalar
                def _(act):
                    def body(i, last):
                        for q in range(2):
                            e = 2 * i + q
                            nc.scalar.activation(b1c[q][:], b1T[:, bass.ds(e * KF, KF)], ACT.Copy).then_inc(bias_in, 1)
                            act.wait_ge(bias_in, e + 1)
                            for f in range(KF):
                                act.wait_ge(h_made, KF * e + f + 1)
                                nc.scalar.activation(hid[:, f, :].rearrange("p (h c) -> p h c", h=2), pH[:, f % 2, :, 0:HH],
                                                     ACT.Gelu, bias=b1c[q][:, f:f + 1]).then_inc(h_out, 1)
                    pair_loop(act, None, lambda: None, body, NE // 2)
                    if prep:
                        prep.scalar(act)

                @block.vector
                def _(dve):
                    def evacuate(e, q):
                        for g, (a, b) in enumerate(GROUPS):
                            dve.wait_ge(x_turned, NG * e + g + 1)
                            nc.vector.tensor_copy(XT[q][:, :, a * P:b * P], pX[:, (NG * q + g) % 2, :, 0:(b - a) * P]).then_inc(x_out, 1)

                    def body(i, last):
                        for q in range(2):
                            e = 2 * i + q
                            if not (last and q):
                                evacuate(e + 1, 1 - q)
                            wait(dve, added, 16 * SLOT_TILES * (e - 1))
                            for j in range(SLOT_TILES):
                                n = SLOT_TILES * e + j
                                dve.wait_ge(o_made, n + 1)
                                y = yb[(SLOT_TILES * q + j) % 2]
                                nc.vector.tensor_tensor(out=y[:], in0=pO[:, (SLOT_TILES * q + j) % 2, 0:D], in1=B2[q][:],
                                                        op=ALU.add).then_inc(o_out, 1)
                                dve.wait_ge(o_out, n + 1)
                                ins = nc.vector.tensor_scalar(Y[q][:, j, :], y[:], XE[q][:, j, D:D + 1], None, ALU.mult)
                                ins.then_inc(y_made, 1)
                    pair_loop(dve, None, lambda: evacuate(0, 0), body, NE // 2)
                    if prep:
                        prep.vector(dve)

                @block.gpsimd
                def _(pool):
                    if m == 0:
                        prep.gpsimd(pool)
                        pool.wait_ge(resid_ready[0], 64)

                    def body(i, last):
                        for q in range(2):
                            e = 2 * i + q
                            wait(pool, added, 16 * SLOT_TILES * e)
                            for j in range(SLOT_TILES):
                                hold(pool, y_made, SLOT_TILES * e + j + 1, passed[1])
                                nc.gpsimd.indirect_dma_start(
                                    out=resid[m], out_offset=bass.IndirectOffsetOnAxis(ap=XE[q][:].bitcast(I32)[:, j, D + 1:D + 2], axis=0),
                                    in_=Y[q][:, j, :], in_offset=None, compute_op=ALU.add).then_inc(added, 16)
                    pair_loop(pool, None, lambda: None, body, NE // 2)
                    pool.wait_ge(added, 16 * SLOT_TILES * NE)

        def qkv(VA, Vscope):
            with ExitStack() as scope:
                nb = norm_buffers(scope, "q")
                RING = 4
                LAG = 2
                ta = [sb(scope, f"ta{r}", [P, CHUNK]) for r in range(2)]
                tb = [sb(scope, f"tb{r}", [P, CHUNK]) for r in range(2)]
                tr = [sb(scope, f"tr{r}", [P, CHUNK]) for r in range(RING)]
                rem = [sb(scope, f"rem{r}", [P, CHUNK]) for r in range(RING)]
                spl = [sb(scope, f"spl{r}", [P, PARTS, CHUNK], BF16) for r in range(RING)]
                pQ = ps(scope, "pQ", [P, 2, CHUNK])
                pV = ps(scope, "pV", [P, 2, 2, D])
                steps_sem = sem("dve_stepsq")
                x_loaded = pair("x_loadedq")
                q_made, q_read, summed = sem("q_made"), sem("q_read"), sem("summed")
                hi, rem_made, mid, low = sem("hi"), sem("rem_made"), sem("mid"), sem("low")
                v_made, v_out = sem("v_made"), sem("v_out")
                stored = [sem(f"parts_stored{r}") for r in range(RING)]
                block = scope.enter_context(nc.Block())
                ITEMS = 2 * FT

                @block.sync
                def _(sp):
                    def load(c, q, n):
                        wait(sp, x_loaded[q], 16 * n)
                        sp.dma_start(XR[:, bass.ds(c * CT, CT), :],
                                     resid[0][bass.ds(c * CHUNK, CHUNK), :].rearrange("(t p) d -> p t d", p=P)).then_inc(x_loaded[q], 16)
                    for q in range(2):
                        load(q, q, 0)
                    with sp.Fori(1, NCH // 2) as i:
                        for q in range(2):
                            load(2 * i + q, q, i)

                    with sp.Fori(0, NCH // 2) as i:
                        for k in range(ITEMS):
                            q, f = divmod(k, FT)
                            sp.wait_ge(low, ITEMS * i + k + 1)
                            sp.wait_ge(mid, ITEMS * i + k + 1)
                            b, qc = i // 2, 2 * (i % 2) + q
                            base = (b * FT + f) * PARTS * P
                            dst = qk_parts[bass.ds(base, PARTS * P), bass.ds(qc * CHUNK, CHUNK)].rearrange("(a p) t -> p a t", a=PARTS)
                            sp.dma_start(dst, spl[k % RING][:]).then_inc(stored[k % RING], 16)
                    for r in range(RING):
                        sp.wait_ge(stored[r], 16 * ITEMS // RING * (NCH // 2))

                @block.tensor
                def _(pe):
                    def turn(c, q):
                        norm_turn(pe, nb, c, q)

                    def body(i, last):
                        for q in range(2):
                            c = 2 * i + q
                            pe.wait_ge(nb.xT_ready, c + 1)
                            for f in range(FT):
                                if f == 2 and not (last and q):
                                    turn(c + 1, 1 - q)
                                wait(pe, q_read, FT * c + f - 1)
                                for k in range(KD):
                                    ins = nc.tensor.matmul(pQ[:, f % 2, :], wqk[:, k, f * P:(f + 1) * P], nb.xT[q][:, k, :],
                                                           start=(k == 0), stop=(k == KD - 1))
                                ins.then_inc(q_made, 1)
                            for g in range(2):
                                wait(pe, v_out, 2 * c + g - 1)
                                for j in range(2):
                                    for k in range(KD):
                                        t = 2 * g + j
                                        ins = nc.tensor.matmul(pV[:, g, j, :], nb.xT[q][:, k, t * P:(t + 1) * P], wv[:, k, :],
                                                               start=(k == 0), stop=(k == KD - 1))
                                ins.then_inc(v_made, 1)
                    pair_loop(pe, None, lambda: turn(0, 0), body, NCH // 2)

                @block.scalar
                def _(act):
                    def evacuate(c, q):
                        wait(act, v_made, 2 * (c - 1))
                        norm_evacuate(act, nb, c, q)

                    def high(n, r, uses):
                        act.wait_ge(summed, n + 1)
                        wait(act, stored[r], 16 * uses)
                        nc.scalar.activation(spl[r][:, 0, :], tr[r][:], ACT.Copy).then_inc(hi, 1)

                    def middle(n, r):
                        act.wait_ge(rem_made, n + 1)
                        nc.scalar.activation(spl[r][:, 1, :], rem[r][:], ACT.Copy).then_inc(mid, 1)

                    def body(i, last):
                        for k in range(ITEMS):
                            n = ITEMS * i + k
                            high(n, k % RING, 2 * i + k // RING)
                            if k % FT == 2 and not (last and k >= FT):
                                evacuate(2 * i + k // FT + 1, 1 - k // FT)
                            if not (isinstance(i, int) and i == 0 and k < LAG):
                                middle(n - LAG, (k - LAG) % RING)
                    pair_loop(act, None, lambda: evacuate(0, 0), body, NCH // 2)
                    total = ITEMS * (NCH // 2)
                    for n in range(total - LAG, total):
                        middle(n, n % RING)

                @block.gpsimd
                def _(pool):
                    def add(n, k):
                        pool.wait_ge(q_read, n + 1)
                        wait(pool, rem_made, n - RING + 1)
                        nc.gpsimd.tensor_tensor(out=tr[k % RING][:], in0=ta[k % 2][:], in1=tb[k % 2][:], op=ALU.add).then_inc(summed, 1)

                    def lowest(n, r):
                        pool.wait_ge(mid, n + 1)
                        nc.gpsimd.tensor_tensor(out=spl[r][:, 2, :], in0=rem[r][:], in1=spl[r][:, 1, :], op=ALU.subtract).then_inc(low, 1)

                    def body(i, last):
                        for k in range(ITEMS):
                            n = ITEMS * i + k
                            if k % FT == 1 and not (last and k >= FT):
                                norm_rstd(pool, nb, 2 * i + k // FT + 1, 1 - k // FT)
                            add(n, k)
                            if not (isinstance(i, int) and i == 0 and k < LAG + 1):
                                lowest(n - LAG - 1, (k - LAG - 1) % RING)
                    pair_loop(pool, None, lambda: norm_rstd(pool, nb, 0, 0), body, NCH // 2)
                    total = ITEMS * (NCH // 2)
                    for n in range(total - LAG - 1, total):
                        lowest(n, n % RING)
                    pool.wait_ge(nb.normed, NCH)
                    pool.wait_ge(low, total)

                @block.vector
                def _(dve):
                    steps = Steps(dve, steps_sem)

                    def stats(c, q, n):
                        hold(dve, x_loaded[q], 16 * (n + 1), passed[0])
                        norm_stats(nb, steps, c, q)

                    def rope(n, k, qc):
                        f = k % FT
                        dve.wait_ge(q_made, n + 1)
                        wait(dve, summed, n - 1)
                        cs = cosT[:, bass.ds(qc * CHUNK, CHUNK)]
                        sn = sinT[:, bass.ds(qc * CHUNK, CHUNK)]
                        nc.vector.scalar_tensor_tensor(out=ta[k % 2][:], in0=pQ[:, f % 2, :], scalar=bqk[:, f:f + 1], in1=cs,
                                                       op0=ALU.add, op1=ALU.mult)
                        for a, b in ((0, 64), (64, 0)):
                            ins = nc.vector.scalar_tensor_tensor(out=tb[k % 2][a:a + 64, :], in0=pQ[b:b + 64, f % 2, :],
                                                                 scalar=bqk[b:b + 64, f:f + 1], in1=sn[b:b + 64, :],
                                                                 op0=ALU.add, op1=ALU.mult)
                        ins.then_inc(q_read, 1)

                    def remainder(n, r):
                        dve.wait_ge(hi, n + 1)
                        wait(dve, low, n - RING + 1)
                        nc.vector.tensor_tensor(out=rem[r][:], in0=tr[r][:], in1=spl[r][:, 0, :], op=ALU.subtract).then_inc(rem_made, 1)

                    def head():
                        stats(0, 0, 0)
                        norm_apply(dve, nb, 0, 0)

                    def body(i, last):
                        for k in range(ITEMS):
                            n = ITEMS * i + k
                            q, f = divmod(k, FT)
                            c = 2 * i + q
                            more = not (last and q)
                            if f == 0 and more:
                                stats(c + 1, 1 - q, i + q)
                            rope(n, k, 2 * (i % 2) + q)
                            if f == 1 and more:
                                norm_apply(dve, nb, c + 1, 1 - q)
                            if not (isinstance(i, int) and i == 0 and k < LAG):
                                remainder(n - LAG, (k - LAG) % RING)
                            if f == 3:
                                for g in range(2):
                                    dve.wait_ge(v_made, 2 * c + g + 1)
                                    nc.vector.tensor_tensor(out=VA[:, bass.ds(c * CT + 2 * g, 2), :], in0=pV[:, g],
                                                            in1=bv[:].unsqueeze(1).to_broadcast([P, 2, D]), op=ALU.add).then_inc(v_out, 1)
                    pair_loop(dve, steps, head, body, NCH // 2)
                    total = ITEMS * (NCH // 2)
                    for n in range(total - LAG, total):
                        remainder(n, n % RING)
                    dve.wait_ge(v_out, 2 * NCH)

        def attention(VA):
            with ExitStack() as scope:
                mq = [sb(scope, f"mq{q}", [QROWS, T], BF16) for q in range(2)]
                mk = [sb(scope, f"mk{q}", [QROWS, T], BF16) for q in range(2)]
                eq = [sb(scope, f"eq{q}", [MROWS, T], BF16) for q in range(2)]
                ek = [sb(scope, f"ek{q}", [MROWS, T], BF16) for q in range(2)]
                RING = 4
                pt = [sb(scope, f"pt{r}", [P, T]) for r in range(RING)]
                vh = [sb(scope, f"vh{q}", [P, KT, 32]) for q in range(2)]
                mx4 = [sb(scope, f"mx4{q}", [P, KT, 4]) for q in range(2)]
                mx = sb(scope, "mx", [P, KT])
                ma = sb(scope, "ma", [P, 3, KT])
                mp = sb(scope, "mp", [P, PARTS, 32], BF16)
                mt = sb(scope, "mt", [P, PARTS, 32], BF16)
                oe = [sb(scope, f"oe{q}", [P, CHUNK]) for q in range(2)]
                den = sb(scope, "den0", [P, H * T // P])
                pS = ps(scope, "pS", [P, 2, 2, CHUNK])
                MB = 3
                pM = ps(scope, "pM", [P, MB, CHUNK])
                pO = ps(scope, "pOv", [P, CHUNK])
                inited = sem("inited")
                m_loaded, e_loaded, m_rows = pair("m_loaded"), pair("e_loaded"), pair("m_rows")
                max_stored = sem("max_stored")
                m_scored, m_reduced, m_done = sem("m_scored"), sem("m_reduced"), sem("m_done")
                pool_steps, m_parted, m_turned = sem("pool_stepsa"), sem("m_parted"), sem("m_turned")
                scored, exped, summed, o_out = sem("scored"), sem("expeda"), sem("summeda"), sem("o_outa")
                v_ready, bias_added = sem("v_ready"), sem("bias_added")
                den_loaded, den_inv, den_stored = sem("den_loaded0"), sem("den_inv0"), sem("den_stored0")
                o_stored = pair("o_stored")
                block = scope.enter_context(nc.Block())
                HALFS = 2 * KT
                MS = 4 * KT

                def maxima_of(n, u):
                    return (n + 1, u + LEAD) if u + LEAD < KT else (n + 2, u + LEAD - KT)

                def exists(h):
                    return not isinstance(h, int) or h < NH

                def run(eng, body, steps=None):
                    body(-1, 1)
                    if steps:
                        per0 = steps.n
                    body(0, 0)
                    if steps:
                        per = steps.n - per0
                    body(1, 1)
                    with eng.Fori(1, NH // 2 - 2) as i:
                        for q in range(2):
                            if steps:
                                steps.restart(per0 + (2 * i + q) * per)
                            body(2 * i + q, q)
                    for n in range(NH - 4, NH):
                        if steps:
                            steps.restart(per0 + n * per)
                        body(n, n % 2)

                @block.sync
                def _(sp):
                    def load(n, dq, dk, sm):
                        for s in range(2):
                            at = 0
                            for part, copies in ((0, 3), (1, 2), (2, 1)):
                                rows = slice((s * SPLIT + at) * HALF, (s * SPLIT + at + copies) * HALF)
                                view = qk_parts.rearrange("(b w g a s h d) t -> w s b g h a d t", b=B, w=2, g=FT // 2, a=PARTS, s=2, h=HT)
                                at_head = (bass.ds(n // H, 1), bass.ds((n // HT) % 2, 1), bass.ds(n % HT, 1))
                                qs = view[(0, s) + at_head + (part,)].rearrange("b g h d t -> (b g h d) t")
                                ks = view[(1, s) + at_head + (slice(0, copies),)].rearrange("b g h a d t -> (b g h) a d t")
                                sp.dma_start(dq[rows, :], qs.unsqueeze(0).to_broadcast([copies, HALF, T])).then_inc(sm, 16)
                                sp.dma_start(dk[rows, :], ks[0]).then_inc(sm, 16)
                                at += copies

                    def max_to_rows(h, q):
                        sp.wait_ge(m_turned, h + 1)
                        sp.dma_start(max_rows[q], mt[:].rearrange("p a i -> p (a i)")).then_inc(max_stored, 16)
                        sp.wait_ge(max_stored, 16 * (h + 1))
                        src = max_rows[q].rearrange("(b j) (a i) -> a j b i", b=4, a=PARTS)[:, 0:KT]
                        for a in range(PARTS):
                            sp.dma_start(eq[q][QROWS + a:QROWS + a + 1, :].rearrange("o (j b i) -> o j b i", j=KT, b=4),
                                         src[a:a + 1]).then_inc(m_rows[q], 16)

                    def body(n, q):
                        first = isinstance(n, int) and n < 0
                        if first:
                            load(0, mq[0], mk[0], m_loaded[0])
                            load(1, mq[1], mk[1], m_loaded[1])
                            load(0, eq[0], ek[0], e_loaded[0])
                            for e in range(NE):
                                sp.dma_start(slots[e * CAP:(e + 1) * CAP, D:D + 2].rearrange("(p j) d -> p j d", p=P),
                                             meta[:]).then_inc(slots_ready, 16)
                        else:
                            if exists(n + 1):
                                wait(sp, scored, HALFS * n)
                                load(n + 1, eq[1 - q], ek[1 - q], e_loaded[1 - q])
                            if not (isinstance(n, int) and n == 0):
                                store(n - 1, 1 - q)
                        if isinstance(n, int) and n == NH - 4:
                            for r in range(2):
                                sp.wait_ge(o_stored[r], 16 * H // 2)
                            sp.dma_start(den[:], denominators(0)).then_inc(den_loaded, 16)
                        if isinstance(n, int) and n == NH - 2:
                            sp.wait_ge(den_inv, 1)
                            sp.dma_start(reciprocals(0), den[:]).then_inc(den_stored, 16)
                        if exists(n + 1):
                            max_to_rows(n + 1, 1 - q)
                            if exists(n + 3):
                                sp.wait_ge(m_reduced, MS * (n + 2))
                                load(n + 3, mq[1 - q], mk[1 - q], m_loaded[1 - q])

                    def store(h, q):
                        sp.wait_ge(o_out, h + 1)
                        sp.dma_start(attn[bass.ds(h * 32, 32), :].rearrange("r (j t) -> j r t", j=4), oe[q][:]).then_inc(o_stored[q], 16)
                    run(sp, body)
                    store(NH - 1, 1)
                    for q in range(2):
                        sp.wait_ge(o_stored[q], 16 * NH // 2)
                    sp.wait_ge(den_stored, 16)

                @block.tensor
                def _(pe):
                    def maxima(h, t, q, j0, j1):
                        if t == 0 and j0 == 0:
                            pe.wait_ge(m_loaded[q], 192 * ((h - q) // 2 + 1 if isinstance(h, int) else h // 2 + 1))
                        for j in range(j0, j1):
                            s = 4 * t + j
                            wait(pe, m_reduced, MS * h + (s - MB + 1 if s else 0))
                            nc.tensor.matmul(pM[:, s % MB, :], mq[q][:, t * P:(t + 1) * P], mk[q][:, j * CHUNK:(j + 1) * CHUNK],
                                             start=True, stop=True).then_inc(m_scored, 1)

                    def scores(n, u, g, q):
                        wait(pe, exped, HALFS * n + 2 * u + g - 1)
                        for j in range(2):
                            ins = nc.tensor.matmul(pS[:, g, j, :], ek[q][:, u * P:(u + 1) * P],
                                                   eq[q][:, (2 * g + j) * CHUNK:(2 * g + j + 1) * CHUNK], start=True, stop=True)
                        ins.then_inc(scored, 1)

                    def values(n, u, q):
                        pe.wait_ge(exped, HALFS * n + 2 * u + 2)
                        if u == 0:
                            pe.wait_ge(v_ready, n + 1)
                            wait(pe, o_out, n)
                        for j in range(4):
                            ins = nc.tensor.matmul(pO[32 * j:32 * (j + 1), :], vh[q][:, u, :], pt[u % RING][:, j * CHUNK:(j + 1) * CHUNK],
                                                   start=(u == 0), stop=(u == KT - 1))
                        ins.then_inc(summed, 1)

                    pe.wait_ge(inited, 1)
                    for t in range(LEAD):
                        maxima(0, t, 0, 0, 4)

                    def body(n, q):
                        real = not (isinstance(n, int) and n < 0)
                        for u in range(KT):
                            h, t = maxima_of(n, u)
                            mqq = 1 - q if t >= LEAD else q
                            if real:
                                if u == 0:
                                    half = n // 2
                                    pe.wait_ge(e_loaded[q], 192 * (half + 1))
                                    pe.wait_ge(m_rows[q], 48 * (half + 1))
                                scores(n, u, 0, q)
                            if exists(h):
                                maxima(h, t, mqq, 0, 2)
                            if real:
                                scores(n, u, 1, q)
                            if exists(h):
                                maxima(h, t, mqq, 2, 3)
                            if real and u:
                                values(n, u - 1, q)
                            elif real and not (isinstance(n, int) and n == 0):
                                values(n - 1, KT - 1, 1 - q)
                            if exists(h):
                                maxima(h, t, mqq, 3, 4)
                    run(pe, body)
                    values(NH - 1, KT - 1, 1)

                @block.scalar
                def _(act):
                    def evacuate(h, q, uses):
                        act.wait_ge(summed, KT * (h + 1))
                        wait(act, o_stored[q], 16 * uses)
                        nc.scalar.activation(oe[q][:], pO[:], ACT.Copy).then_inc(o_out, 1)

                    def body(n, q):
                        if isinstance(n, int) and n < 0:
                            return
                        for u in range(KT):
                            wait(act, summed, KT * n + u - RING + 1)
                            for g in range(2):
                                act.wait_ge(scored, HALFS * n + 2 * u + g + 1)
                                nc.scalar.activation(pt[u % RING][:, g * 1024:(g + 1) * 1024], pS[:, g], ACT.Exp,
                                                     scale=DH ** -0.5).then_inc(exped, 1)
                            if u == 0 and not (isinstance(n, int) and n == 0):
                                evacuate(n - 1, 1 - q, (n - 1) // 2)
                    run(act, body)
                    evacuate(NH - 1, 1, NH // 2 - 1)

                @block.vector
                def _(dve):
                    def reduce(h, t, q):
                        for j in range(4):
                            s = 4 * t + j
                            dve.wait_ge(m_scored, MS * h + s + 1)
                            nc.vector.tensor_reduce(out=mx4[q][:, t, j:j + 1], in_=pM[:, s % MB, :], axis=AX.X,
                                                    op=ALU.max).then_inc(m_reduced, 1)

                    for q in range(2):
                        nc.vector.memset(vh[q][:], 1.0)
                        nc.vector.memset(ek[q][QROWS:MROWS, :], 1.0)
                    nc.vector.memset(mp[:], 0.0).then_inc(inited, 1)
                    for t in range(LEAD):
                        reduce(0, t, 0)

                    def body(n, q):
                        for u in range(KT):
                            h, t = maxima_of(n, u)
                            if exists(h):
                                reduce(h, t, 1 - q if t >= LEAD else q)
                                if t == KT - 1:
                                    dve.wait_ge(m_reduced, MS * (h + 1))
                                    wait(dve, m_parted, h)
                                    nc.vector.tensor_reduce(out=mx[:], in_=mx4[1 - q][:], axis=AX.X, op=ALU.max).then_inc(m_done, 1)
                            if u == KT - 3 and exists(n + 1):
                                dve.wait_ge(m_parted, n + 2)
                                wait(dve, max_stored, 16 * (n + 1))
                                nc.vector.transpose(mt[:], mp[:]).then_inc(m_turned, 1)
                        if isinstance(n, int) and n == NH - 3:
                            dve.wait_ge(den_loaded, 16)
                            nc.vector.reciprocal(den[:], den[:]).then_inc(den_inv, 1)
                    run(dve, body)

                @block.gpsimd
                def _(pool):
                    steps = Steps(pool, pool_steps)

                    def split_maxima(h):
                        pool.wait_ge(m_done, h + 1)
                        hold(pool, m_turned, h, passed[1])
                        steps.add(nc.gpsimd.tensor_scalar(ma[:, 0], mx[:], -1.0, None, ALU.mult))
                        for a in range(2):
                            steps.settle_alone(passed[1])
                            steps.add(nc.gpsimd.tensor_copy(mp[:, a, 0:KT], ma[:, a]))
                            steps.settle()
                            steps.add(nc.gpsimd.tensor_tensor(out=ma[:, a + 1], in0=ma[:, a], in1=mp[:, a, 0:KT], op=ALU.subtract))
                        steps.settle_alone(passed[1])
                        nc.gpsimd.tensor_copy(mp[:, 2, 0:KT], ma[:, 2]).then_inc(m_parted, 1)

                    pool.wait_ge(inited, 1)

                    def body(n, q):
                        if exists(n + 1):
                            hold(pool, summed, KT * n, passed[1])
                            b = (n + 1) // H
                            h0 = ((n + 1) % H) * DH
                            src = VA[:, bass.ds(b * KT, KT), bass.ds(h0, DH)]
                            nc.gpsimd.tensor_copy(vh[1 - q][:, :, 0:DH], src).then_inc(v_ready, 1)
                            split_maxima(n + 1)
                        if not (isinstance(n, int) and n < 0):
                            xs = XR[:, bass.ds(n, 1), :].rearrange("p a d -> p (a d)")
                            nc.gpsimd.tensor_tensor(out=xs, in0=xs, in1=bp[:], op=ALU.add).then_inc(bias_added, 1)
                    run(pool, body, steps)
                    pool.wait_ge(bias_added, TILES)

        with ExitStack() as scope:
            route(0, False, setup(scope))
        experts(0)
        with ExitStack() as scope:
            VA = sb(scope, "VA", [P, TILES, D])
            qkv(VA, scope)
            attention(VA)
        route(1, True)
        experts(1)
        with ExitStack() as scope:
            out_stored = sem("out_stored")
            block = scope.enter_context(nc.Block())

            @block.sync
            def _(sp):
                sp.dma_start(out, resid[1][0:N, :]).then_inc(out_stored, 16)
                sp.wait_ge(out_stored, 16)


_INS = ["L0_attn_x", "L0_attn_sin", "L0_attn_cos", "L0_attn_w_qkv", "L0_attn_b_qkv", "L0_attn_w_proj", "L0_attn_b_proj",
        "L0_ffn_w_router", "L0_ffn_b_router", "L0_ffn_w1", "L0_ffn_b1", "L0_ffn_w2", "L0_ffn_b2"]


def kernel(**inputs):
    import numpy as np
    import concourse.bacc as bacc
    from concourse.bass_utils import run_bass_kernel_spmd

    shapes = {"L0_attn_x": (N, D), "L0_attn_b_qkv": (1, 3 * D), "L0_attn_b_proj": (1, D), "L0_ffn_b_router": (1, NE),
              "L0_ffn_w1": (NE * D, FF), "L0_ffn_w2": (NE * FF, D)}
    nc = bacc.Bacc("TRN2", target_bir_lowering=False, num_devices=1)
    arrays, args = {}, []
    for name in _INS:
        a = np.ascontiguousarray(inputs[name])
        a = a.reshape(shapes.get(name, a.shape))
        arrays[name] = a
        args.append(nc.dram_tensor(name, a.shape, mybir.dt.from_np(a.dtype), kind="ExternalInput").ap())
    out = nc.dram_tensor("out", (N, D), F32, kind="ExternalOutput").ap()
    build(nc, *args, out)
    r = run_bass_kernel_spmd(nc, [arrays], core_ids=[0])
    return r.results[0]["out"].reshape(B, T, D)
```

```python
from contextlib import ExitStack

import concourse.bass as bass
from concourse import mybir

F32, F32R, BF16, I32 = mybir.dt.float32, mybir.dt.float32r, mybir.dt.bfloat16, mybir.dt.int32
ALU = mybir.AluOpType
ACT = mybir.ActivationFunctionType
AX = mybir.AxisListType

P = 128
B, T, D = 2, 2048, 256
N = B * T
KD = D // P
H, DH = 16, 16
HALF = DH // 2
N_ROPE = 1369
PREFIX = T - N_ROPE
NE, FF = 8, 1024
KF = FF // P
CAP = int(1.25 * N / NE)
SLOT_TILES = CAP // P
TILES = N // P
CHUNK = 512
CT = CHUNK // P
NCH = N // CHUNK
BCH = T // CHUNK
ROW = D + 2
SLOTS = NE * CAP
EPS = 1e-5
NH = B * H
KT = T // P
PARTS = 3
SPLIT = 6
QROWS = SPLIT * DH
MROWS = QROWS + PARTS
LEAD = 5
HEADS = 4
LOADS = 12 * 16
EARLY = 4
FT = 4
HT = P // DH
HH = CAP // 2


def wait(eng, sem, value):
    if not isinstance(value, int) or value > 0:
        eng.wait_ge(sem, value)


def hold(eng, sem, value, passed):
    if not isinstance(value, int) or value > 0:
        eng.wait_ge(sem, value)
        eng.sem_inc(passed, 1)


class Norm:
    pass


class Steps:

    def __init__(self, eng, sem):
        self.eng, self.sem, self.base, self.n = eng, sem, 0, 0

    def add(self, ins):
        ins.then_inc(self.sem, 1)
        self.n += 1

    def settle(self):
        self.eng.wait_ge(self.sem, self.base + self.n)

    def settle_alone(self, passed):
        hold(self.eng, self.sem, self.base + self.n, passed)

    def restart(self, base):
        self.base, self.n = base, 0


def pair_loop(eng, steps, head, body, pairs):
    head()
    at = steps.n if steps else 0
    body(0, False)
    per = steps.n - at if steps else 0
    with eng.Fori(1, pairs - 1) as i:
        if steps:
            steps.restart(i * per + at)
        body(i, False)
    if steps:
        steps.restart((pairs - 1) * per + at)
    body(pairs - 1, True)


def build(nc, x, sin, cos, w_qkv, b_qkv, w_proj, b_proj, w_router, b_router, w1, b1, w2, b2, out):
    ctx = ExitStack()

    def sem(name):
        return ctx.enter_context(nc.semaphore(name))

    def pair(name):
        return [sem(f"{name}{q}") for q in range(2)]

    def sb(scope, name, shape, dt=F32):
        return scope.enter_context(nc.sbuf_tensor(name, shape, dt))

    def ps(scope, name, shape, dt=F32):
        return scope.enter_context(nc.psum_tensor(name, shape, dt))

    slots = nc.dram_tensor("slots", [SLOTS + 2 * N, ROW], F32).ap()
    resid = [nc.dram_tensor("resid0", [N + CAP, D], F32).ap(), out]
    qk_parts = nc.dram_tensor("qk_parts", [B * FT * PARTS * P, T], BF16).ap()
    max_rows = nc.dram_tensor("max_rows", [2, P, PARTS * 32], BF16).ap()
    attn = nc.dram_tensor("attn", [NH * 32, T], F32).ap()
    rden = nc.dram_tensor("rden", [NH, T], F32).ap()

    with ctx:
        W1 = [sb(ctx, f"W1_{q}", [P, KD, FF]) for q in range(2)]
        W2 = [sb(ctx, f"W2_{q}", [P, KF, D]) for q in range(2)]
        B2 = [sb(ctx, f"B2_{q}", [P, D]) for q in range(2)]
        b1T = sb(ctx, "b1T", [P, NE * KF])
        ident = sb(ctx, "ident", [P, P])
        ones = sb(ctx, "ones", [P, P], BF16)
        before = sb(ctx, "before", [P, P], BF16)
        em8 = sb(ctx, "em8", [P, CT, NE])
        tok_id = sb(ctx, "tok_id", [P, TILES], I32)
        trash = sb(ctx, "trash", [P, 2, TILES])
        mhalf = sb(ctx, "mhalf", [P, CT])
        wr = sb(ctx, "wr", [P, KD, NE])
        br = sb(ctx, "br", [P, NE])
        wqk = sb(ctx, "wqk", [P, KD, FT * P])
        wv = sb(ctx, "wv", [P, KD, D])
        wp = sb(ctx, "wp", [P, KD, D])
        bqk = sb(ctx, "bqk", [P, FT])
        bv = sb(ctx, "bv", [P, D])
        bp = sb(ctx, "bp", [P, D])
        meta = sb(ctx, "meta", [P, SLOT_TILES, 2])
        cosT = sb(ctx, "cosT", [P, T])
        sinT = sb(ctx, "sinT", [P, T])

        w_loaded = pair("w_loaded")
        slots_ready = sem("slots_ready")
        spare_ready = sem("spare_ready")
        passed = [sem(f"passed_{e}") for e in ("dve", "pool", "sp")]
        resid_ready = [sem(f"resid_ready{m}") for m in range(2)]

        def load_weights(sp, e, q):
            sp.dma_start(W1[q][:], w1[bass.ds(e * D, D), :].rearrange("(k p) f -> p k f", p=P)).then_inc(w_loaded[q], 16)
            sp.dma_start(W2[q][:], w2[bass.ds(e * FF, FF), :].rearrange("(k p) f -> p k f", p=P)).then_inc(w_loaded[q], 16)
            sp.dma_start(B2[q][:], b2[bass.ds(e, 1), :].to_broadcast([P, D])).then_inc(w_loaded[q], 16)

        consts = sem("consts")
        CONSTS = 3

        class Setup:
            pass

        def setup(scope):
            b1_nat = sb(scope, "b1_nat", [NE * KF, P])
            empty = sb(scope, "empty", [P, SLOT_TILES, ROW])
            itmp = sb(scope, "itmp", [P, CT * NE], I32)
            itrash = sb(scope, "itrash", [P, 2 * TILES], I32)
            empty_made, setup_steps = sem("empty_made"), sem("setup_steps")
            first_loaded, b1_turned, b1_out = sem("first_loaded"), sem("b1_turned"), sem("b1_out")
            start = Setup()
            start.first_loaded = first_loaded

            def sync(sp):
                sp.dma_start(wr[:], w_router.rearrange("(k p) f -> p k f", p=P)).then_inc(first_loaded, 16)
                sp.dma_start(br[:], b_router.to_broadcast([P, NE])).then_inc(first_loaded, 16)
                sp.dma_start(b1_nat[:], b1.rearrange("e (k p) -> (e k) p", p=P)).then_inc(first_loaded, 16)

            def gpsimd(pool):
                steps = Steps(pool, setup_steps)
                steps.add(nc.gpsimd.memset(empty[:], 0.0))
                nc.gpsimd.memset(mhalf[:], -0.5)
                steps.settle()
                nc.gpsimd.iota(empty[:].bitcast(I32)[:, :, D + 1], pattern=[[1, SLOT_TILES]], base=N,
                               channel_multiplier=SLOT_TILES).then_inc(empty_made, 1)
                steps.add(nc.gpsimd.memset(ident[:], 0.0))
                steps.add(nc.gpsimd.memset(before[:], 0.0))
                nc.gpsimd.memset(ones[:], 1.0)
                steps.settle()
                nc.gpsimd.affine_select(out=ident[:], in_=ident[:], compare_op=ALU.not_equal, fill=1.0, base=0,
                                        pattern=[[-1, P]], channel_multiplier=1)
                nc.gpsimd.affine_select(out=before[:], in_=before[:], compare_op=ALU.is_ge, fill=1.0, base=0,
                                        pattern=[[-1, P]], channel_multiplier=1).then_inc(consts, 1)
                nc.gpsimd.iota(tok_id[:], pattern=[[P, TILES]], base=0, channel_multiplier=1)
                steps.add(nc.gpsimd.iota(itmp[:], pattern=[[0, CT], [1, NE]], base=-NE, channel_multiplier=0))
                steps.add(nc.gpsimd.iota(itrash[:], pattern=[[N, 2], [P, TILES]], base=SLOTS, channel_multiplier=1))
                steps.settle()
                nc.gpsimd.tensor_copy(em8[:].rearrange("p a b -> p (a b)"), itmp[:])
                nc.gpsimd.tensor_copy(trash[:].rearrange("p a b -> p (a b)"), itrash[:]).then_inc(consts, 1)
                nc.gpsimd.tensor_copy(meta[:].bitcast(I32)[:, :, 0], empty[:].bitcast(I32)[:, :, D])
                pool.wait_ge(empty_made, 1)
                nc.gpsimd.tensor_copy(meta[:].bitcast(I32)[:, :, 1], empty[:].bitcast(I32)[:, :, D + 1]).then_inc(consts, 1)

            def tensor(pe):
                pe.wait_ge(consts, 1)
                pe.wait_ge(first_loaded, 48)
                nc.tensor.transpose(start.bank, b1_nat[:], ident[0:NE * KF, 0:NE * KF]).then_inc(b1_turned, 1)
                pe.wait_ge(b1_out, 1)

            def scalar(act):
                act.wait_ge(empty_made, 1)
                for e in range(NE):
                    act.dma_start(slots[e * CAP:(e + 1) * CAP, :].rearrange("(p j) d -> p j d", p=P), empty[:]).then_inc(slots_ready, 16)
                for m in range(2):
                    act.dma_start(resid[m][N:N + CAP, :].rearrange("(p j) d -> p j d", p=P), empty[:, :, 0:D]).then_inc(spare_ready, 16)
                act.wait_ge(b1_turned, 1)
                nc.scalar.activation(b1T[:], start.bank, ACT.Copy).then_inc(b1_out, 1)

            start.sync, start.gpsimd, start.tensor, start.scalar = sync, gpsimd, tensor, scalar
            return start

        class Prepare:
            pass

        def prepare(scope):
            wq_nat = sb(scope, "wq_nat", [P, KD, 3 * D])
            tab = sb(scope, "tab", [P, 2, KT, DH])
            wide = sb(scope, "wide", [P, 2, 4, P])
            small_loaded, tab_set, tab_loaded = sem("small_loaded"), sem("tab_set"), sem("tab_loaded")
            wide_made, wide_turned, tab_written = sem("wide_made"), sem("wide_turned"), sem("tab_written")
            weights_made = sem("weights_made")
            SMALL = 4 + 2 * FT
            prep = Prepare()

            def sync(sp):
                sp.dma_start(wq_nat[:], w_qkv.rearrange("(k p) f -> p k f", p=P)).then_inc(small_loaded, 16)
                sp.dma_start(wp[:], w_proj.rearrange("(k p) f -> p k f", p=P)).then_inc(small_loaded, 16)
                sp.dma_start(bv[:], b_qkv[:, 2 * D:3 * D].to_broadcast([P, D])).then_inc(small_loaded, 16)
                sp.dma_start(bp[:], b_proj.to_broadcast([P, D])).then_inc(small_loaded, 16)
                for f in range(FT):
                    for s in range(2):
                        src = b_qkv[0, f * P:(f + 1) * P].rearrange("(h s d) -> s h d", h=HT, s=2)[s]
                        sp.dma_start(bqk[s * 64:(s + 1) * 64, f:f + 1], src).then_inc(small_loaded, 16)
                sp.wait_ge(tab_set, 1)
                t0, p0 = PREFIX // P, PREFIX % P
                for n, src in enumerate((cos, sin)):
                    sp.dma_start(tab[p0:P, n, t0, :], src[0:P - p0, :]).then_inc(tab_loaded, 16)
                    sp.dma_start(tab[:, n, t0 + 1:KT, :],
                                 src[P - p0:N_ROPE, :].rearrange("(t p) d -> p t d", p=P)).then_inc(tab_loaded, 16)

            def gpsimd(pool):
                nc.gpsimd.memset(tab[:, 0], 1.0)
                nc.gpsimd.memset(tab[:, 1], 0.0).then_inc(tab_set, 1)
                pool.wait_ge(small_loaded, 16 * SMALL)
                for k in range(KD):
                    for f in range(FT):
                        dst = wqk[:, k, f * P:(f + 1) * P].rearrange("p (s h d) -> p s h d", s=2, h=HT)
                        src = wq_nat[:, k, f * P:(f + 1) * P].rearrange("p (h s d) -> p s h d", h=HT, s=2)
                        nc.gpsimd.tensor_copy(dst, src)
                nc.gpsimd.tensor_copy(wv[:], wq_nat[:, :, 2 * D:3 * D]).then_inc(weights_made, 1)
                pool.wait_ge(weights_made, 1)

            def vector(dve):
                dve.wait_ge(tab_loaded, 64)
                for g in range(8):
                    n, t0 = g // 4, 4 * (g % 4)
                    if g >= 2:
                        dve.wait_ge(wide_turned, g - 1)
                    for s in range(2):
                        src = s if n == 0 else 1 - s
                        src = tab[:, n, t0:t0 + 4, src * HALF:(src + 1) * HALF].unsqueeze(2).to_broadcast([P, 4, HT, HALF])
                        dst = wide[:, g % 2, :, s * 64:(s + 1) * 64].rearrange("p t (h d) -> p t h d", h=HT)
                        last = nc.vector.tensor_scalar(dst, src, -1.0 if n == 1 and s == 1 else 1.0, None, ALU.mult)
                    last.then_inc(wide_made, 1)

            def tensor(pe):
                for g in range(8):
                    pe.wait_ge(wide_made, g + 1)
                    if g >= 2:
                        pe.wait_ge(tab_written, g - 1)
                    for j in range(4):
                        last = nc.tensor.transpose(prep.banks[g % 2][:, j * P:(j + 1) * P], wide[:, g % 2, j, :], ident[:])
                    last.then_inc(wide_turned, 1)

            def scalar(act):
                for g in range(8):
                    act.wait_ge(wide_turned, g + 1)
                    dst = (cosT, sinT)[g // 4][:, (g % 4) * CHUNK:(g % 4 + 1) * CHUNK]
                    nc.scalar.activation(dst, prep.banks[g % 2], ACT.Copy).then_inc(tab_written, 1)
                act.wait_ge(tab_written, 8)

            prep.sync, prep.gpsimd, prep.vector, prep.tensor, prep.scalar = sync, gpsimd, vector, tensor, scalar
            return prep

        def denominators(b):
            rows = attn[b * H * 32:(b + 1) * H * 32, :].rearrange("(h r) (a t) -> r h a t", r=32, a=P // H)
            return rows[DH]

        def reciprocals(b):
            return rden[b * H:(b + 1) * H, :].rearrange("h (a t) -> (h a) t", a=P // H)

        def norm_buffers(scope, tag, XR):
            nb = Norm()
            nb.x = XR
            nb.st = [sb(scope, f"st{tag}{q}", [P, CT, 6]) for q in range(2)]
            nb.mv = [sb(scope, f"mv{tag}{q}", [P, CT, 2]) for q in range(2)]
            nb.ve = [sb(scope, f"ve{tag}{q}", [P, CT]) for q in range(2)]
            nb.rs = [sb(scope, f"rs{tag}{q}", [P, CT]) for q in range(2)]
            nb.xn = [sb(scope, f"xn{tag}{q}", [P, CT, D]) for q in range(2)]
            nb.xT = [sb(scope, f"xT{tag}{q}", [P, KD, CHUNK]) for q in range(2)]
            nb.pT = ps(scope, f"pT{tag}", [P, KD, CHUNK])
            nb.stats, nb.ve_made, nb.rstd = sem(f"stats{tag}"), sem(f"ve_made{tag}"), sem(f"rstd{tag}")
            nb.normed, nb.turned, nb.xT_ready = sem(f"normed{tag}"), sem(f"turned{tag}"), sem(f"xT_ready{tag}")
            return nb

        def norm_stats(nb, steps, c, q):
            for j in range(CT):
                ins = nc.vector.bn_stats(nb.st[q][:, j, :], nb.x[:, bass.ds(c * CT + j, 1), :].rearrange("p a d -> p (a d)"))
            steps.add(ins)
            steps.settle_alone(passed[0])
            for j in range(CT):
                ins = nc.vector.bn_aggr(nb.mv[q][:, j, :], nb.st[q][:, j, :])
            ins.then_inc(nb.stats, 1)

        def norm_rstd(pool, nb, c, q):
            hold(pool, nb.stats, c + 1, passed[1])
            nc.gpsimd.tensor_scalar(nb.ve[q][:], nb.mv[q][:, :, 1], EPS, None, ALU.add).then_inc(nb.ve_made, 1)
            pool.wait_ge(nb.ve_made, c + 1)
            nc.gpsimd.tensor_tensor(out=nb.rs[q][:], in0=nb.ve[q][:], in1=mhalf[:], op=ALU.pow).then_inc(nb.rstd, 1)

        def norm_apply(dve, nb, c, q):
            wait(dve, nb.turned, c - 1)
            dve.wait_ge(nb.stats, c + 1)
            dve.wait_ge(nb.rstd, c + 1)
            for j in range(CT):
                ins = nc.vector.tensor_scalar(nb.xn[q][:, j, :], nb.x[:, bass.ds(c * CT + j, 1), :].rearrange("p a d -> p (a d)"),
                                              nb.mv[q][:, j, 0:1], nb.rs[q][:, j:j + 1], ALU.subtract, ALU.mult)
            ins.then_inc(nb.normed, 1)

        def norm_turn(pe, nb, c, q):
            pe.wait_ge(nb.normed, c + 1)
            wait(pe, nb.xT_ready, c)
            for k in range(KD):
                for j in range(CT):
                    ins = nc.tensor.transpose(nb.pT[:, k, j * P:(j + 1) * P], nb.xn[q][:, j, k * P:(k + 1) * P], ident[:])
            ins.then_inc(nb.turned, 1)

        def norm_evacuate(act, nb, c, q):
            act.wait_ge(nb.turned, c + 1)
            nc.scalar.activation(nb.xT[q][:], nb.pT[:], ACT.Copy).then_inc(nb.xT_ready, 1)

        def load_sums(sp, i, q, num, rcp, o_loaded):
            b, qc = i // 2, 2 * (i % 2) + q
            for k in range(KD):
                h0 = b * H + k * HT
                src = attn[bass.ds(h0 * 32, HT * 32), bass.ds(qc * CHUNK, CHUNK)]
                sp.dma_start(num[q][:, k], src.rearrange("(h r) t -> h r t", r=32)[:, 0:DH, :]).then_inc(o_loaded[q], 16)
                src = rden[bass.ds(h0, HT), bass.ds(qc * CHUNK, CHUNK)]
                sp.dma_start(rcp[q][:, k], src.unsqueeze(1).to_broadcast([HT, DH, CHUNK])).then_inc(o_loaded[q], 16)

        def bank_pair(scope, name):
            banks = ps(scope, name, [P, 2, CHUNK])
            return [banks[:, q, 0:CT * NE].rearrange("p (j e) -> p j e", j=CT) for q in range(2)]

        def route(m, project, XR, start=None, num=None, rcp=None, o_loaded=None):
            tag = f"r{m}"
            with ExitStack() as scope:
                nb = norm_buffers(scope, tag, XR)
                rows = [sb(scope, f"rows{tag}{q}", [P, 2, CT, ROW]) for q in range(2)]
                lg = [sb(scope, f"lg{tag}{q}", [P, CT, NE]) for q in range(2)]
                l2 = [sb(scope, f"l2{tag}{q}", [P, CT, NE]) for q in range(2)]
                eq = [sb(scope, f"eq{tag}{q}", [P, 2, CT, NE]) for q in range(2)]
                oh = [sb(scope, f"oh{tag}{q}", [P, 2, CT, NE]) for q in range(2)]
                top = [sb(scope, f"top{tag}{q}", [P, 2, CT]) for q in range(2)]
                em = [sb(scope, f"em{tag}{q}", [P, 2, CT]) for q in range(2)]
                mask = [sb(scope, f"mask{tag}{q}", [P, CT, NE], BF16) for q in range(2)]
                less = [sb(scope, f"less{tag}{q}", [P, CT, NE + 1]) for q in range(2)]
                ex = [sb(scope, f"ex{tag}{q}", [P, CT, NE + 1]) for q in range(2)]
                seen = [sb(scope, f"seen{tag}{q}", [P, NE]) for q in range(2)]
                seen_b = [sb(scope, f"seen_b{tag}{q}", [P, NE], BF16) for q in range(2)]
                here = sb(scope, f"here{tag}", [P, NE])
                hit = sb(scope, f"hit{tag}", [P, 2, CT, NE])
                pos = sb(scope, f"pos{tag}", [P, 2, CT])
                keep = sb(scope, f"keep{tag}", [P, 2, CT])
                slot = sb(scope, f"slot{tag}", [P, 2, CT])
                off = sb(scope, f"off{tag}", [P, 2, CT])
                gate = sb(scope, f"gate{tag}", [P, 2, CT])
                gsum = sb(scope, f"gsum{tag}", [P, 2, CT])
                dest = [sb(scope, f"dest{tag}{q}", [P, 2, CT], I32) for q in range(2)]
                pL = bank_pair(scope, f"pL{tag}")
                pP = bank_pair(scope, f"pP{tag}")
                steps_sem = sem(f"dve_steps{tag}")
                x_loaded = pair(f"x_loaded{tag}")
                row_copied, logits = sem(f"row_copied{tag}"), sem(f"logits{tag}")
                masked, prefixed = sem(f"masked{tag}"), sem(f"prefixed{tag}")
                less_made, exped = sem(f"less_made{tag}"), sem(f"exped{tag}")
                routed, scattered = sem(f"routed{tag}"), pair(f"scattered{tag}")
                x_ready, x_stored = sem(f"x_ready{tag}"), sem(f"x_stored{tag}")
                if project:
                    onT = [sb(scope, f"onT{q}", [P, KD, CHUNK]) for q in range(2)]
                    den = sb(scope, "den1", [P, H * T // P])
                    pY = ps(scope, "pY", [P, 2, 2, D])
                    den_loaded, den_inv, rden_stored = sem("den_loaded"), sem("den_inv"), sem("rden_stored")
                    o_made, projected = sem("o_made"), sem("projected")
                if not project:
                    start.bank = nb.pT[:, 0, 0:NE * KF]
                block = scope.enter_context(nc.Block())

                @block.sync
                def _(sp):
                    if not project:

                        def load(c, q, n):
                            wait(sp, x_loaded[q], 16 * n)
                            sp.dma_start(XR[:, bass.ds(c * CT, CT), :],
                                         x[bass.ds(c * CHUNK, CHUNK), :].rearrange("(t p) d -> p t d", p=P)).then_inc(x_loaded[q], 16)
                        load(0, 0, 0)
                        load(1, 1, 0)
                        start.sync(sp)
                        with sp.Fori(1, NCH // 2) as i:
                            for q in range(2):
                                load(2 * i + q, q, i)
                        quarter = N // 4
                        for g in range(4):
                            sp.wait_ge(routed, 3 + g)
                            if g % 2 == 0:
                                load_weights(sp, g // 2, g // 2)
                            sp.dma_start(resid[m][g * quarter:(g + 1) * quarter, :],
                                         x[g * quarter:(g + 1) * quarter, :]).then_inc(resid_ready[m], 16)
                        return

                    def load(i, q):
                        hold(sp, o_made, 2 * i + q - 1, passed[2])
                        load_sums(sp, i, q, num, rcp, o_loaded)

                    def store(c):
                        sp.wait_ge(x_ready, c + 1)
                        sp.dma_start(resid[m][bass.ds(c * CHUNK, CHUNK), :].rearrange("(t p) d -> p t d", p=P),
                                     XR[:, bass.ds(c * CT, CT), :]).then_inc(x_stored, 16)
                        hold(sp, x_stored, 16 * (c + 1), passed[2])
                    sp.dma_start(den[:], denominators(1)).then_inc(den_loaded, 16)
                    for q in range(2):
                        load(1, q)
                        store(q)
                    sp.wait_ge(den_inv, 1)
                    sp.dma_start(reciprocals(1), den[:]).then_inc(rden_stored, 16)
                    sp.wait_ge(rden_stored, 16)
                    with sp.Fori(2, NCH // 2) as i:
                        for q in range(2):
                            load(i, q)
                            store(2 * i + q - 2)
                    for c in (NCH - 2, NCH - 1):
                        store(c)

                @block.tensor
                def _(pe):
                    def attend(c, q):
                        pe.wait_ge(o_made, c + 1)
                        wait(pe, x_ready, c)
                        for j in range(CT):
                            for k in range(KD):
                                ins = nc.tensor.matmul(pY[:, j // 2, j % 2, :], onT[q][:, k, j * P:(j + 1) * P], wp[:, k, :],
                                                       start=(k == 0), stop=(k == KD - 1))
                            if j % 2:
                                ins.then_inc(projected, 1)

                    def score(c, q):
                        pe.wait_ge(nb.xT_ready, c + 1)
                        wait(pe, masked, c - 1)
                        for j in range(CT):
                            for k in range(KD):
                                ins = nc.tensor.matmul(pL[q][:, j, :], nb.xT[q][:, k, j * P:(j + 1) * P], wr[:, k, :],
                                                       start=(k == 0), stop=(k == KD - 1))
                        ins.then_inc(logits, 1)

                    def prefix(c, q):
                        pe.wait_ge(masked, c + 1)
                        nc.tensor.matmul(pP[q], before[:], mask[q][:], start=True, stop=False)
                        for j in range(CT - 1):
                            nc.tensor.matmul(pP[q][:, j + 1:CT, :], ones[:],
                                             mask[q][:, j:j + 1, :].to_broadcast([P, CT - 1 - j, NE]), start=False, stop=False)
                        nc.tensor.matmul(pP[q], ones[:], seen_b[q][:].unsqueeze(1).to_broadcast([P, CT, NE]),
                                         start=False, stop=True).then_inc(prefixed, 1)

                    def head():
                        if project:
                            attend(0, 0)
                            attend(1, 1)
                        else:
                            start.tensor(pe)
                        norm_turn(pe, nb, 0, 0)
                        score(0, 0)

                    def body(i, last):
                        for q in range(2):
                            c = 2 * i + q
                            if project and not last:
                                attend(c + 2, q)
                            if not (last and q):
                                norm_turn(pe, nb, c + 1, 1 - q)
                            prefix(c, q)
                            if not (last and q):
                                score(c + 1, 1 - q)
                    pair_loop(pe, None, head, body, NCH // 2)

                @block.scalar
                def _(act):
                    def evacuate(c, q):
                        wait(act, logits, c - 1)
                        norm_evacuate(act, nb, c, q)

                    def body(i, last):
                        for q in range(2):
                            c = 2 * i + q
                            if not (last and q):
                                evacuate(c + 1, 1 - q)
                            act.wait_ge(less_made, c + 1)
                            nc.scalar.activation(ex[q][:], less[q][:], ACT.Exp).then_inc(exped, 1)
                            act.wait_ge(nb.normed, c + 1)
                            wait(act, scattered[q], 128 * i)
                            nc.scalar.activation(rows[q][:, :, :, 0:D], nb.xn[q][:].unsqueeze(1).to_broadcast([P, 2, CT, D]),
                                                 ACT.Copy).then_inc(row_copied, 1)

                    def head():
                        if not project:
                            start.scalar(act)
                        evacuate(0, 0)
                    pair_loop(act, None, head, body, NCH // 2)

                @block.gpsimd
                def _(pool):
                    def scatter(c, q):
                        pool.wait_ge(routed, c + 1)
                        hold(pool, row_copied, c + 1, passed[1])
                        for k in range(2):
                            for j in range(CT):
                                nc.gpsimd.indirect_dma_start(
                                    out=slots, out_offset=bass.IndirectOffsetOnAxis(ap=dest[q][:, k, j:j + 1], axis=0),
                                    in_=rows[q][:, k, j, :], in_offset=None).then_inc(scattered[q], 16)

                    def body(i, last):
                        for q in range(2):
                            if not last:
                                norm_rstd(pool, nb, 2 * i + q + 2, q)
                            scatter(2 * i + q, q)

                    def head():
                        if not project:
                            start.gpsimd(pool)
                        norm_rstd(pool, nb, 0, 0)
                        norm_rstd(pool, nb, 1, 1)
                        pool.wait_ge(slots_ready, 16 * NE * (m + 1))
                    pair_loop(pool, None, head, body, NCH // 2)
                    for q in range(2):
                        pool.wait_ge(scattered[q], 128 * (NCH // 2))
                    pool.wait_ge(spare_ready, 32)

                @block.vector
                def _(dve):
                    steps = Steps(dve, steps_sem)

                    def divide(c, q, n):
                        dve.wait_ge(o_loaded[q], 64 * (n + 1))
                        wait(dve, projected, 2 * (c - 1))
                        nc.vector.tensor_tensor(out=onT[q][:], in0=num[q], in1=rcp[q], op=ALU.mult).then_inc(o_made, 1)

                    def residual(c, q, n):
                        if not project:
                            hold(dve, x_loaded[q], 16 * (n + 1), passed[0])
                            return
                        for g in range(2):
                            dve.wait_ge(projected, 2 * c + g + 1)
                            xs = XR[:, bass.ds(c * CT + 2 * g, 2), :]
                            ins = nc.vector.tensor_tensor(out=xs, in0=pY[:, g], in1=xs, op=ALU.add)
                        ins.then_inc(x_ready, 1)
                        hold(dve, x_ready, c + 1, passed[0])

                    def bc(ap):
                        return ap.unsqueeze(2).to_broadcast([P, CT, NE])

                    def choose(c, q):
                        dve.wait_ge(logits, c + 1)
                        steps.add(nc.vector.tensor_tensor(out=lg[q][:], in0=pL[q],
                                                          in1=br[:].unsqueeze(1).to_broadcast([P, CT, NE]), op=ALU.add))
                        steps.settle()
                        for k, src in enumerate((lg[q], l2[q])):
                            steps.add(nc.vector.tensor_reduce(out=top[q][:, k, :], in_=src[:], axis=AX.X, op=ALU.max))
                            steps.settle()
                            steps.add(nc.vector.tensor_tensor(out=eq[q][:, k], in0=src[:], in1=bc(top[q][:, k, :]), op=ALU.is_equal))
                            steps.settle()
                            steps.add(nc.vector.tensor_tensor(out=hit[:, k], in0=eq[q][:, k], in1=em8[:], op=ALU.mult))
                            steps.settle()
                            steps.add(nc.vector.tensor_reduce(out=em[q][:, k, :], in_=hit[:, k], axis=AX.X, op=ALU.min))
                            steps.settle()
                            steps.add(nc.vector.tensor_tensor(out=oh[q][:, k], in0=em8[:], in1=bc(em[q][:, k, :]), op=ALU.is_equal))
                            steps.settle()
                            if k == 0:
                                steps.add(nc.vector.scalar_tensor_tensor(out=l2[q][:], in0=oh[q][:, 0], scalar=-3e38,
                                                                         in1=lg[q][:], op0=ALU.mult, op1=ALU.add))
                                steps.settle()
                        nc.vector.tensor_tensor(out=mask[q][:], in0=oh[q][:, 0], in1=oh[q][:, 1], op=ALU.add).then_inc(masked, 1)
                        nc.vector.tensor_tensor(out=less[q][:, :, 0:NE], in0=lg[q][:], in1=bc(top[q][:, 0, :]), op=ALU.subtract)
                        nc.vector.tensor_tensor(out=less[q][:, :, NE], in0=top[q][:, 1, :], in1=top[q][:, 0, :],
                                                op=ALU.subtract).then_inc(less_made, 1)

                    def place(c, q, n):
                        dve.wait_ge(prefixed, c + 1)
                        dve.wait_ge(masked, c + 1)
                        steps.add(nc.vector.tensor_tensor(out=hit[:], in0=oh[q][:],
                                                          in1=pP[q].unsqueeze(1).to_broadcast([P, 2, CT, NE]), op=ALU.mult))
                        steps.add(nc.vector.tensor_reduce(out=here[:], in_=mask[q][:].rearrange("p j e -> p e j"), axis=AX.X, op=ALU.add))
                        steps.settle()
                        steps.add(nc.vector.tensor_reduce(out=pos[:], in_=hit[:], axis=AX.X, op=ALU.add))
                        steps.add(nc.vector.tensor_tensor(out=seen[1 - q][:], in0=seen[q][:], in1=here[:], op=ALU.add))
                        steps.add(nc.vector.tensor_scalar(slot[:], em[q][:], float(NE), float(CAP), ALU.add, ALU.mult))
                        dve.wait_ge(exped, c + 1)
                        steps.add(nc.vector.tensor_reduce(out=gsum[:, 0, :], in_=ex[q][:, :, 0:NE], axis=AX.X, op=ALU.add))
                        steps.settle()
                        steps.add(nc.vector.tensor_copy(seen_b[1 - q][:], seen[1 - q][:]))
                        steps.add(nc.vector.tensor_scalar(keep[:], pos[:], float(CAP), None, ALU.is_lt))
                        steps.add(nc.vector.tensor_tensor(out=off[:], in0=slot[:], in1=pos[:], op=ALU.add))
                        steps.add(nc.vector.reciprocal(gate[:, 0, :], gsum[:, 0, :]))
                        steps.settle()
                        steps.add(nc.vector.tensor_tensor(out=off[:], in0=off[:], in1=trash[:, :, bass.ds(c * CT, CT)], op=ALU.subtract))
                        steps.add(nc.vector.tensor_tensor(out=gate[:, 1, :], in0=ex[q][:, :, NE], in1=gate[:, 0, :], op=ALU.mult))
                        steps.settle()
                        steps.add(nc.vector.tensor_tensor(out=off[:], in0=off[:], in1=keep[:], op=ALU.mult))
                        steps.add(nc.vector.tensor_tensor(out=gate[:], in0=gate[:], in1=keep[:], op=ALU.mult))
                        steps.settle()
                        wait(dve, scattered[q], 128 * n)
                        steps.add(nc.vector.tensor_tensor(out=dest[q][:], in0=off[:], in1=trash[:, :, bass.ds(c * CT, CT)], op=ALU.add))
                        steps.add(nc.vector.tensor_tensor(out=gsum[:, 0, :], in0=gate[:, 0, :], in1=gate[:, 1, :], op=ALU.add))
                        steps.settle()
                        steps.add(nc.vector.tensor_scalar(gsum[:, 0, :], gsum[:, 0, :], 1e-6, 2.0, ALU.max, ALU.mult))
                        steps.settle()
                        steps.add(nc.vector.reciprocal(gsum[:, 1, :], gsum[:, 0, :]))
                        steps.settle()
                        nc.vector.tensor_copy(rows[q][:].bitcast(I32)[:, :, :, D + 1],
                                              tok_id[:, bass.ds(c * CT, CT)].unsqueeze(1).to_broadcast([P, 2, CT]))
                        nc.vector.tensor_tensor(out=rows[q][:, :, :, D], in0=gate[:],
                                                in1=gsum[:, 1, :].unsqueeze(1).to_broadcast([P, 2, CT]),
                                                op=ALU.mult).then_inc(routed, 1)

                    def normalise(c, q):
                        wait(dve, row_copied, c - 1)
                        norm_apply(dve, nb, c, q)

                    def head():
                        steps.add(nc.vector.memset(seen[0][:], 0.0))
                        steps.add(nc.vector.memset(seen_b[0][:], 0.0))
                        if project:
                            divide(0, 0, 0)
                            divide(1, 1, 0)
                        residual(0, 0, 0)
                        norm_stats(nb, steps, 0, 0)
                        residual(1, 1, 0)
                        normalise(0, 0)
                        norm_stats(nb, steps, 1, 1)
                        if not project:
                            dve.wait_ge(consts, CONSTS)
                            dve.wait_ge(start.first_loaded, 48)

                    def body(i, last):
                        for q in range(2):
                            c = 2 * i + q
                            if project and not last:
                                divide(c + 2, q, i + 1)
                            if not (last and q):
                                normalise(c + 1, 1 - q)
                            choose(c, q)
                            if not last:
                                residual(c + 2, q, i + 1)
                                norm_stats(nb, steps, c + 2, q)
                            place(c, q, i)
                            if project and isinstance(i, int) and c == 0:
                                dve.wait_ge(den_loaded, 16)
                                nc.vector.reciprocal(den[:], den[:]).then_inc(den_inv, 1)
                    pair_loop(dve, steps, head, body, NCH // 2)

        def experts(m):
            tag = f"e{m}"
            with ExitStack() as scope:
                prep = prepare(scope) if m == 0 else None
                XE = [sb(scope, f"XE{tag}{q}", [P, SLOT_TILES, ROW]) for q in range(2)]
                XT = [sb(scope, f"XT{tag}{p}", [P, KD, CAP], F32R) for p in ("hi", "lo")]
                W1s = [sb(scope, f"W1s{tag}{p}", [P, KD, FF], F32R) for p in ("hi", "lo")]
                W2s = [sb(scope, f"W2s{tag}{p}", [P, KF, D], F32R) for p in ("hi", "lo")]
                hid = [sb(scope, f"hid{tag}{p}", [P, KF, CAP], F32R) for p in ("hi", "lo")]
                HRING = 2
                hf = [sb(scope, f"hf{tag}{r}", [P, CAP]) for r in range(HRING)]
                PASSES = ((0, 0), (0, 1), (1, 0))
                b1c = [sb(scope, f"b1c{tag}{q}", [P, KF]) for q in range(2)]
                Y = [sb(scope, f"Y{tag}{q}", [P, SLOT_TILES, D]) for q in range(2)]
                yb = [sb(scope, f"yb{tag}{q}", [P, D]) for q in range(2)]
                pX = ps(scope, f"pX{tag}", [P, 2, KD, D])
                pH = ps(scope, f"pH{tag}", [P, 2, 2, CHUNK])
                pO = ps(scope, f"pO{tag}", [P, 2, CHUNK])
                x_in, x_turned, x_out = pair(f"x_in{tag}"), sem(f"x_turned{tag}"), sem(f"x_out{tag}")
                h_made, h_out, bias_in = sem(f"h_made{tag}"), sem(f"h_out{tag}"), sem(f"bias_in{tag}")
                o_made, o_out, y_made = sem(f"o_made{tag}"), sem(f"o_out{tag}"), sem(f"y_made{tag}")
                added = sem(f"added{tag}")
                g_made, hid_hi, xt_hi = sem(f"g_made{tag}"), sem(f"hid_hi{tag}"), sem(f"xt_hi{tag}")
                w1_hi, w1_lo, w2_hi, w2_lo = (sem(f"{w}{tag}") for w in ("w1_hi", "w1_lo", "w2_hi", "w2_lo"))
                block = scope.enter_context(nc.Block())
                if prep:
                    prep.banks = [pO[:, g, :] for g in range(2)]
                GROUPS = [(0, 2), (2, 4), (4, 5)]
                NG = len(GROUPS)

                @block.sync
                def _(sp):
                    def load_slots(e, q):
                        sp.dma_start(XE[q][:], slots[bass.ds(e * CAP, CAP), :].rearrange("(j p) d -> p j d", p=P)).then_inc(x_in[q], 16)

                    for q in range(2):
                        load_slots(q, q)
                    if prep:
                        prep.sync(sp)

                    def body(i):
                        for q in range(2):
                            e = 2 * i + q + 2
                            sp.wait_ge(added, 16 * SLOT_TILES * (e - 1))
                            load_slots(e, q)
                            sp.wait_ge(o_out, SLOT_TILES * (e - 1))
                            load_weights(sp, e, q)
                    with sp.Fori(0, NE // 2 - 1) as i:
                        body(i)
                    if m == 0:
                        for q in range(2):
                            sp.wait_ge(o_out, SLOT_TILES * (NE - 1 + q))
                            load_weights(sp, q, q)

                @block.tensor
                def _(pe):
                    def turn(e, q, n, g0, g1):
                        pe.wait_ge(x_in[q], 16 * (n + 1))
                        for g in range(g0, g1):
                            a, b = GROUPS[g]
                            wait(pe, x_out, NG * e + g - 1)
                            for j in range(a, b):
                                for k in range(KD):
                                    ins = nc.tensor.transpose(pX[:, (NG * q + g) % 2, k, (j - a) * P:(j - a + 1) * P],
                                                              XE[q][:, j, k * P:(k + 1) * P], ident[:])
                            ins.then_inc(x_turned, 1)

                    def up(e):
                        pe.wait_ge(w1_lo, e + 1)
                        pe.wait_ge(x_out, NG * (e + 1))
                        for f in range(KF):
                            wait(pe, g_made, KF * e + f - 1)
                            for h in range(2):
                                for k in range(KD):
                                    for n, (a, b) in enumerate(PASSES):
                                        ins = nc.tensor.matmul(pH[:, f % 2, h, 0:HH], W1s[a][:, k, f * P:(f + 1) * P],
                                                               XT[b][:, k, h * HH:(h + 1) * HH],
                                                               start=(k == 0 and n == 0), stop=(k == KD - 1 and n == 2))
                            ins.then_inc(h_made, 1)

                    def down(e, q, j0, j1):
                        pe.wait_ge(w2_lo, e + 1)
                        for j in range(j0, j1):
                            wait(pe, o_out, SLOT_TILES * e + j - 1)
                            for f in range(KF):
                                if j == 0:
                                    pe.wait_ge(h_out, KF * e + f + 1)
                                for n, (a, b) in enumerate(PASSES):
                                    ins = nc.tensor.matmul(pO[:, (SLOT_TILES * q + j) % 2, 0:D], hid[b][:, f, j * P:(j + 1) * P],
                                                           W2s[a][:, f, :], start=(f == 0 and n == 0), stop=(f == KF - 1 and n == 2))
                            ins.then_inc(o_made, 1)

                    def body(i, last):
                        for q in range(2):
                            e = 2 * i + q
                            up(e)
                            if not (last and q):
                                turn(e + 1, 1 - q, i + q, 0, 2)
                            down(e, q, 0, 1)
                            if not (last and q):
                                turn(e + 1, 1 - q, i + q, 2, NG)
                            down(e, q, 1, SLOT_TILES)
                    pair_loop(pe, None, lambda: turn(0, 0, 0, 0, NG), body, NE // 2)
                    if prep:
                        pe.wait_ge(o_out, SLOT_TILES * NE)
                        prep.tensor(pe)

                @block.scalar
                def _(act):
                    def high1(e, q, n):
                        act.wait_ge(w_loaded[q], 48 * (n + 1 + (NE // 2) * m))
                        wait(act, h_made, KF * e)
                        nc.scalar.activation(W1s[0][:], W1[q][:], ACT.Copy).then_inc(w1_hi, 1)

                    def body(i, last):
                        for q in range(2):
                            e = 2 * i + q
                            nc.scalar.activation(b1c[q][:], b1T[:, bass.ds(e * KF, KF)], ACT.Copy).then_inc(bias_in, 1)
                            act.wait_ge(bias_in, e + 1)
                            for f in range(KF):
                                act.wait_ge(h_made, KF * e + f + 1)
                                wait(act, h_out, KF * e + f - HRING + 1)
                                nc.scalar.activation(hf[f % HRING][:].rearrange("p (h c) -> p h c", h=2), pH[:, f % 2, :, 0:HH],
                                                     ACT.Gelu, bias=b1c[q][:, f:f + 1]).then_inc(g_made, 1)
                                if f == 1:
                                    wait(act, o_made, SLOT_TILES * e)
                                    nc.scalar.activation(W2s[0][:], W2[q][:], ACT.Copy).then_inc(w2_hi, 1)
                            if not (last and q):
                                high1(e + 1, 1 - q, i + q)
                    pair_loop(act, None, lambda: high1(0, 0, 0), body, NE // 2)
                    if prep:
                        prep.scalar(act)

                @block.vector
                def _(dve):
                    def evacuate(e, q):
                        for g, (a, b) in enumerate(GROUPS):
                            dve.wait_ge(x_turned, NG * e + g + 1)
                            wait(dve, h_made, KF * e)
                            src = pX[:, (NG * q + g) % 2, :, 0:(b - a) * P]
                            high = XT[0][:, :, a * P:b * P]
                            nc.vector.tensor_copy(high, src).then_inc(xt_hi, 1)
                            dve.wait_ge(xt_hi, NG * e + g + 1)
                            nc.vector.tensor_tensor(out=XT[1][:, :, a * P:b * P], in0=src, in1=high, op=ALU.subtract).then_inc(x_out, 1)

                    def low1(e, q):
                        dve.wait_ge(w1_hi, e + 1)
                        nc.vector.tensor_tensor(out=W1s[1][:], in0=W1[q][:], in1=W1s[0][:], op=ALU.subtract).then_inc(w1_lo, 1)

                    def hidden(e, f):
                        n = KF * e + f
                        dve.wait_ge(g_made, n + 1)
                        nc.vector.tensor_copy(hid[0][:, f, :], hf[f % HRING][:]).then_inc(hid_hi, 1)
                        dve.wait_ge(hid_hi, n + 1)
                        nc.vector.tensor_tensor(out=hid[1][:, f, :], in0=hf[f % HRING][:], in1=hid[0][:, f, :],
                                                op=ALU.subtract).then_inc(h_out, 1)

                    def result(e, q, j):
                        n = SLOT_TILES * e + j
                        dve.wait_ge(o_made, n + 1)
                        y = yb[(SLOT_TILES * q + j) % 2]
                        nc.vector.tensor_tensor(out=y[:], in0=pO[:, (SLOT_TILES * q + j) % 2, 0:D], in1=B2[q][:],
                                                op=ALU.add).then_inc(o_out, 1)
                        dve.wait_ge(o_out, n + 1)
                        nc.vector.tensor_scalar(Y[q][:, j, :], y[:], XE[q][:, j, D:D + 1], None, ALU.mult).then_inc(y_made, 1)

                    def head():
                        low1(0, 0)
                        evacuate(0, 0)

                    def body(i, last):
                        for q in range(2):
                            e = 2 * i + q
                            for f in range(KF):
                                hidden(e, f)
                            if not (last and q):
                                evacuate(e + 1, 1 - q)
                            wait(dve, added, 16 * SLOT_TILES * (e - 1))
                            for j in range(SLOT_TILES):
                                result(e, q, j)
                                if j == 0 and not (last and q):
                                    low1(e + 1, 1 - q)
                    pair_loop(dve, None, head, body, NE // 2)
                    if prep:
                        prep.vector(dve)

                @block.gpsimd
                def _(pool):
                    if m == 0:
                        prep.gpsimd(pool)
                        pool.wait_ge(resid_ready[0], 64)

                    def low2(e, q):
                        pool.wait_ge(w2_hi, e + 1)
                        nc.gpsimd.tensor_tensor(out=W2s[1][:], in0=W2[q][:], in1=W2s[0][:], op=ALU.subtract).then_inc(w2_lo, 1)

                    def body(i, last):
                        for q in range(2):
                            e = 2 * i + q
                            low2(e, q)
                            wait(pool, added, 16 * SLOT_TILES * e)
                            for j in range(SLOT_TILES):
                                hold(pool, y_made, SLOT_TILES * e + j + 1, passed[1])
                                nc.gpsimd.indirect_dma_start(
                                    out=resid[m], out_offset=bass.IndirectOffsetOnAxis(ap=XE[q][:].bitcast(I32)[:, j, D + 1:D + 2], axis=0),
                                    in_=Y[q][:, j, :], in_offset=None, compute_op=ALU.add).then_inc(added, 16)
                    pair_loop(pool, None, lambda: None, body, NE // 2)
                    pool.wait_ge(added, 16 * SLOT_TILES * NE)

        def load_parts(sp, n, dq, dk, sm):
            for s in range(2):
                at = 0
                for part, copies in ((0, 3), (1, 2), (2, 1)):
                    rows = slice((s * SPLIT + at) * HALF, (s * SPLIT + at + copies) * HALF)
                    view = qk_parts.rearrange("(b w g a s h d) t -> w s b g h a d t", b=B, w=2, g=FT // 2, a=PARTS, s=2, h=HT)
                    at_head = (bass.ds(n // H, 1), bass.ds((n // HT) % 2, 1), bass.ds(n % HT, 1))
                    qs = view[(0, s) + at_head + (part,)].rearrange("b g h d t -> (b g h d) t")
                    ks = view[(1, s) + at_head + (slice(0, copies),)].rearrange("b g h a d t -> (b g h) a d t")
                    sp.dma_start(dq[rows, :], qs.unsqueeze(0).to_broadcast([copies, HALF, T])).then_inc(sm, 16)
                    sp.dma_start(dk[rows, :], ks[0]).then_inc(sm, 16)
                    at += copies

        def qkv(VA, XR, hq0, hk0, mx40, hd_loaded, m_scored, m_reduced):
            with ExitStack() as scope:
                nb = norm_buffers(scope, "q", XR)
                RING = 4
                LAG = 2
                ta = [sb(scope, f"ta{r}", [P, CHUNK]) for r in range(2)]
                tb = [sb(scope, f"tb{r}", [P, CHUNK]) for r in range(2)]
                tr = [sb(scope, f"tr{r}", [P, CHUNK]) for r in range(RING)]
                rem = [sb(scope, f"rem{r}", [P, CHUNK]) for r in range(RING)]
                spl = [sb(scope, f"spl{r}", [P, PARTS, CHUNK], BF16) for r in range(RING)]
                pQ = ps(scope, "pQ", [P, 2, CHUNK])
                pV = ps(scope, "pV", [P, 2, 2, D])
                steps_sem = sem("dve_stepsq")
                x_loaded = pair("x_loadedq")
                q_made, q_read, summed = sem("q_made"), sem("q_read"), sem("summed")
                hi, rem_made, mid, low = sem("hi"), sem("rem_made"), sem("mid"), sem("low")
                v_made, v_out = sem("v_made"), sem("v_out")
                stored = [sem(f"parts_stored{r}") for r in range(RING)]
                block = scope.enter_context(nc.Block())
                ITEMS = 2 * FT

                @block.sync
                def _(sp):
                    def load(c, q, n):
                        wait(sp, x_loaded[q], 16 * n)
                        sp.dma_start(XR[:, bass.ds(c * CT, CT), :],
                                     resid[0][bass.ds(c * CHUNK, CHUNK), :].rearrange("(t p) d -> p t d", p=P)).then_inc(x_loaded[q], 16)
                    for q in range(2):
                        load(q, q, 0)
                    with sp.Fori(1, NCH // 2) as i:
                        for q in range(2):
                            load(2 * i + q, q, i)

                    def store(i, k0, k1):
                        for k in range(k0, k1):
                            q, f = divmod(k, FT)
                            sp.wait_ge(low, ITEMS * i + k + 1)
                            sp.wait_ge(mid, ITEMS * i + k + 1)
                            b, qc = i // 2, 2 * (i % 2) + q
                            base = (b * FT + f) * PARTS * P
                            dst = qk_parts[bass.ds(base, PARTS * P), bass.ds(qc * CHUNK, CHUNK)].rearrange("(a p) t -> p a t", a=PARTS)
                            sp.dma_start(dst, spl[k % RING][:]).then_inc(stored[k % RING], 16)
                    with sp.Fori(0, NCH // 2 - 1) as i:
                        store(i, 0, ITEMS)
                    for r in range(RING):
                        sp.wait_ge(stored[r], 16 * (ITEMS // RING) * (NCH // 2 - 1))
                    load_parts(sp, 0, hq0, hk0, hd_loaded[0])
                    store(NCH // 2 - 1, 0, ITEMS)
                    for r in range(RING):
                        sp.wait_ge(stored[r], 16 * (ITEMS // RING) * (NCH // 2))

                @block.tensor
                def _(pe):
                    def turn(c, q):
                        norm_turn(pe, nb, c, q)

                    def body(i, last):
                        for q in range(2):
                            c = 2 * i + q
                            pe.wait_ge(nb.xT_ready, c + 1)
                            for f in range(FT):
                                if f == 3 and not (last and q):
                                    turn(c + 1, 1 - q)
                                wait(pe, q_read, FT * c + f - 1)
                                for k in range(KD):
                                    ins = nc.tensor.matmul(pQ[:, f % 2, :], wqk[:, k, f * P:(f + 1) * P], nb.xT[q][:, k, :],
                                                           start=(k == 0), stop=(k == KD - 1))
                                ins.then_inc(q_made, 1)
                                if f not in (1, 2):
                                    continue
                                g = f - 1
                                wait(pe, v_out, 2 * c + g - 1)
                                for j in range(2):
                                    for k in range(KD):
                                        t = 2 * g + j
                                        ins = nc.tensor.matmul(pV[:, g, j, :], nb.xT[q][:, k, t * P:(t + 1) * P], wv[:, k, :],
                                                               start=(k == 0), stop=(k == KD - 1))
                                ins.then_inc(v_made, 1)
                    pair_loop(pe, None, lambda: turn(0, 0), body, NCH // 2)
                    pe.wait_ge(hd_loaded[0], LOADS)
                    pe.wait_ge(q_read, ITEMS * (NCH // 2))
                    for s in range(4 * EARLY):
                        t, j = divmod(s, 4)
                        wait(pe, m_reduced, s - 1)
                        nc.tensor.matmul(pQ[:, s % 2, :], hq0[0:QROWS, t * P:(t + 1) * P], hk0[0:QROWS, j * CHUNK:(j + 1) * CHUNK],
                                         start=True, stop=True).then_inc(m_scored, 1)

                @block.scalar
                def _(act):
                    def evacuate(c, q):
                        wait(act, q_made, FT * (c - 1))
                        norm_evacuate(act, nb, c, q)

                    def high(n, r, uses):
                        act.wait_ge(summed, n + 1)
                        wait(act, stored[r], 16 * uses)
                        nc.scalar.activation(spl[r][:, 0, :], tr[r][:], ACT.Copy).then_inc(hi, 1)

                    def middle(n, r):
                        act.wait_ge(rem_made, n + 1)
                        nc.scalar.activation(spl[r][:, 1, :], rem[r][:], ACT.Copy).then_inc(mid, 1)

                    def body(i, last):
                        for k in range(ITEMS):
                            n = ITEMS * i + k
                            if k % FT == 3 and not (last and k >= FT):
                                evacuate(2 * i + k // FT + 1, 1 - k // FT)
                            high(n, k % RING, 2 * i + k // RING)
                            if not (isinstance(i, int) and i == 0 and k < LAG):
                                middle(n - LAG, (k - LAG) % RING)
                    pair_loop(act, None, lambda: evacuate(0, 0), body, NCH // 2)
                    total = ITEMS * (NCH // 2)
                    for n in range(total - LAG, total):
                        middle(n, n % RING)

                @block.gpsimd
                def _(pool):
                    def add(n, k):
                        pool.wait_ge(q_read, n + 1)
                        wait(pool, rem_made, n - RING + 1)
                        nc.gpsimd.tensor_tensor(out=tr[k % RING][:], in0=ta[k % 2][:], in1=tb[k % 2][:], op=ALU.add).then_inc(summed, 1)

                    def lowest(n, r):
                        pool.wait_ge(mid, n + 1)
                        nc.gpsimd.tensor_tensor(out=spl[r][:, 2, :], in0=rem[r][:], in1=spl[r][:, 1, :], op=ALU.subtract).then_inc(low, 1)

                    def body(i, last):
                        for k in range(ITEMS):
                            n = ITEMS * i + k
                            if k % FT == 0 and not (last and k >= FT):
                                norm_rstd(pool, nb, 2 * i + k // FT + 1, 1 - k // FT)
                            add(n, k)
                            if not (isinstance(i, int) and i == 0 and k < LAG + 1):
                                lowest(n - LAG - 1, (k - LAG - 1) % RING)
                    pair_loop(pool, None, lambda: norm_rstd(pool, nb, 0, 0), body, NCH // 2)
                    total = ITEMS * (NCH // 2)
                    for n in range(total - LAG - 1, total):
                        lowest(n, n % RING)
                    pool.wait_ge(nb.normed, NCH)
                    pool.wait_ge(low, total)

                @block.vector
                def _(dve):
                    steps = Steps(dve, steps_sem)

                    def stats(c, q, n):
                        hold(dve, x_loaded[q], 16 * (n + 1), passed[0])
                        norm_stats(nb, steps, c, q)

                    def rope(n, k, qc):
                        f = k % FT
                        dve.wait_ge(q_made, n + 1)
                        wait(dve, summed, n - 1)
                        cs = cosT[:, bass.ds(qc * CHUNK, CHUNK)]
                        sn = sinT[:, bass.ds(qc * CHUNK, CHUNK)]
                        nc.vector.scalar_tensor_tensor(out=ta[k % 2][:], in0=pQ[:, f % 2, :], scalar=bqk[:, f:f + 1], in1=cs,
                                                       op0=ALU.add, op1=ALU.mult)
                        for a, b in ((0, 64), (64, 0)):
                            ins = nc.vector.scalar_tensor_tensor(out=tb[k % 2][a:a + 64, :], in0=pQ[b:b + 64, f % 2, :],
                                                                 scalar=bqk[b:b + 64, f:f + 1], in1=sn[b:b + 64, :],
                                                                 op0=ALU.add, op1=ALU.mult)
                        ins.then_inc(q_read, 1)

                    def remainder(n, r):
                        dve.wait_ge(hi, n + 1)
                        wait(dve, low, n - RING + 1)
                        nc.vector.tensor_tensor(out=rem[r][:], in0=tr[r][:], in1=spl[r][:, 0, :], op=ALU.subtract).then_inc(rem_made, 1)

                    def head():
                        stats(0, 0, 0)
                        stats(1, 1, 0)
                        norm_apply(dve, nb, 0, 0)

                    def body(i, last):
                        for k in range(ITEMS):
                            n = ITEMS * i + k
                            q, f = divmod(k, FT)
                            c = 2 * i + q
                            more = not (last and q)
                            if f == 3 and not last:
                                stats(c + 2, q, i + 1)
                            rope(n, k, 2 * (i % 2) + q)
                            if f == 1 and more:
                                norm_apply(dve, nb, c + 1, 1 - q)
                            if not (isinstance(i, int) and i == 0 and k < LAG):
                                remainder(n - LAG, (k - LAG) % RING)
                            if f in (1, 2):
                                g = f - 1
                                dve.wait_ge(v_made, 2 * c + g + 1)
                                nc.vector.tensor_tensor(out=VA[:, bass.ds(c * CT + 2 * g, 2), :], in0=pV[:, g],
                                                        in1=bv[:].unsqueeze(1).to_broadcast([P, 2, D]), op=ALU.add).then_inc(v_out, 1)
                    pair_loop(dve, steps, head, body, NCH // 2)
                    dve.wait_ge(v_out, 2 * NCH)
                    total = ITEMS * (NCH // 2)
                    for s in range(4 * EARLY):
                        if s in (3, 6):
                            n = total - LAG + s // 3 - 1
                            remainder(n, n % RING)
                        t, j = divmod(s, 4)
                        dve.wait_ge(m_scored, s + 1)
                        nc.vector.tensor_reduce(out=mx40[:, t, j:j + 1], in_=pQ[:, s % 2, :], axis=AX.X,
                                                op=ALU.max).then_inc(m_reduced, 1)
                    dve.wait_ge(m_reduced, 4 * EARLY)

        def attention(VA, XR, hq0, hk0, mx40, hd_loaded, m_scored, m_reduced, num, rcp, o_loaded):
            with ExitStack() as scope:
                hq = [hq0] + [sb(scope, f"hq{r}", [MROWS, T], BF16) for r in range(1, HEADS)]
                hk = [hk0] + [sb(scope, f"hk{r}", [MROWS, T], BF16) for r in range(1, HEADS)]
                RING = 4
                pt = [sb(scope, f"pt{r}", [P, T]) for r in range(RING)]
                vh = [sb(scope, f"vh{q}", [P, KT, 32]) for q in range(2)]
                mx4 = [mx40, sb(scope, "mx41", [P, KT, 4])]
                mx = sb(scope, "mx", [P, KT])
                ma = sb(scope, "ma", [P, 3, KT])
                mp = sb(scope, "mp", [P, PARTS, 32], BF16)
                mt = sb(scope, "mt", [P, PARTS, 32], BF16)
                oe = [sb(scope, f"oe{q}", [P, CHUNK]) for q in range(2)]
                den = sb(scope, "den0", [P, H * T // P])
                pS = ps(scope, "pS", [P, 2, 2, CHUNK])
                MB = 3
                pM = ps(scope, "pM", [P, MB, CHUNK])
                pO = ps(scope, "pOv", [P, CHUNK])
                inited = sem("inited")
                m_rows = pair("m_rows")
                max_stored = sem("max_stored")
                m_done = sem("m_done")
                pool_steps, m_parted, m_turned = sem("pool_stepsa"), sem("m_parted"), sem("m_turned")
                scored, exped, summed, o_out = sem("scored"), sem("expeda"), sem("summeda"), sem("o_outa")
                v_ready, bias_added = sem("v_ready"), sem("bias_added")
                den_loaded, den_inv, den_stored = sem("den_loaded0"), sem("den_inv0"), sem("den_stored0")
                o_stored = pair("o_stored")
                block = scope.enter_context(nc.Block())
                HALFS = 2 * KT
                MS = 4 * KT

                def maxima_of(n, u):
                    return (n + 1, u + LEAD) if u + LEAD < KT else (n + 2, u + LEAD - KT)

                bank = [s % MB for s in range(MS - 1)] + [1]
                before_bank = [max(r for r in range(s - MS, s) if bank[r % MS] == bank[s]) + 1 for s in range(MS)]

                def exists(h):
                    return not isinstance(h, int) or h < NH

                def run(eng, body, steps=None):
                    body(-1, HEADS - 1)
                    if steps:
                        per0 = steps.n
                    body(0, 0)
                    if steps:
                        per = steps.n - per0
                    for n in range(1, HEADS):
                        body(n, n)
                    with eng.Fori(1, NH // HEADS - 1) as i:
                        for r in range(HEADS):
                            if steps:
                                steps.restart(per0 + (HEADS * i + r) * per)
                            body(HEADS * i + r, r)
                    for n in range(NH - HEADS, NH):
                        if steps:
                            steps.restart(per0 + n * per)
                        body(n, n % HEADS)

                @block.sync
                def _(sp):
                    def max_to_rows(h, r):
                        q = r % 2
                        sp.wait_ge(m_turned, h + 1)
                        sp.dma_start(max_rows[q], mt[:].rearrange("p a i -> p (a i)")).then_inc(max_stored, 16)
                        sp.wait_ge(max_stored, 16 * (h + 1))
                        src = max_rows[q].rearrange("(b j) (a i) -> a j b i", b=4, a=PARTS)[:, 0:KT]
                        for a in range(PARTS):
                            sp.dma_start(hq[r][QROWS + a:QROWS + a + 1, :].rearrange("o (j b i) -> o j b i", j=KT, b=4),
                                         src[a:a + 1]).then_inc(m_rows[q], 16)

                    def body(n, r):
                        q = r % 2
                        if isinstance(n, int) and n < 0:
                            for h in (1, 2):
                                load_parts(sp, h, hq[h], hk[h], hd_loaded[h])
                            for e in range(NE):
                                sp.dma_start(slots[e * CAP:(e + 1) * CAP, D:D + 2].rearrange("(p j) d -> p j d", p=P),
                                             meta[:]).then_inc(slots_ready, 16)
                        elif exists(n + 3):
                            wait(sp, scored, HALFS * n)
                            load_parts(sp, n + 3, hq[(r + 3) % HEADS], hk[(r + 3) % HEADS], hd_loaded[(r + 3) % HEADS])
                        if not (isinstance(n, int) and n <= 0):
                            store(n - 1, 1 - q)
                        if isinstance(n, int) and n == NH - 4:
                            for parity in range(2):
                                sp.wait_ge(o_stored[parity], 16 * H // 2)
                            sp.dma_start(den[:], denominators(0)).then_inc(den_loaded, 16)
                        if isinstance(n, int) and n == NH - 2:
                            sp.wait_ge(den_inv, 1)
                            sp.dma_start(reciprocals(0), den[:]).then_inc(den_stored, 16)
                        if exists(n + 1):
                            max_to_rows(n + 1, (r + 1) % HEADS)

                    def store(h, q):
                        sp.wait_ge(o_out, h + 1)
                        sp.dma_start(attn[bass.ds(h * 32, 32), :].rearrange("r (j t) -> j r t", j=4), oe[q][:]).then_inc(o_stored[q], 16)
                    run(sp, body)
                    sp.wait_ge(den_stored, 16)
                    for q in range(2):
                        load_sums(sp, 0, q, num, rcp, o_loaded)
                    store(NH - 1, 1)
                    for q in range(2):
                        sp.wait_ge(o_stored[q], 16 * NH // 2)

                @block.tensor
                def _(pe):
                    def loaded(h, r):
                        pe.wait_ge(hd_loaded[r], LOADS * (h // HEADS + 1))

                    def maxima(h, t, r, j0, j1):
                        if t == 0 and j0 == 0:
                            loaded(h, r)
                        for j in range(j0, j1):
                            s = 4 * t + j
                            wait(pe, m_reduced, MS * h + before_bank[s])
                            nc.tensor.matmul(pM[:, bank[s], :], hq[r][0:QROWS, t * P:(t + 1) * P], hk[r][0:QROWS, j * CHUNK:(j + 1) * CHUNK],
                                             start=True, stop=True).then_inc(m_scored, 1)

                    def scores(n, u, g, r):
                        wait(pe, exped, HALFS * n + 2 * u + g - 1)
                        for j in range(2):
                            ins = nc.tensor.matmul(pS[:, g, j, :], hk[r][:, u * P:(u + 1) * P],
                                                   hq[r][:, (2 * g + j) * CHUNK:(2 * g + j + 1) * CHUNK], start=True, stop=True)
                        ins.then_inc(scored, 1)

                    def values(n, u, q):
                        pe.wait_ge(exped, HALFS * n + 2 * u + 2)
                        if u == 0:
                            pe.wait_ge(v_ready, n + 1)
                            wait(pe, o_out, n)
                        for j in range(4):
                            ins = nc.tensor.matmul(pO[32 * j:32 * (j + 1), :], vh[q][:, u, :], pt[u % RING][:, j * CHUNK:(j + 1) * CHUNK],
                                                   start=(u == 0), stop=(u == KT - 1))
                        ins.then_inc(summed, 1)

                    for t in range(EARLY, LEAD):
                        maxima(0, t, 0, 0, 4)

                    def body(n, r):
                        q = r % 2
                        real = not (isinstance(n, int) and n < 0)
                        for u in range(KT):
                            h, t = maxima_of(n, u)
                            mr = (r + (1 if t >= LEAD else 2)) % HEADS
                            if real:
                                if u == 0:
                                    if isinstance(n, int) and n == 0:
                                        pe.wait_ge(inited, 1)
                                    loaded(n, r)
                                    pe.wait_ge(m_rows[q], 48 * (n // 2 + 1))
                                scores(n, u, 0, r)
                            if exists(h):
                                maxima(h, t, mr, 0, 2)
                            if real:
                                scores(n, u, 1, r)
                            if exists(h):
                                maxima(h, t, mr, 2, 3)
                            if real and u:
                                values(n, u - 1, q)
                            elif real and not (isinstance(n, int) and n == 0):
                                values(n - 1, KT - 1, 1 - q)
                            if exists(h):
                                maxima(h, t, mr, 3, 4)
                    run(pe, body)
                    values(NH - 1, KT - 1, 1)

                @block.scalar
                def _(act):
                    def evacuate(h, q, uses):
                        act.wait_ge(summed, KT * (h + 1))
                        wait(act, o_stored[q], 16 * uses)
                        nc.scalar.activation(oe[q][:], pO[:], ACT.Copy).then_inc(o_out, 1)

                    def body(n, r):
                        q = r % 2
                        if isinstance(n, int) and n < 0:
                            return
                        for u in range(KT):
                            wait(act, summed, KT * n + u - RING + 1)
                            for g in range(2):
                                act.wait_ge(scored, HALFS * n + 2 * u + g + 1)
                                nc.scalar.activation(pt[u % RING][:, g * 1024:(g + 1) * 1024], pS[:, g], ACT.Exp,
                                                     scale=DH ** -0.5).then_inc(exped, 1)
                            if u == 0 and not (isinstance(n, int) and n == 0):
                                evacuate(n - 1, 1 - q, (n - 1) // 2)
                    run(act, body)
                    evacuate(NH - 1, 1, NH // 2 - 1)

                @block.vector
                def _(dve):
                    def reduce(h, t, q, j0, j1):
                        for j in range(j0, j1):
                            s = 4 * t + j
                            dve.wait_ge(m_scored, MS * h + s + 1)
                            nc.vector.tensor_reduce(out=mx4[q][:, t, j:j + 1], in_=pM[:, bank[s], :], axis=AX.X,
                                                    op=ALU.max).then_inc(m_reduced, 1)

                    def finish(h, u, q):
                        if u == KT - LEAD:
                            dve.wait_ge(m_reduced, MS * (h + 1))
                            wait(dve, m_parted, h)
                            nc.vector.tensor_reduce(out=mx[:], in_=mx4[q][:], axis=AX.X, op=ALU.max).then_inc(m_done, 1)
                        if u == KT - LEAD + 1:
                            dve.wait_ge(m_parted, h + 1)
                            wait(dve, max_stored, 16 * h)
                            nc.vector.transpose(mt[:], mp[:]).then_inc(m_turned, 1)

                    for t in range(EARLY, LEAD):
                        reduce(0, t, 0, 0, 4)

                    def body(n, r):
                        q = r % 2
                        for u in range(KT):
                            h, t = maxima_of(n, u)
                            mqq = 1 - q if t >= LEAD else q
                            if exists(h):
                                reduce(h, t, mqq, 0, 3)
                            if exists(n + 1):
                                finish(n + 1, u, 1 - q)
                            if exists(h):
                                reduce(h, t, mqq, 3, 4)
                        if isinstance(n, int) and n == NH - 3:
                            dve.wait_ge(den_loaded, 16)
                            nc.vector.reciprocal(den[:], den[:]).then_inc(den_inv, 1)
                    run(dve, body)

                @block.gpsimd
                def _(pool):
                    steps = Steps(pool, pool_steps)

                    def split_maxima(h):
                        pool.wait_ge(m_done, h + 1)
                        hold(pool, m_turned, h, passed[1])
                        steps.add(nc.gpsimd.tensor_scalar(ma[:, 0], mx[:], -1.0, None, ALU.mult))
                        for a in range(2):
                            steps.settle_alone(passed[1])
                            steps.add(nc.gpsimd.tensor_copy(mp[:, a, 0:KT], ma[:, a]))
                            steps.settle()
                            steps.add(nc.gpsimd.tensor_tensor(out=ma[:, a + 1], in0=ma[:, a], in1=mp[:, a, 0:KT], op=ALU.subtract))
                        steps.settle_alone(passed[1])
                        nc.gpsimd.tensor_copy(mp[:, 2, 0:KT], ma[:, 2]).then_inc(m_parted, 1)

                    for r in range(HEADS):
                        steps.add(nc.gpsimd.memset(hk[r][QROWS:MROWS, :], 1.0))
                        steps.settle()
                    for q in range(2):
                        steps.add(nc.gpsimd.memset(vh[q][:], 1.0))
                        steps.settle()
                    nc.gpsimd.memset(mp[:], 0.0).then_inc(inited, 1)
                    pool.wait_ge(inited, 1)

                    def body(n, r):
                        q = r % 2
                        if exists(n + 1):
                            hold(pool, summed, KT * n, passed[1])
                            b = (n + 1) // H
                            h0 = ((n + 1) % H) * DH
                            src = VA[:, bass.ds(b * KT, KT), bass.ds(h0, DH)]
                            nc.gpsimd.tensor_copy(vh[1 - q][:, :, 0:DH], src).then_inc(v_ready, 1)
                            split_maxima(n + 1)
                        if not (isinstance(n, int) and n < 0):
                            xs = XR[:, bass.ds(n, 1), :].rearrange("p a d -> p (a d)")
                            nc.gpsimd.tensor_tensor(out=xs, in0=xs, in1=bp[:], op=ALU.add).then_inc(bias_added, 1)
                    run(pool, body, steps)
                    pool.wait_ge(bias_added, TILES)

        with ExitStack() as scope:
            XR = sb(scope, "XR0", [P, TILES, D])
            route(0, False, XR, setup(scope))
        experts(0)
        with ExitStack() as scope:
            XR = sb(scope, "XR1", [P, TILES, D])
            num, rcp = ([t[:, q * KD * CHUNK:(q + 1) * KD * CHUNK].rearrange("p (k t) -> p k t", k=KD) for q in range(2)]
                        for t in (cosT, sinT))
            o_loaded = pair("o_loaded")
            with ExitStack() as inner:
                VA = sb(inner, "VA", [P, TILES, D])
                hq0 = sb(inner, "hq0", [MROWS, T], BF16)
                hk0 = sb(inner, "hk0", [MROWS, T], BF16)
                mx40 = sb(inner, "mx40", [P, KT, 4])
                hd_loaded = [sem(f"hd_loaded{r}") for r in range(HEADS)]
                m_scored, m_reduced = sem("m_scored"), sem("m_reduced")
                qkv(VA, XR, hq0, hk0, mx40, hd_loaded, m_scored, m_reduced)
                attention(VA, XR, hq0, hk0, mx40, hd_loaded, m_scored, m_reduced, num, rcp, o_loaded)
            route(1, True, XR, None, num, rcp, o_loaded)
        experts(1)


_INS = ["L0_attn_x", "L0_attn_sin", "L0_attn_cos", "L0_attn_w_qkv", "L0_attn_b_qkv", "L0_attn_w_proj", "L0_attn_b_proj",
        "L0_ffn_w_router", "L0_ffn_b_router", "L0_ffn_w1", "L0_ffn_b1", "L0_ffn_w2", "L0_ffn_b2"]


def kernel(**inputs):
    import numpy as np
    import concourse.bacc as bacc
    from concourse.bass_utils import run_bass_kernel_spmd

    shapes = {"L0_attn_x": (N, D), "L0_attn_b_qkv": (1, 3 * D), "L0_attn_b_proj": (1, D), "L0_ffn_b_router": (1, NE),
              "L0_ffn_w1": (NE * D, FF), "L0_ffn_w2": (NE * FF, D)}
    nc = bacc.Bacc("TRN2", target_bir_lowering=False, num_devices=1)
    arrays, args = {}, []
    for name in _INS:
        a = np.ascontiguousarray(inputs[name])
        a = a.reshape(shapes.get(name, a.shape))
        arrays[name] = a
        args.append(nc.dram_tensor(name, a.shape, mybir.dt.from_np(a.dtype), kind="ExternalInput").ap())
    out = nc.dram_tensor("out", (N + CAP, D), F32, kind="ExternalOutput").ap()
    build(nc, *args, out)
    r = run_bass_kernel_spmd(nc, [arrays], core_ids=[0])
    return r.results[0]["out"][:N].reshape(B, T, D)
```
